# Optimizing a Trainium2 kernel written in Bass

```python
import numpy as np
import jax
import jax.numpy as jnp

def _softmax(x, axis=-1):
    return jax.nn.softmax(x, axis=axis)

def _gelu(x):
    return jax.nn.gelu(x, approximate=True)

def _silu(x):
    return jax.nn.silu(x)

def _sigmoid(x):
    return jax.nn.sigmoid(x)

def _layernorm(x, axis=-1, eps=1e-05):
    m = jnp.mean(x, axis=axis, keepdims=True)
    v = jnp.var(x, axis=axis, keepdims=True)
    return (x - m) / jnp.sqrt(v + eps)

def _scatter_add(tgt, idx, src, axis=0):
    return tgt.at[idx].add(src)

def _segment_sum(src, seg, n):
    return jax.ops.segment_sum(src, seg, n)
kernel_name = 'mk_decoder_preln_d2_seqx_r4_d26e22'

def setup_inputs(seed: int=0):
    np.random.seed(seed)
    _w = jnp.asarray

    def _rec_inputs():
        import jax
        import jax.numpy as jnp
        _rk = jax.random.key(seed)
        x = -0.0003929 + 0.9999 * jax.random.normal(jax.random.fold_in(_rk, 1), (16, 112, 256), jnp.float32)
        _lenS = 112 - jax.random.randint(jax.random.fold_in(_rk, 7), (16,), 0, max(1, 112 // 4) + 1, jnp.int32)
        _lenS2 = 375 - jax.random.randint(jax.random.fold_in(_rk, 8), (16,), 0, max(1, 375 // 4) + 1, jnp.int32)
        _ctx_1024P = jax.random.normal(jax.random.fold_in(_rk, 11), (16, 16, 256), jnp.float32)
        _ctx_1024c = jax.random.dirichlet(jax.random.fold_in(_rk, 511), 0.3 * jnp.ones((16,), jnp.float32), (16, 375))
        _ctx_1024t = jnp.einsum('bsk,bkd->bsd', _ctx_1024c, _ctx_1024P)
        _ctx_1024t = _ctx_1024t * jax.lax.rsqrt(jnp.mean(jnp.square(_ctx_1024t)) + 1e-12) * 0.953939
        ctx_1024 = -1.39393e-06 + 0.999914 * (_ctx_1024t + 0.3 * jax.random.normal(jax.random.fold_in(_rk, 611), (16, 375, 256), jnp.float32))
        _validS = jnp.arange(112)[None, :] < _lenS[:, None]
        _validS2 = jnp.arange(375)[None, :] < _lenS2[:, None]
        _causal = jnp.tril(jnp.ones((112, 112), dtype=bool))
        mask_BxS2_bf1 = jnp.ones((16, 375), dtype=bool)
        return (x, ctx_1024, mask_BxS2_bf1)
    x, ctx_1024, mask_BxS2_bf1 = _rec_inputs()

    def _L0_attn_setup():
        import jax, jax.numpy as jnp
        import numpy as np
        D_MODEL = 256
        D_STATE = 16
        D_CONV = 4
        EXPAND = 2
        D_INNER = D_MODEL * EXPAND
        B, L = (4, 512)

        def _forward(x, norm_w, norm_b, W_in, conv_w, conv_b, x_proj_w, dt_w, dt_b, A_log, D, W_out):
            Bsz, Lln, _ = x.shape
            residual = x
            mu = jnp.mean(x, -1, keepdims=True)
            var = jnp.var(x, -1, keepdims=True)
            xn = (x - mu) * jax.lax.rsqrt(var + 1e-05) * norm_w + norm_b
            xz = xn @ W_in
            xc, z = jnp.split(xz, 2, axis=-1)
            x_pad = jnp.pad(xc, ((0, 0), (D_CONV - 1, 0), (0, 0)))
            xc = sum((x_pad[:, k:k + Lln, :] * conv_w[:, k] for k in range(D_CONV))) + conv_b
            xc = jax.nn.silu(xc)
            A = -jnp.exp(A_log)
            dbc = xc @ x_proj_w
            dt = jax.nn.softplus(dbc[..., :1] * dt_w + dt_b)
            Bp = dbc[..., 1:1 + D_STATE]
            Cp = dbc[..., 1 + D_STATE:]

            def step(h, inp):
                x_t, dt_t, B_t, C_t = inp
                A_bar = jnp.exp(dt_t[..., None] * A)
                h = A_bar * h + dt_t[..., None] * B_t[:, None, :] * x_t[..., None]
                y_t = jnp.einsum('bdn,bn->bd', h, C_t)
                return (h, y_t)
            h0 = jnp.zeros((Bsz, D_INNER, D_STATE), xc.dtype)
            xs = (jnp.moveaxis(xc, 1, 0), jnp.moveaxis(dt, 1, 0), jnp.moveaxis(Bp, 1, 0), jnp.moveaxis(Cp, 1, 0))
            _, ys = jax.lax.scan(step, h0, xs)
            y = jnp.moveaxis(ys, 0, 1) + xc * D
            y = y * jax.nn.silu(z)
            return y @ W_out + residual
        key = jax.random.key(seed)
        ks = jax.random.split(key, 12)
        s = lambda k, shape, fan: jax.random.normal(k, shape, jnp.float32) / np.sqrt(fan)
        return {'x': jax.random.normal(ks[0], (B, L, D_MODEL), jnp.float32), 'norm_w': jnp.ones((D_MODEL,), jnp.float32), 'norm_b': jnp.zeros((D_MODEL,), jnp.float32), 'W_in': s(ks[1], (D_MODEL, 2 * D_INNER), D_MODEL), 'conv_w': s(ks[2], (D_INNER, D_CONV), D_CONV), 'conv_b': jnp.zeros((D_INNER,), jnp.float32), 'x_proj_w': s(ks[3], (D_INNER, 2 * D_STATE + 1), D_INNER), 'dt_w': s(ks[4], (D_INNER,), 1), 'dt_b': jnp.zeros((D_INNER,), jnp.float32), 'A_log': jax.random.normal(ks[5], (D_INNER, D_STATE), jnp.float32) * 0.5, 'D': jnp.ones((D_INNER,), jnp.float32), 'W_out': s(ks[6], (D_INNER, D_MODEL), D_INNER)}
    _L0_attn_all = _L0_attn_setup()
    _L0_attn_in = {k: v for k, v in _L0_attn_all.items() if k in ('norm_w', 'norm_b', 'W_in', 'conv_w', 'conv_b', 'x_proj_w', 'dt_w', 'dt_b', 'A_log', 'D', 'W_out')}
    del _L0_attn_all

    def _L0_xattn_setup():
        import jax, jax.numpy as jnp
        import numpy as np
        GAMMA = 10.0
        BASE = 10000.0
        SCALE = 64 ** (-0.5)
        NUM_HEADS = 16

        def _larope(t, seq_len):
            B, H, L, D = t.shape
            inv_freq = 1.0 / BASE ** (jnp.arange(0, D, 2, dtype=jnp.float32) / D)
            pos = GAMMA * (jnp.arange(L, dtype=jnp.float32) / float(seq_len))
            ang = pos[:, None] * inv_freq
            cos = jnp.cos(ang)
            sin = jnp.sin(ang)
            te, to = (t[..., 0::2], t[..., 1::2])
            re = te * cos - to * sin
            ro = te * sin + to * cos
            return jnp.stack([re, ro], axis=-1).reshape(t.shape)
        key = jax.random.key(seed)
        ks = jax.random.split(key, 8)
        B, Lq, Lk, D = (8, 512, 128, 256)
        s = D ** (-0.5)
        return {'x': jax.random.normal(ks[0], (B, Lq, D), jnp.float32), 'context': jax.random.normal(ks[1], (B, Lk, D), jnp.float32), 'context_mask': jnp.ones((B, Lk), dtype=bool), 'Wq': jax.random.normal(ks[2], (D, D), jnp.float32) * s, 'bq': jnp.zeros((D,), jnp.float32), 'Wkv': jax.random.normal(ks[3], (D, 2 * D), jnp.float32) * s, 'bkv': jnp.zeros((2 * D,), jnp.float32), 'Wo': jax.random.normal(ks[4], (D, D), jnp.float32) * s, 'bo': jnp.zeros((D,), jnp.float32)}
    _L0_xattn_all = _L0_xattn_setup()
    _L0_xattn_in = {k: v for k, v in _L0_xattn_all.items() if k in ('Wq', 'bq', 'Wkv', 'bkv', 'Wo', 'bo')}
    del _L0_xattn_all

    def _L0_ffn_setup():
        import jax, jax.numpy as jnp
        import numpy as np
        H = 256
        I = 176
        E = 64
        TOP_K = 8
        NG = 8
        TOPK_GROUP = 4
        N_SHARED = 2
        ROUTED_SCALE = 2.5
        S_I = I * N_SHARED

        def _route(x, gate_w, gate_bias):
            T = x.shape[0]
            logits = x @ gate_w.T
            scores = jax.nn.sigmoid(logits)
            scores_for_choice = scores + gate_bias[None, :]
            grp = scores_for_choice.reshape(T, NG, E // NG)
            group_scores = jnp.sum(jax.lax.top_k(grp, 2)[0], axis=-1)
            _, gidx = jax.lax.top_k(group_scores, TOPK_GROUP)
            gmask = jnp.zeros((T, NG), dtype=scores.dtype).at[jnp.arange(T)[:, None], gidx].set(1.0)
            emask = jnp.repeat(gmask, E // NG, axis=1)
            masked = jnp.where(emask > 0, scores_for_choice, 0.0)
            _, topk_idx = jax.lax.top_k(masked, TOP_K)
            topk_w = jnp.take_along_axis(scores, topk_idx, axis=1)
            topk_w = topk_w / (jnp.sum(topk_w, axis=-1, keepdims=True) + 1e-20)
            topk_w = topk_w * ROUTED_SCALE
            rw = jnp.zeros((T, E), dtype=scores.dtype).at[jnp.arange(T)[:, None], topk_idx].add(topk_w)
            return rw

        def _mlp(x, gw, uw, dw):
            return jax.nn.silu(x @ gw.T) * (x @ uw.T) @ dw.T
        key = jax.random.key(seed)
        ks = jax.random.split(key, 10)
        sc = 0.02
        return {'hidden_states': jax.random.normal(ks[0], (1, 256, H), dtype=jnp.float32), 'gate_w': sc * jax.random.normal(ks[1], (E, H), dtype=jnp.float32), 'gate_bias': sc * jax.random.normal(ks[2], (E,), dtype=jnp.float32), 'Wg': sc * jax.random.normal(ks[3], (E, I, H), dtype=jnp.float32), 'Wu': sc * jax.random.normal(ks[4], (E, I, H), dtype=jnp.float32), 'Wd': sc * jax.random.normal(ks[5], (E, H, I), dtype=jnp.float32), 'Sg': sc * jax.random.normal(ks[6], (S_I, H), dtype=jnp.float32), 'Su': sc * jax.random.normal(ks[7], (S_I, H), dtype=jnp.float32), 'Sd': sc * jax.random.normal(ks[8], (H, S_I), dtype=jnp.float32)}
    _L0_ffn_all = _L0_ffn_setup()
    _L0_ffn_in = {k: v for k, v in _L0_ffn_all.items() if k in ('gate_w', 'gate_bias', 'Wg', 'Wu', 'Wd', 'Sg', 'Su', 'Sd')}
    del _L0_ffn_all

    def _L1_attn_setup():
        import jax, jax.numpy as jnp
        import numpy as np
        DIM = 256
        DIM_INNER = 512
        B, S = (4, 1024)

        def heinsen_associative_scan_log(log_coeffs, log_values):
            a_star = jnp.cumsum(log_coeffs, axis=1)
            log_h0_plus_b_star = jax.lax.cumlogsumexp(log_values - a_star, axis=1)
            return jnp.exp(a_star + log_h0_plus_b_star)
        key = jax.random.key(seed)
        k1, k2, k3 = jax.random.split(key, 3)
        x = jax.random.normal(k1, (B, S, DIM), dtype=jnp.float32)
        W_hg = jax.random.normal(k2, (DIM, 2 * DIM_INNER), dtype=jnp.float32) / np.sqrt(DIM)
        W_out = jax.random.normal(k3, (DIM_INNER, DIM), dtype=jnp.float32) / np.sqrt(DIM_INNER)
        return {'x': x, 'W_hg': W_hg, 'W_out': W_out}
    _L1_attn_all = _L1_attn_setup()
    _L1_attn_in = {k: v for k, v in _L1_attn_all.items() if k in ('W_hg', 'W_out')}
    del _L1_attn_all

    def _L1_xattn_setup():
        import math
        import jax, jax.numpy as jnp
        import numpy as np
        H = 16
        D_MODEL = 256
        DK = D_MODEL // H
        K_FACTOR = 2

        def _time_delay_agg_inference(v, corr):
            B, _, _, L = v.shape
            top_k = min(int(K_FACTOR * math.log(L)), L)
            mean_value = jnp.mean(corr, axis=(1, 2))
            weights, delay = jax.lax.top_k(mean_value, top_k)
            tmp_corr = jax.nn.softmax(weights, axis=-1)
            idx = (delay[:, :, None] + jnp.arange(L)) % L
            gathered = jnp.take_along_axis(v[:, None], idx[:, :, None, None, :], axis=-1)
            return jnp.einsum('bk,bkhdl->bhdl', tmp_corr, gathered)
        key = jax.random.key(seed)
        ks = jax.random.split(key, 11)
        B, L, D = (4, 512, D_MODEL)
        s = 1.0 / math.sqrt(D)
        return {'queries': jax.random.normal(ks[0], (B, L, D), jnp.float32), 'keys': jax.random.normal(ks[1], (B, L, D), jnp.float32), 'values': jax.random.normal(ks[2], (B, L, D), jnp.float32), 'Wq': jax.random.normal(ks[3], (D, H * DK), jnp.float32) * s, 'bq': jnp.zeros((H * DK,), jnp.float32), 'Wk': jax.random.normal(ks[4], (D, H * DK), jnp.float32) * s, 'bk': jnp.zeros((H * DK,), jnp.float32), 'Wv': jax.random.normal(ks[5], (D, H * DK), jnp.float32) * s, 'bv': jnp.zeros((H * DK,), jnp.float32), 'Wo': jax.random.normal(ks[6], (H * DK, D), jnp.float32) * s, 'bo': jnp.zeros((D,), jnp.float32)}
    _L1_xattn_all = _L1_xattn_setup()
    _L1_xattn_in = {k: v for k, v in _L1_xattn_all.items() if k in ('Wq', 'bq', 'Wk', 'bk', 'Wv', 'bv', 'Wo', 'bo')}
    del _L1_xattn_all

    def _L1_ffn_setup():
        import jax, jax.numpy as jnp
        import numpy as np
        T, Z, D_DIM = (8, 512, 256)
        N_EXP, P_SLOT, H = (64, 32, 256)
        LN_EPS = 1e-05
        key = jax.random.key(seed)
        k = jax.random.split(key, 5)
        s = 0.02
        return {'x': jax.random.normal(k[0], (T, Z, D_DIM), dtype=jnp.float32), 'phi_w': jax.random.normal(k[1], (N_EXP * P_SLOT, D_DIM), dtype=jnp.float32) * s, 'phi_b': jax.random.normal(k[2], (N_EXP * P_SLOT,), dtype=jnp.float32) * s, 'expert_w': jax.random.normal(k[3], (N_EXP, D_DIM, H), dtype=jnp.float32) * s, 'expert_b': jax.random.normal(k[4], (N_EXP, H), dtype=jnp.float32) * s}
    _L1_ffn_all = _L1_ffn_setup()
    _L1_ffn_in = {k: v for k, v in _L1_ffn_all.items() if k in ('phi_w', 'phi_b', 'expert_w', 'expert_b')}
    del _L1_ffn_all
    return {'x': x, 'ctx_1024': ctx_1024, 'mask_BxS2_bf1': mask_BxS2_bf1, 'L0_attn_norm_w': _L0_attn_in['norm_w'], 'L0_attn_norm_b': _L0_attn_in['norm_b'], 'L0_attn_W_in': _L0_attn_in['W_in'], 'L0_attn_conv_w': _L0_attn_in['conv_w'], 'L0_attn_conv_b': _L0_attn_in['conv_b'], 'L0_attn_x_proj_w': _L0_attn_in['x_proj_w'], 'L0_attn_dt_w': _L0_attn_in['dt_w'], 'L0_attn_dt_b': _L0_attn_in['dt_b'], 'L0_attn_A_log': _L0_attn_in['A_log'], 'L0_attn_D': _L0_attn_in['D'], 'L0_attn_W_out': _L0_attn_in['W_out'], 'L0_xattn_Wq': _L0_xattn_in['Wq'], 'L0_xattn_bq': _L0_xattn_in['bq'], 'L0_xattn_Wkv': _L0_xattn_in['Wkv'], 'L0_xattn_bkv': _L0_xattn_in['bkv'], 'L0_xattn_Wo': _L0_xattn_in['Wo'], 'L0_xattn_bo': _L0_xattn_in['bo'], 'L0_ffn_gate_w': _L0_ffn_in['gate_w'], 'L0_ffn_gate_bias': _L0_ffn_in['gate_bias'], 'L0_ffn_Wg': _L0_ffn_in['Wg'], 'L0_ffn_Wu': _L0_ffn_in['Wu'], 'L0_ffn_Wd': _L0_ffn_in['Wd'], 'L0_ffn_Sg': _L0_ffn_in['Sg'], 'L0_ffn_Su': _L0_ffn_in['Su'], 'L0_ffn_Sd': _L0_ffn_in['Sd'], 'L1_attn_W_hg': _L1_attn_in['W_hg'], 'L1_attn_W_out': _L1_attn_in['W_out'], 'L1_xattn_Wq': _L1_xattn_in['Wq'], 'L1_xattn_bq': _L1_xattn_in['bq'], 'L1_xattn_Wk': _L1_xattn_in['Wk'], 'L1_xattn_bk': _L1_xattn_in['bk'], 'L1_xattn_Wv': _L1_xattn_in['Wv'], 'L1_xattn_bv': _L1_xattn_in['bv'], 'L1_xattn_Wo': _L1_xattn_in['Wo'], 'L1_xattn_bo': _L1_xattn_in['bo'], 'L1_ffn_phi_w': _L1_ffn_in['phi_w'], 'L1_ffn_phi_b': _L1_ffn_in['phi_b'], 'L1_ffn_expert_w': _L1_ffn_in['expert_w'], 'L1_ffn_expert_b': _L1_ffn_in['expert_b']}

def reference(x, ctx_1024, mask_BxS2_bf1, L0_attn_norm_w, L0_attn_norm_b, L0_attn_W_in, L0_attn_conv_w, L0_attn_conv_b, L0_attn_x_proj_w, L0_attn_dt_w, L0_attn_dt_b, L0_attn_A_log, L0_attn_D, L0_attn_W_out, L0_xattn_Wq, L0_xattn_bq, L0_xattn_Wkv, L0_xattn_bkv, L0_xattn_Wo, L0_xattn_bo, L0_ffn_gate_w, L0_ffn_gate_bias, L0_ffn_Wg, L0_ffn_Wu, L0_ffn_Wd, L0_ffn_Sg, L0_ffn_Su, L0_ffn_Sd, L1_attn_W_hg, L1_attn_W_out, L1_xattn_Wq, L1_xattn_bq, L1_xattn_Wk, L1_xattn_bk, L1_xattn_Wv, L1_xattn_bv, L1_xattn_Wo, L1_xattn_bo, L1_ffn_phi_w, L1_ffn_phi_b, L1_ffn_expert_w, L1_ffn_expert_b):
    import jax
    import jax.numpy as jnp

    def _L0_attn_ref(x, norm_w, norm_b, W_in, conv_w, conv_b, x_proj_w, dt_w, dt_b, A_log, D, W_out):
        import jax, jax.numpy as jnp
        import numpy as np
        D_MODEL = 256
        D_STATE = 16
        D_CONV = 4
        EXPAND = 2
        D_INNER = D_MODEL * EXPAND
        B, L = (4, 512)

        def _forward(x, norm_w, norm_b, W_in, conv_w, conv_b, x_proj_w, dt_w, dt_b, A_log, D, W_out):
            Bsz, Lln, _ = x.shape
            residual = x
            mu = jnp.mean(x, -1, keepdims=True)
            var = jnp.var(x, -1, keepdims=True)
            xn = (x - mu) * jax.lax.rsqrt(var + 1e-05) * norm_w + norm_b
            xz = xn @ W_in
            xc, z = jnp.split(xz, 2, axis=-1)
            x_pad = jnp.pad(xc, ((0, 0), (D_CONV - 1, 0), (0, 0)))
            xc = sum((x_pad[:, k:k + Lln, :] * conv_w[:, k] for k in range(D_CONV))) + conv_b
            xc = jax.nn.silu(xc)
            A = -jnp.exp(A_log)
            dbc = xc @ x_proj_w
            dt = jax.nn.softplus(dbc[..., :1] * dt_w + dt_b)
            Bp = dbc[..., 1:1 + D_STATE]
            Cp = dbc[..., 1 + D_STATE:]

            def step(h, inp):
                x_t, dt_t, B_t, C_t = inp
                A_bar = jnp.exp(dt_t[..., None] * A)
                h = A_bar * h + dt_t[..., None] * B_t[:, None, :] * x_t[..., None]
                y_t = jnp.einsum('bdn,bn->bd', h, C_t)
                return (h, y_t)
            h0 = jnp.zeros((Bsz, D_INNER, D_STATE), xc.dtype)
            xs = (jnp.moveaxis(xc, 1, 0), jnp.moveaxis(dt, 1, 0), jnp.moveaxis(Bp, 1, 0), jnp.moveaxis(Cp, 1, 0))
            _, ys = jax.lax.scan(step, h0, xs)
            y = jnp.moveaxis(ys, 0, 1) + xc * D
            y = y * jax.nn.silu(z)
            return y @ W_out + residual
        return _forward(x, norm_w, norm_b, W_in, conv_w, conv_b, x_proj_w, dt_w, dt_b, A_log, D, W_out)

    def _L0_xattn_ref(x, context, context_mask, Wq, bq, Wkv, bkv, Wo, bo):
        import jax, jax.numpy as jnp
        import numpy as np
        GAMMA = 10.0
        BASE = 10000.0
        SCALE = 64 ** (-0.5)
        NUM_HEADS = 16

        def _larope(t, seq_len):
            B, H, L, D = t.shape
            inv_freq = 1.0 / BASE ** (jnp.arange(0, D, 2, dtype=jnp.float32) / D)
            pos = GAMMA * (jnp.arange(L, dtype=jnp.float32) / float(seq_len))
            ang = pos[:, None] * inv_freq
            cos = jnp.cos(ang)
            sin = jnp.sin(ang)
            te, to = (t[..., 0::2], t[..., 1::2])
            re = te * cos - to * sin
            ro = te * sin + to * cos
            return jnp.stack([re, ro], axis=-1).reshape(t.shape)
        B, Lq, D = x.shape
        Lk = context.shape[1]
        H = NUM_HEADS
        hd = D // H
        q = x @ Wq + bq
        kv = context @ Wkv + bkv
        k, v = jnp.split(kv, 2, axis=-1)
        q = q.reshape(B, Lq, H, hd).transpose(0, 2, 1, 3)
        k = k.reshape(B, Lk, H, hd).transpose(0, 2, 1, 3)
        v = v.reshape(B, Lk, H, hd).transpose(0, 2, 1, 3)
        q = _larope(q, Lq)
        k = _larope(k, Lk)
        scores = jnp.einsum('bhqd,bhkd->bhqk', q, k) * SCALE
        scores = jnp.where(context_mask[:, None, None, :], scores, -jnp.inf)
        attn = jax.nn.softmax(scores, axis=-1)
        out = jnp.einsum('bhqk,bhkd->bhqd', attn, v)
        out = out.transpose(0, 2, 1, 3).reshape(B, Lq, H * hd)
        return out @ Wo + bo

    def _L0_ffn_ref(hidden_states, gate_w, gate_bias, Wg, Wu, Wd, Sg, Su, Sd):
        import jax, jax.numpy as jnp
        import numpy as np
        H = 256
        I = 176
        E = 64
        TOP_K = 8
        NG = 8
        TOPK_GROUP = 4
        N_SHARED = 2
        ROUTED_SCALE = 2.5
        S_I = I * N_SHARED

        def _route(x, gate_w, gate_bias):
            T = x.shape[0]
            logits = x @ gate_w.T
            scores = jax.nn.sigmoid(logits)
            scores_for_choice = scores + gate_bias[None, :]
            grp = scores_for_choice.reshape(T, NG, E // NG)
            group_scores = jnp.sum(jax.lax.top_k(grp, 2)[0], axis=-1)
            _, gidx = jax.lax.top_k(group_scores, TOPK_GROUP)
            gmask = jnp.zeros((T, NG), dtype=scores.dtype).at[jnp.arange(T)[:, None], gidx].set(1.0)
            emask = jnp.repeat(gmask, E // NG, axis=1)
            masked = jnp.where(emask > 0, scores_for_choice, 0.0)
            _, topk_idx = jax.lax.top_k(masked, TOP_K)
            topk_w = jnp.take_along_axis(scores, topk_idx, axis=1)
            topk_w = topk_w / (jnp.sum(topk_w, axis=-1, keepdims=True) + 1e-20)
            topk_w = topk_w * ROUTED_SCALE
            rw = jnp.zeros((T, E), dtype=scores.dtype).at[jnp.arange(T)[:, None], topk_idx].add(topk_w)
            return rw

        def _mlp(x, gw, uw, dw):
            return jax.nn.silu(x @ gw.T) * (x @ uw.T) @ dw.T
        B, S, _ = hidden_states.shape
        x = hidden_states.reshape(B * S, H)
        rw = _route(x, gate_w, gate_bias)
        expert_out = jax.vmap(lambda gw_, uw_, dw_: _mlp(x, gw_, uw_, dw_))(Wg, Wu, Wd)
        routed = jnp.einsum('eth,te->th', expert_out, rw)
        shared = _mlp(x, Sg, Su, Sd)
        out = (routed + shared).reshape(B, S, H)
        return out

    def _L1_attn_ref(x, W_hg, W_out):
        import jax, jax.numpy as jnp
        import numpy as np
        DIM = 256
        DIM_INNER = 512
        B, S = (4, 1024)

        def heinsen_associative_scan_log(log_coeffs, log_values):
            a_star = jnp.cumsum(log_coeffs, axis=1)
            log_h0_plus_b_star = jax.lax.cumlogsumexp(log_values - a_star, axis=1)
            return jnp.exp(a_star + log_h0_plus_b_star)
        hg = jnp.einsum('bsd,de->bse', x, W_hg)
        hidden, gate = jnp.split(hg, 2, axis=-1)
        log_z = jax.nn.log_sigmoid(gate)
        log_coeffs = -jax.nn.softplus(gate)
        hidden_log = jnp.log(jax.nn.relu(hidden) + 0.5)
        log_values = hidden_log + log_z
        h = heinsen_associative_scan_log(log_coeffs, log_values)
        out = jnp.einsum('bse,ed->bsd', h, W_out)
        return out

    def _L1_xattn_ref(queries, keys, values, Wq, bq, Wk, bk, Wv, bv, Wo, bo):
        import math
        import jax, jax.numpy as jnp
        import numpy as np
        H = 16
        D_MODEL = 256
        DK = D_MODEL // H
        K_FACTOR = 2

        def _time_delay_agg_inference(v, corr):
            B, _, _, L = v.shape
            top_k = min(int(K_FACTOR * math.log(L)), L)
            mean_value = jnp.mean(corr, axis=(1, 2))
            weights, delay = jax.lax.top_k(mean_value, top_k)
            tmp_corr = jax.nn.softmax(weights, axis=-1)
            idx = (delay[:, :, None] + jnp.arange(L)) % L
            gathered = jnp.take_along_axis(v[:, None], idx[:, :, None, None, :], axis=-1)
            return jnp.einsum('bk,bkhdl->bhdl', tmp_corr, gathered)
        B, Lq, _ = queries.shape
        Lk = keys.shape[1]
        q = (queries @ Wq + bq).reshape(B, Lq, H, DK)
        k = (keys @ Wk + bk).reshape(B, Lk, H, DK)
        v = (values @ Wv + bv).reshape(B, Lk, H, DK)
        if Lq > Lk:
            pad = ((0, 0), (0, Lq - Lk), (0, 0), (0, 0))
            k = jnp.pad(k, pad)
            v = jnp.pad(v, pad)
        else:
            k = k[:, :Lq]
            v = v[:, :Lq]
        qt = jnp.transpose(q, (0, 2, 3, 1))
        kt = jnp.transpose(k, (0, 2, 3, 1))
        vt = jnp.transpose(v, (0, 2, 3, 1))
        qf = jnp.fft.rfft(qt)
        kf = jnp.fft.rfft(kt)
        c = qf.real * kf.real + 1j * -(qf.imag * kf.imag)
        corr = jnp.fft.irfft(c, n=Lq).astype(qt.dtype)
        agg = _time_delay_agg_inference(vt, corr)
        out = jnp.transpose(agg, (0, 3, 1, 2)).reshape(B, Lq, H * DK)
        return out @ Wo + bo

    def _L1_ffn_ref(x, phi_w, phi_b, expert_w, expert_b):
        import jax, jax.numpy as jnp
        import numpy as np
        T, Z, D_DIM = (8, 512, 256)
        N_EXP, P_SLOT, H = (64, 32, 256)
        LN_EPS = 1e-05
        t, z, d = x.shape
        n = expert_w.shape[0]
        p = phi_w.shape[0] // n
        logits = (jnp.einsum('tzd,ed->tze', x, phi_w) + phi_b).reshape(t, z, n, p)
        D = jax.nn.softmax(logits, axis=3)
        C = jax.nn.softmax(logits, axis=2)
        X_tilde = jnp.einsum('tznp,tzd->npd', D, x)
        X_tilde = jnp.clip(X_tilde, -33000.0, 65000.0)
        mu = jnp.mean(X_tilde, axis=-1, keepdims=True)
        var = jnp.mean(jnp.square(X_tilde - mu), axis=-1, keepdims=True)
        X_tilde = (X_tilde - mu) * jax.lax.rsqrt(var + LN_EPS)
        X_tilde = jnp.tanh(X_tilde)
        Y_tilde = jnp.einsum('npd,ndH->npH', X_tilde, expert_w) + expert_b[:, None, :]
        Y = jnp.einsum('tznp,npH->tzH', C, Y_tilde)
        return Y
    x = x + _L0_attn_ref(_layernorm(x, axis=-1), L0_attn_norm_w, L0_attn_norm_b, L0_attn_W_in, L0_attn_conv_w, L0_attn_conv_b, L0_attn_x_proj_w, L0_attn_dt_w, L0_attn_dt_b, L0_attn_A_log, L0_attn_D, L0_attn_W_out)
    x = x + _L0_xattn_ref(_layernorm(x, axis=-1), ctx_1024, mask_BxS2_bf1, L0_xattn_Wq, L0_xattn_bq, L0_xattn_Wkv, L0_xattn_bkv, L0_xattn_Wo, L0_xattn_bo)
    x = x + _L0_ffn_ref(_layernorm(x, axis=-1), L0_ffn_gate_w, L0_ffn_gate_bias, L0_ffn_Wg, L0_ffn_Wu, L0_ffn_Wd, L0_ffn_Sg, L0_ffn_Su, L0_ffn_Sd)
    x = x + _L1_attn_ref(_layernorm(x, axis=-1), L1_attn_W_hg, L1_attn_W_out)
    x = x + _L1_xattn_ref(_layernorm(x, axis=-1), ctx_1024, ctx_1024, L1_xattn_Wq, L1_xattn_bq, L1_xattn_Wk, L1_xattn_bk, L1_xattn_Wv, L1_xattn_bv, L1_xattn_Wo, L1_xattn_bo)
    x = x + _L1_ffn_ref(_layernorm(x, axis=-1), L1_ffn_phi_w, L1_ffn_phi_b, L1_ffn_expert_w, L1_ffn_expert_b)
    return x

_drawn_inputs = setup_inputs


def setup_inputs(seed=0):
    import zlib

    import numpy as np

    out = dict(_drawn_inputs(seed))
    spreads = {'L0_attn_norm_w': (1.0, 0.2),
     'L0_attn_norm_b': (0.0, 0.1),
     'L0_attn_conv_b': (0.0, 0.1),
     'L0_attn_dt_b': (0.0, 0.588),
     'L0_attn_D': (1.0, 0.2),
     'L0_xattn_bq': (0.0, 0.8),
     'L0_xattn_bkv': (0.0, 0.1),
     'L0_xattn_bo': (0.0, 0.1),
     'L1_xattn_bq': (0.0, 2.0),
     'L1_xattn_bk': (0.0, 2.0),
     'L1_xattn_bv': (0.0, 0.324),
     'L1_xattn_bo': (0.0, 0.327)}
    factors = {'L0_ffn_gate_w': 4.673,
     'L0_ffn_gate_bias': 8.0,
     'L0_ffn_Wg': 5.973,
     'L0_ffn_Wu': 5.965,
     'L0_ffn_Wd': 8.0,
     'L0_ffn_Sg': 5.004,
     'L0_ffn_Su': 5.055,
     'L0_ffn_Sd': 4.155,
     'L1_ffn_phi_b': 64.0,
     'L1_ffn_phi_w': 7.143,
     'L1_ffn_expert_b': 4.271}
    for name, (base, spread) in spreads.items():
        noise = np.random.default_rng([zlib.crc32(name.encode()), seed]).standard_normal(out[name].shape)
        drawn = base * np.exp(spread * noise) if base else spread * noise
        out[name] = jnp.asarray(drawn.astype(out[name].dtype))
    for name, factor in factors.items():
        out[name] = (out[name] * factor).astype(out[name].dtype)
    return out
```

```python
from contextlib import ExitStack, contextmanager

import numpy as np

import concourse.bass as bass
from concourse import mybir

F32 = mybir.dt.float32
I32 = mybir.dt.int32
U8 = mybir.dt.uint8
ALU = mybir.AluOpType
ACT = mybir.ActivationFunctionType
AX = mybir.AxisListType.X
ds = bass.ds

P = 128
B, L, D = 16, 112, 256
T = B * L
DH = D // P
CW = 448
NCH = T // CW
BPC = CW // L
EPS = 1e-5
DI, DIC, NST, TAPS = 512, 4, 16, 4
HW = T // 2
BPH = HW // L
S2, NHEAD, HD, KC = 375, 16, 16, 125
HPT = P // HD
SCALE = 64 ** -0.5
BIG = 3.0e38
E, I, NG, TOPG, TOPK = 64, 176, 8, 4, 8
EG = E // NG
TT = T // P
SLOT_TILES = 176
NSLOT = SLOT_TILES * P
SI = 2 * I
NF = L // 2
TOPD = 9
NE, PS = 64, 32
NP_ = NE * PS


def chunk(i, size):
    return ds(i * size, size)


@contextmanager
def loop(eng, n, step=1):
    with eng.Fori(0, n // step) as i:
        yield i * step if step > 1 else i


class Kit:

    def __init__(self, nc, outer):
        self.nc, self.outer, self.n = nc, outer, 0
        self.stage_sems = []

    def sem(self, name):
        self.stage_sems.append(self.nc.alloc_semaphore(name=name))
        return self.stage_sems[-1]

    def end_stage(self):
        self.nc.clear_and_free_semaphores(self.stage_sems)
        self.nc.all_engine_barrier()
        self.stage_sems = []

    def kept_sem(self, name):
        return self.outer.enter_context(self.nc.semaphore(name))

    def sems(self, name, n):
        return [self.sem(f"{name}{i}") for i in range(n)]

    def sb(self, ctx, name, shape, dt=F32):
        self.n += 1
        return ctx.enter_context(self.nc.sbuf_tensor(f"{name}_{self.n}", shape, dt))

    def ps(self, ctx, name, shape):
        self.n += 1
        return ctx.enter_context(self.nc.psum_tensor(f"{name}_{self.n}", shape, F32))

    def dram(self, name, shape, dt=F32):
        return self.nc.dram_tensor(name, shape, dt).ap()


class Steps:

    def __init__(self, eng, sem, base=0):
        self.eng, self.sem, self.base, self.n = eng, sem, base, 0

    def did(self, ins):
        self.n += 1
        ins.then_inc(self.sem, 1)

    def wait(self):
        self.eng.wait_ge(self.sem, self.base + self.n)


def load_constants(k, g, ins):
    nc = k.nc
    loaded = k.sem("constants_loaded")
    filled = k.sem("constants_filled")
    with nc.Block() as block:
        @block.sync
        def _(sp):
            sp.dma_start(g.x[:], ins["xT"].rearrange("(h p) t -> p h t", p=P)).then_inc(loaded, 16)
            sp.dma_start(g.ident[:], ins["ident"]).then_inc(loaded, 16)
            sp.wait_ge(loaded, 32)

        @block.gpsimd
        def _(pool):
            pool.memset(g.mean_w[:], 1.0 / D)
            pool.memset(g.ones[:], 1.0)
            pool.memset(g.eps[:], EPS).then_inc(filled, 1)
            pool.wait_ge(filled, 1)


class LayerNorm:

    def __init__(self, k):
        self.k, self.calls = k, 0
        self.mean_ready, self.centred, self.squared = k.kept_sem("ln_mean_ready"), k.kept_sem("ln_centred"), k.kept_sem("ln_squared")
        self.var_ready, self.std_ready = k.kept_sem("ln_var_ready"), k.kept_sem("ln_std_ready")
        self.recip_ready, self.normed, self.done = k.kept_sem("ln_recip_ready"), k.kept_sem("ln_normed"), k.kept_sem("ln_done")

    def __call__(self, g, src, dst, weight=None, bias=None):
        k, nc, base = self.k, self.k.nc, NCH * self.calls
        self.calls += 1
        with ExitStack() as ctx:
            xc = k.sb(ctx, "ln_xc", [P, 2, DH, CW])
            sq = k.sb(ctx, "ln_sq", [P, 2, DH, CW])
            std = k.sb(ctx, "ln_std", [P, 2, CW])
            mean = k.ps(ctx, "ln_mean", [P, 2, 512])
            var = k.ps(ctx, "ln_var", [P, 2, 512])
            block = ctx.enter_context(nc.Block())

            @block.tensor
            def _(pe):
                with loop(pe, NCH, 2) as i:
                    pe.wait_ge(self.centred, base + i)
                    for s in range(2):
                        for h in range(DH):
                            mm = pe.matmul(mean[:, s, 0:CW], g.mean_w[:], src[:, h, chunk(i + s, CW)], start=(h == 0), stop=(h == DH - 1))
                        mm.then_inc(self.mean_ready, 1)
                    pe.wait_ge(self.std_ready, base + i)
                    for s in range(2):
                        pe.wait_ge(self.squared, base + i + s + 1)
                        for h in range(DH):
                            mm = pe.matmul(var[:, s, 0:CW], g.mean_w[:], sq[:, s, h, :], start=(h == 0), stop=(h == DH - 1))
                        mm.then_inc(self.var_ready, 1)

            @block.vector
            def _(dve):
                with loop(dve, NCH, 2) as i:
                    dve.wait_ge(self.done, base + i)
                    for s in range(2):
                        dve.wait_ge(self.mean_ready, base + i + s + 1)
                        m = mean[:, s, 0:CW].unsqueeze(1).to_broadcast([P, DH, CW])
                        dve.tensor_tensor(xc[:, s], src[:, :, chunk(i + s, CW)], m, ALU.subtract).then_inc(self.centred, 1)
                    for s in range(2):
                        dve.wait_ge(self.std_ready, base + i + s + 1)
                        dve.reciprocal(std[:, s], std[:, s]).then_inc(self.recip_ready, 1)
                    for s in range(2):
                        dve.wait_ge(self.recip_ready, base + i + s + 1)
                        r = std[:, s].unsqueeze(1).to_broadcast([P, DH, CW])
                        if weight is None:
                            dve.tensor_tensor(dst[:, :, chunk(i + s, CW)], xc[:, s], r, ALU.mult).then_inc(self.done, 1)
                            continue
                        dve.tensor_tensor(sq[:, s], xc[:, s], r, ALU.mult).then_inc(self.normed, 1)
                        dve.wait_ge(self.normed, i + s + 1)
                        for h in range(DH):
                            last = dve.tensor_scalar(dst[:, h, chunk(i + s, CW)], sq[:, s, h], weight[:, h:h + 1], bias[:, h:h + 1], ALU.mult, ALU.add)
                        last.then_inc(self.done, 1)

            @block.scalar
            def _(act):
                with loop(act, NCH, 2) as i:
                    act.wait_ge(self.var_ready, base + i)
                    act.wait_ge(self.done, base + i)
                    for s in range(2):
                        act.wait_ge(self.centred, base + i + s + 1)
                        act.activation(sq[:, s], xc[:, s], ACT.Square).then_inc(self.squared, 1)
                    for s in range(2):
                        act.wait_ge(self.var_ready, base + i + s + 1)
                        act.activation(std[:, s], var[:, s, 0:CW], ACT.Sqrt, bias=g.eps[:]).then_inc(self.std_ready, 1)


def mamba(k, g, ins, norm):
    nc = k.nc
    b_dram = k.dram("mamba_b", [2 * NST, HW])
    c_dram = k.dram("mamba_c", [2 * NST, HW])
    small_loaded = k.sem("mamba_small_loaded")
    w_in_loaded = k.sem("mamba_w_in_loaded")
    with ExitStack() as ctx:
        xs = k.sb(ctx, "mamba_xs", [P, DIC, T])
        gate = k.sb(ctx, "mamba_gate", [P, DIC, T])
        small = k.sb(ctx, "mamba_small", [P, DIC, TAPS + 4 + NST])
        conv_w, conv_b = small[:, :, 0:TAPS], small[:, :, TAPS]
        dt_w, dt_b, skip = small[:, :, TAPS + 1], small[:, :, TAPS + 2], small[:, :, TAPS + 3]
        a_neg = small[:, :, TAPS + 4:]
        norm_wb = k.sb(ctx, "mamba_norm_wb", [P, 2, DH])
        xp_w = k.sb(ctx, "mamba_xp_w", [P, DIC, 2 * NST])
        dt_rep = k.sb(ctx, "mamba_dt_rep", [P, DIC, P])

        with ExitStack() as c1:
            xn1 = k.sb(c1, "mamba_xn1", [P, DH, T])
            w_in = k.sb(c1, "mamba_w_in", [P, DH, 2 * DI])
            a_exp, a_sign = k.sem("mamba_a_exp"), k.sem("mamba_a_sign")
            with nc.Block() as block:
                @block.sync
                def _(sp):
                    sp.dma_start(small[:], ins["mamba_small"].rearrange("(c p) n -> p c n", p=P)).then_inc(small_loaded, 16)
                    sp.dma_start(norm_wb[:], ins["mamba_norm"]).then_inc(small_loaded, 16)
                    sp.dma_start(xp_w[:], ins["mamba_xp_w"].rearrange("(c p) n -> p c n", p=P)).then_inc(small_loaded, 16)
                    sp.dma_start(dt_rep[:], ins["mamba_dt_rep"].rearrange("(c p) n -> p c n", p=P)).then_inc(small_loaded, 16)
                    sp.dma_start(w_in[:], ins["mamba_w_in"].rearrange("(h p) n -> p h n", p=P)).then_inc(w_in_loaded, 16)
                    sp.wait_ge(small_loaded, 64)

                @block.scalar
                def _(act):
                    act.wait_ge(small_loaded, 64)
                    act.activation(a_neg, a_neg, ACT.Exp).then_inc(a_exp, 1)

                @block.vector
                def _(dve):
                    dve.wait_ge(a_exp, 1)
                    dve.tensor_scalar(a_neg, a_neg, -1.0, None, ALU.mult).then_inc(a_sign, 1)
                    dve.wait_ge(a_sign, 1)
            norm(g, g.x, xn1)
            norm(g, xn1, g.xn, norm_wb[:, 0], norm_wb[:, 1])

            proj_ready = k.sem("mamba_proj_ready")
            tap_done, conv_done = k.sem("mamba_tap_done"), k.sem("mamba_conv_done")
            silu_done, gate_done = k.sem("mamba_silu_done"), k.sem("mamba_gate_done")
            res_done = k.sem("mamba_res_done")
            with ExitStack() as c2:
                xz = k.ps(c2, "mamba_xz", [P, 2 * DIC, 512])
                pre = k.sb(c2, "mamba_pre", [P, DIC, CW])
                block = c2.enter_context(nc.Block())

                @block.tensor
                def _(pe):
                    pe.wait_ge(w_in_loaded, 16)
                    with loop(pe, NCH) as j:
                        for m in range(2 * DIC):
                            pe.wait_ge(*((conv_done, DIC * j) if m < DIC else (gate_done, DIC * j)))
                            for h in range(DH):
                                mm = pe.matmul(xz[:, m, 0:CW], w_in[:, h, m * P:(m + 1) * P], g.xn[:, h, chunk(j, CW)], start=(h == 0), stop=(h == DH - 1))
                            mm.then_inc(proj_ready, 1)

                @block.vector
                def _(dve):
                    with loop(dve, NCH) as j:
                        dve.wait_ge(silu_done, DIC * j)
                        taps = Steps(dve, tap_done, DIC * (TAPS - 1) * j)
                        for c in range(DIC):
                            dve.wait_ge(proj_ready, 2 * DIC * j + c + 1)
                            taps.did(dve.tensor_scalar(pre[:, c], xz[:, c, 0:CW], conv_w[:, c, TAPS - 1:TAPS], conv_b[:, c:c + 1], ALU.mult, ALU.add))
                            src = xz[:, c, 0:CW].rearrange("p (b l) -> p b l", l=L)
                            dst = pre[:, c].rearrange("p (b l) -> p b l", l=L)
                            for lag in range(1, TAPS):
                                taps.wait()
                                tap = dve.scalar_tensor_tensor(dst[:, :, lag:], src[:, :, :L - lag], conv_w[:, c, TAPS - 1 - lag:TAPS - lag], dst[:, :, lag:], ALU.mult, ALU.add)
                                if lag < TAPS - 1:
                                    taps.did(tap)
                                else:
                                    tap.then_inc(conv_done, 1)

                @block.scalar
                def _(act):
                    with loop(act, NCH) as j:
                        for c in range(DIC):
                            act.wait_ge(proj_ready, 2 * DIC * j + DIC + c + 1)
                            act.activation(gate[:, c, chunk(j, CW)], xz[:, DIC + c, 0:CW], ACT.Silu).then_inc(gate_done, 1)
                        for c in range(DIC):
                            act.wait_ge(conv_done, DIC * j + c + 1)
                            act.activation(xs[:, c, chunk(j, CW)], pre[:, c], ACT.Silu).then_inc(silu_done, 1)

                @block.gpsimd
                def _(pool):
                    for h in range(DH):
                        pool.tensor_tensor(g.x[:, h], g.x[:, h], xn1[:, h], ALU.add).then_inc(res_done, 1)
                    pool.wait_ge(res_done, DH)

        with ExitStack() as c3:
            dt = k.sb(c3, "mamba_dt", [P, DIC, T])
            u = k.sb(c3, "mamba_u", [P, DIC, T])

            raw_ready, bc_ready = k.sem("mamba_raw_ready"), k.sem("mamba_bc_ready")
            raw_used, bc_used = k.sem("mamba_raw_used"), k.sem("mamba_bc_used")
            abs_done, exp_done, ln_done, relu_done = k.sem("mamba_abs_done"), k.sem("mamba_exp_done"), k.sem("mamba_ln_done"), k.sem("mamba_relu_done")
            dt_done, u_done, bc_stored = k.sem("mamba_dt_done"), k.sem("mamba_u_done"), k.sem("mamba_bc_stored")
            with ExitStack() as c2:
                raw = k.ps(c2, "mamba_raw", [P, 512])
                bc = k.ps(c2, "mamba_bc", [2 * NST, 512])
                bc_sb = k.sb(c2, "mamba_bc_sb", [2 * NST, T])
                soft = k.sb(c2, "mamba_soft", [P, DIC, CW])
                relu = k.sb(c2, "mamba_relu", [P, DIC, CW])
                block = c2.enter_context(nc.Block())

                @block.tensor
                def _(pe):
                    with loop(pe, NCH) as j:
                        pe.wait_ge(raw_used, DIC * j)
                        for c in range(DIC):
                            mm = pe.matmul(raw[:, 0:CW], dt_rep[:, c], xs[:, c, chunk(j, CW)], start=(c == 0), stop=(c == DIC - 1))
                        mm.then_inc(raw_ready, 1)
                        pe.wait_ge(bc_used, j)
                        after_wait(pe, g)
                        for c in range(DIC):
                            mm = pe.matmul(bc[:, 0:CW], xp_w[:, c], xs[:, c, chunk(j, CW)], start=(c == 0), stop=(c == DIC - 1))
                        mm.then_inc(bc_ready, 1)

                @block.scalar
                def _(act):
                    with loop(act, NCH) as j:
                        act.wait_ge(raw_ready, j + 1)
                        act.wait_ge(dt_done, DIC * j)
                        for c in range(DIC):
                            act.activation(soft[:, c], raw[:, 0:CW], ACT.Abs, bias=dt_b[:, c:c + 1], scale=dt_w[:, c:c + 1]).then_inc(abs_done, 1)
                            act.activation(relu[:, c], raw[:, 0:CW], ACT.Relu, bias=dt_b[:, c:c + 1], scale=dt_w[:, c:c + 1]).then_inc(raw_used, 1)
                        act.wait_ge(abs_done, DIC * j + DIC)
                        act.activation(soft[:], soft[:], ACT.Exp, scale=-1.0).then_inc(exp_done, 1)
                        act.wait_ge(exp_done, j + 1)
                        act.activation(soft[:], soft[:], ACT.Ln, bias=1.0).then_inc(ln_done, 1)

                @block.vector
                def _(dve):
                    with loop(dve, NCH) as j:
                        dve.wait_ge(bc_ready, j + 1)
                        dve.tensor_copy(bc_sb[:, chunk(j, CW)], bc[:, 0:CW]).then_inc(bc_used, 1)
                        dve.wait_ge(ln_done, j + 1)
                        dve.wait_ge(raw_used, DIC * j + DIC)
                        for c in range(DIC):
                            dve.tensor_tensor(dt[:, c, chunk(j, CW)], soft[:, c], relu[:, c], ALU.add).then_inc(dt_done, 1)
                        for c in range(DIC):
                            dve.wait_ge(dt_done, DIC * j + c + 1)
                            dve.tensor_tensor(u[:, c, chunk(j, CW)], dt[:, c, chunk(j, CW)], xs[:, c, chunk(j, CW)], ALU.mult)

                @block.sync
                def _(sp):
                    sp.wait_ge(bc_used, NCH)
                    for hh in range(2):
                        sp.dma_start(b_dram[hh * NST:(hh + 1) * NST, :], bc_sb[0:NST, hh * HW:(hh + 1) * HW]).then_inc(bc_stored, 16)
                        sp.dma_start(c_dram[hh * NST:(hh + 1) * NST, :], bc_sb[NST:2 * NST, hh * HW:(hh + 1) * HW]).then_inc(bc_stored, 16)
                    sp.wait_ge(bc_stored, 64)

            b_loaded, c_loaded = k.sems("mamba_b_loaded", 2), k.sems("mamba_c_loaded", 2)
            skip_ready = k.sem("mamba_skip_ready")
            decay_ready, input_ready = k.sem("mamba_decay_ready"), k.sem("mamba_input_ready")
            state_ready, out_ready, summed = k.sem("mamba_state_ready"), k.sem("mamba_out_ready"), k.sem("mamba_summed")
            y_ready, y_done = k.sem("mamba_y_ready"), k.sem("mamba_y_done")
            QH = NST * DIC
            with ExitStack() as c2:
                b_all = k.sb(c2, "mamba_b_all", [P, 2, HW])
                c_all = k.sb(c2, "mamba_c_all", [P, 2, HW])
                decay = k.sb(c2, "mamba_decay", [P, 2, HW])
                fed = k.sb(c2, "mamba_fed", [P, 2, HW])
                state = k.sb(c2, "mamba_state", [P, 2, HW])
                read = k.sb(c2, "mamba_read", [P, 2, HW])
                skip_diag = k.sb(c2, "mamba_skip_diag", [P, DIC, P])
                y = k.ps(c2, "mamba_y", [P, DIC, 2, 512])
                block = c2.enter_context(nc.Block())
                by_batch = [decay[:, s].rearrange("p (b l) -> p b l", l=L) for s in range(2)]

                def load(sp, n, s):
                    sp.dma_start(b_all[:, s], b_dram[ds(n, 1), :].partition_broadcast(P)).then_inc(b_loaded[s], 16)
                    sp.dma_start(c_all[:, s], c_dram[ds(n, 1), :].partition_broadcast(P)).then_inc(c_loaded[s], 16)

                @block.sync
                def _(sp):
                    for s in range(2):
                        load(sp, s, s)
                    with loop(sp, 2 * NST - 2, 2) as n:
                        for s in range(2):
                            sp.wait_ge(out_ready, 2 + DIC * (n + s + 1))
                            after_wait(sp, g)
                            load(sp, n + s + 2, s)

                @block.scalar
                def _(act):
                    for hh in range(2):
                        tok = slice(hh * HW, (hh + 1) * HW)
                        with loop(act, NST, 2) as n:
                            for s in range(2):
                                for c in range(DIC):
                                    act.wait_ge(state_ready, hh * QH + DIC * (n + s) + c + 1)
                                    src = dt[:, c, tok].rearrange("p (b l) -> p b l", l=L)
                                    act.activation(by_batch[c % 2][:, :, 1:], src[:, :, 1:], ACT.Exp, scale=a_neg[:, c, ds(n + s, 1)]).then_inc(decay_ready, 1)

                @block.gpsimd
                def _(pool):
                    for hh in range(2):
                        tok = slice(hh * HW, (hh + 1) * HW)
                        with loop(pool, NST, 2) as n:
                            for s in range(2):
                                pool.wait_ge(b_loaded[s], 8 * NST * hh + 8 * n + 16)
                                for c in range(DIC):
                                    pool.wait_ge(state_ready, hh * QH + DIC * (n + s) + c + 1)
                                    pool.tensor_tensor(fed[:, c % 2], u[:, c, tok], b_all[:, s], ALU.mult).then_inc(input_ready, 1)

                @block.vector
                def _(dve):
                    for c in range(DIC):
                        diag = dve.tensor_scalar(skip_diag[:, c], g.ident[:], skip[:, c:c + 1], None, ALU.mult)
                    diag.then_inc(skip_ready, 1)
                    for s in range(2):
                        zeros = dve.memset(by_batch[s][:, :, 0:1], 0.0)
                    zeros.then_inc(state_ready, 2)
                    dve.memset(read[:, :, 0:1], 0.0).then_inc(out_ready, 2)
                    for hh in range(2):
                        tok = slice(hh * HW, (hh + 1) * HW)
                        with loop(dve, NST, 2) as n:
                            q0 = hh * QH + DIC * n

                            def scan(q):
                                dve.wait_ge(decay_ready, q0 + q + 1)
                                dve.wait_ge(input_ready, q0 + q + 1)
                                dve.wait_ge(out_ready, q0 + q + 1)
                                dve.tensor_tensor_scan(state[:, q % 2], decay[:, q % 2], fed[:, q % 2], 0.0, ALU.mult, ALU.add).then_inc(state_ready, 1)

                            def read_out(q):
                                if q % DIC == 0:
                                    dve.wait_ge(c_loaded[q // DIC], 8 * NST * hh + 8 * n + 16)
                                dve.wait_ge(state_ready, q0 + q + 3)
                                dve.wait_ge(summed, q0 + q + 1)
                                dve.tensor_tensor(read[:, q % 2], state[:, q % 2], c_all[:, q // DIC], ALU.mult).then_inc(out_ready, 1)

                            scan(0)
                            for q in range(1, 2 * DIC):
                                scan(q)
                                read_out(q - 1)
                            read_out(2 * DIC - 1)
                        dve.wait_ge(y_ready, hh + 1)
                        for c in range(DIC):
                            for w in range(2):
                                part = slice(hh * HW + w * CW, hh * HW + (w + 1) * CW)
                                dve.tensor_tensor(xs[:, c, part], y[:, c, w, 0:CW], gate[:, c, part], ALU.mult).then_inc(y_done, 1)

                @block.tensor
                def _(pe):
                    pe.wait_ge(skip_ready, 1)
                    for hh in range(2):
                        if hh:
                            pe.wait_ge(y_done, 2 * DIC * hh)
                        for c in range(DIC):
                            for w in range(2):
                                part = slice(hh * HW + w * CW, hh * HW + (w + 1) * CW)
                                mm = pe.matmul(y[:, c, w, 0:CW], skip_diag[:, c], xs[:, c, part], start=True, stop=False, skip_group_check=True)
                        if hh == 0:
                            mm.then_inc(summed, 2)
                        with loop(pe, NST, 2) as n:
                            for q in range(2 * DIC):
                                pe.wait_ge(out_ready, hh * QH + DIC * n + q + 3)
                                for w in range(2):
                                    mm = pe.matmul(y[:, q % DIC, w, 0:CW], g.ident[:], read[:, q % 2, w * CW:(w + 1) * CW], start=False, stop=False, skip_group_check=True)
                                mm.then_inc(summed, 1)
                        pe.matmul(y[0:1, 0, 0, 510:511], g.ident[:, 0:1], g.ident[:, 0:1], start=True, stop=True, skip_group_check=True).then_inc(y_ready, 1)

        add_projection(k, g, "mamba_wout", ins["mamba_w_out"], xs, DIC)


def add_projection(k, g, name, w_dram, src, kc, bias=None):
    nc = k.nc
    loaded, ready, added = k.sem(f"{name}_loaded"), k.sem(f"{name}_ready"), k.sem(f"{name}_added")
    with ExitStack() as ctx:
        w = k.sb(ctx, f"{name}_w", [P, kc, D])
        acc = k.ps(ctx, f"{name}_acc", [P, 2, DH, 512])
        block = ctx.enter_context(nc.Block())

        @block.sync
        def _(sp):
            sp.dma_start(w[:], w_dram.rearrange("(c p) n -> p c n", p=P)).then_inc(loaded, 16)

        @block.tensor
        def _(pe):
            pe.wait_ge(loaded, 16)
            with loop(pe, NCH, 2) as j:
                pe.wait_ge(added, DH * j)
                for s in range(2):
                    for m in range(DH):
                        for c in range(kc):
                            mm = pe.matmul(acc[:, s, m, 0:CW], w[:, c, m * P:(m + 1) * P], src[:, c, chunk(j + s, CW)], start=(c == 0), stop=(c == kc - 1))
                        mm.then_inc(ready, 1)

        @block.vector
        def _(dve):
            with loop(dve, NCH, 2) as j:
                for s in range(2):
                    for m in range(DH):
                        dve.wait_ge(ready, DH * (j + s) + m + 1)
                        x = g.x[:, m, chunk(j + s, CW)]
                        if bias is None:
                            dve.tensor_tensor(x, acc[:, s, m, 0:CW], x, ALU.add).then_inc(added, 1)
                        else:
                            dve.scalar_tensor_tensor(x, acc[:, s, m, 0:CW], bias[:, m:m + 1], x, ALU.add, ALU.add).then_inc(added, 1)


def cross_attention(k, g, ins, norm):
    nc = k.nc
    norm(g, g.x, g.xn)
    with ExitStack() as ctx:
        q = k.sb(ctx, "xattn_q", [P, DH, T])
        merged = k.sb(ctx, "xattn_merged", [P, DH, T])
        bias = k.sb(ctx, "xattn_bias", [P, 2 * DH + 2 * DH + DH + DH])
        bq, bk, bv, bo = bias[:, 0:4], bias[:, 4:8], bias[:, 8:10], bias[:, 10:12]
        rope = k.sb(ctx, "xattn_rope", [P, 2 * (L + S2)])
        q_cos, q_sin = rope[:, 0:L], rope[:, L:2 * L]
        k_cos, k_sin = rope[:, 2 * L:2 * L + S2], rope[:, 2 * L + S2:]
        w_kv = k.sb(ctx, "xattn_w_kv", [P, DH, 3 * D])
        own_head = k.sb(ctx, "xattn_own_head", [P, HPT])
        keep = k.sb(ctx, "xattn_keep", [L, B * S2], U8)
        small_loaded, kv_loaded = k.sem("xattn_small_loaded"), k.sem("xattn_kv_loaded")

        q_ready, q_cosed, q_sined, q_done = k.sem("xattn_q_ready"), k.sem("xattn_q_cosed"), k.sem("xattn_q_sined"), k.sem("xattn_q_done")
        with ExitStack() as c2:
            w_q = k.sb(c2, "xattn_w_q", [P, DH, 2 * D])
            tmp = k.sb(c2, "xattn_q_tmp", [P, 2, DH, CW])
            qp = k.ps(c2, "xattn_qp", [P, 2, DH, 512])
            block = c2.enter_context(nc.Block())

            @block.sync
            def _(sp):
                sp.dma_start(w_q[:], ins["xattn_w_q"].rearrange("(h p) n -> p h n", p=P)).then_inc(small_loaded, 16)
                sp.dma_start(bias[:], ins["xattn_bias"]).then_inc(small_loaded, 16)
                sp.dma_start(rope[:], ins["xattn_rope"]).then_inc(small_loaded, 16)
                sp.dma_start(own_head[:], ins["xattn_own_head"]).then_inc(small_loaded, 16)
                sp.dma_start(w_kv[:], ins["xattn_w_kv"].rearrange("(h p) n -> p h n", p=P)).then_inc(kv_loaded, 16)
                sp.dma_start(keep[:], ins["xattn_keep"].partition_broadcast(L)).then_inc(kv_loaded, 16)
                sp.wait_ge(kv_loaded, 32)

            @block.tensor
            def _(pe):
                pe.wait_ge(small_loaded, 64)
                with loop(pe, NCH) as j:
                    pe.wait_ge(q_sined, DH * j)
                    for m in range(DH):
                        for swap in range(2):
                            at = (swap * DH + m) * P
                            for h in range(DH):
                                mm = pe.matmul(qp[:, swap, m, 0:CW], w_q[:, h, at:at + P], g.xn[:, h, chunk(j, CW)], start=(h == 0), stop=(h == DH - 1))
                        mm.then_inc(q_ready, 1)

            @block.vector
            def _(dve):
                dve.wait_ge(small_loaded, 64)

                def turned(out, m, swap, table):
                    src = qp[:, swap, m, 0:CW].rearrange("p (b l) -> p b l", l=L)
                    table = table.unsqueeze(1).to_broadcast([P, BPC, L])
                    return dve.scalar_tensor_tensor(out.rearrange("p (b l) -> p b l", l=L), src, bq[:, swap * DH + m:swap * DH + m + 1], table, ALU.add, ALU.mult)

                with loop(dve, NCH) as j:
                    dve.wait_ge(q_done, DH * j)
                    for m in range(DH):
                        dve.wait_ge(q_ready, DH * j + m + 1)
                        turned(tmp[:, 0, m], m, 0, q_cos).then_inc(q_cosed, 1)
                        turned(tmp[:, 1, m], m, 1, q_sin).then_inc(q_sined, 1)

            @block.gpsimd
            def _(pool):
                with loop(pool, NCH) as j:
                    for m in range(DH):
                        pool.wait_ge(q_cosed, DH * j + m + 1)
                        pool.wait_ge(q_sined, DH * j + m + 1)
                        pool.tensor_tensor(q[:, m, chunk(j, CW)], tmp[:, 0, m], tmp[:, 1, m], ALU.add).then_inc(q_done, 1)

        ctx_loaded = k.sems("xattn_ctx_loaded", 2)
        kproj_ready, k_read, k_summed = k.sem("xattn_kproj_ready"), k.sem("xattn_k_read"), k.sem("xattn_k_summed")
        k_cosed, v_ready, v_read = k.sem("xattn_k_cosed"), k.sem("xattn_v_ready"), k.sem("xattn_v_read")
        blocked, mask_ready = k.sem("xattn_blocked"), k.sem("xattn_mask_ready")
        s_ready, biased, p_ready, t_ready = k.sem("xattn_s_ready"), k.sem("xattn_biased"), k.sem("xattn_p_ready"), k.sem("xattn_t_ready")
        pt_ready, pv_done = k.sems("xattn_pt_ready", 2), k.sem("xattn_pv_done")
        inverted, o_normed, o_turned, o_stored = k.sem("xattn_inverted"), k.sem("xattn_o_normed"), k.sem("xattn_o_turned"), k.sem("xattn_o_stored")
        CK = S2 // KC
        with ExitStack() as c2:
            context = k.sb(c2, "xattn_context", [P, 2, DH, S2])
            kT = k.sb(c2, "xattn_kT", [P, 2, DH, S2])
            turn = k.sb(c2, "xattn_turn", [P, 2, DH, S2])
            v = k.sb(c2, "xattn_v", [KC, 2, CK, D])
            qb = k.sb(c2, "xattn_qb", [P, 2, DH, HPT, L])
            mask = k.sb(c2, "xattn_mask", [L, 2, S2])
            sm = k.sb(c2, "xattn_sm", [L, 2, S2])
            least = k.sb(c2, "xattn_least", [L, 2, NHEAD])
            prob = k.sb(c2, "xattn_prob", [L, 2, S2])
            total = k.sb(c2, "xattn_total", [L, 2, NHEAD])
            pt = k.sb(c2, "xattn_pt", [KC, 2, CK, L])
            o_sb = k.sb(c2, "xattn_o_sb", [L, 2, D])
            kv_ps = k.ps(c2, "xattn_kv_ps", [P, 2, 512])
            s_ps = k.ps(c2, "xattn_s_ps", [P, 2, 512])
            pt_ps = k.ps(c2, "xattn_pt_ps", [P, 2, 512])
            o_ps = k.ps(c2, "xattn_o_ps", [P, 512])
            ot_ps = k.ps(c2, "xattn_ot_ps", [P, 512])
            block = c2.enter_context(nc.Block())
            ot_view = ot_ps[:, 0:DH * L].rearrange("p (h l) -> p h l", h=DH)

            @block.sync
            def _(sp):
                def load(b, s):
                    sp.dma_start(context[:, s], ins["ctxT"][ds(b, 1)].rearrange("b (h p) t -> p (b h) t", p=P)).then_inc(ctx_loaded[s], 16)

                for s in range(2):
                    load(s, s)
                with loop(sp, B - 2, 2) as b:
                    for s in range(2):
                        sp.wait_ge(v_ready, b + s + 1)
                        load(b + s + 2, s)
                sp.wait_ge(v_ready, B - 1)
                load(B, 0)

            @block.gpsimd
            def _(pool):
                def spread(b, s):
                    for m in range(DH):
                        src = q[:, m, chunk(b, L)].unsqueeze(1).to_broadcast([P, HPT, L])
                        own = own_head[:].unsqueeze(2).to_broadcast([P, HPT, L])
                        pool.tensor_tensor(qb[:, s, m], src, own, ALU.mult).then_inc(blocked, 1)

                for s in range(2):
                    spread(s, s)
                with loop(pool, B - 2, 2) as b:
                    for s in range(2):
                        pool.wait_ge(s_ready, NHEAD * (b + s + 1))
                        spread(b + s + 2, s)

            @block.tensor
            def _(pe):
                def k_half(b, s, m):
                    if m == 0:
                        pe.wait_ge(ctx_loaded[s], 8 * (b - s) + 16)
                        pe.wait_ge(v_read, b)
                    else:
                        pe.wait_ge(k_read, DH * b + 1)
                    for swap in range(2):
                        at = (swap * DH + m) * P
                        for h in range(DH):
                            mm = pe.matmul(kv_ps[:, swap, 0:S2], w_kv[:, h, at:at + P], context[:, s, h], start=(h == 0), stop=(h == DH - 1))
                    mm.then_inc(kproj_ready, 1)

                def values(b, s):
                    pe.wait_ge(k_read, DH * b + 2)
                    for c in range(CK):
                        for h in range(DH):
                            mm = pe.matmul(kv_ps[0:KC, c // 2, (c % 2) * D:(c % 2 + 1) * D], context[:, s, h, c * KC:(c + 1) * KC], w_kv[:, h, 2 * D:], start=(h == 0), stop=(h == DH - 1))
                    mm.then_inc(v_ready, 1)

                def scores(b, s, h):
                    if h % HPT == 0:
                        pe.wait_ge(blocked, DH * b + h // HPT + 1)
                        pe.wait_ge(k_summed, DH * b + h // HPT + 1)
                    pe.wait_ge(biased, NHEAD * b + h + 1)
                    pe.matmul(s_ps[0:L, h % 2, 0:S2], qb[:, s, h // HPT, h % HPT], kT[:, s, h // HPT], start=True, stop=True).then_inc(s_ready, 1)

                def turn_probs(b, h):
                    pe.wait_ge(p_ready, NHEAD * b + h + 1)
                    pe.wait_ge(pt_ready[h % 2], NHEAD // 2 * b + h // 2)
                    for c in range(CK):
                        mm = pe.transpose(pt_ps[0:KC, h % 2, c * L:(c + 1) * L], prob[:, h % 2, c * KC:(c + 1) * KC], g.ident[0:L, 0:L])
                    mm.then_inc(t_ready, 1)

                def weigh(b, s, h):
                    pe.wait_ge(pt_ready[h % 2], NHEAD // 2 * b + h // 2 + 1)
                    if h == 0:
                        pe.wait_ge(v_read, b + 1)
                    for c in range(CK):
                        mm = pe.matmul(o_ps[0:L, h * HD:(h + 1) * HD], pt[:, h % 2, c], v[:, s, c, h * HD:(h + 1) * HD], start=(c == 0), stop=(c == CK - 1))
                    mm.then_inc(pv_done, 1)

                def batch(b, s):
                    for h in range(NHEAD + 2):
                        if h < NHEAD:
                            scores(b, s, h)
                        if 1 <= h <= NHEAD:
                            turn_probs(b, h - 1)
                        if h >= 2:
                            weigh(b, s, h - 2)
                        if h == 6:
                            k_half(b + 1, 1 - s, 0)
                        if h == 9:
                            k_half(b + 1, 1 - s, 1)
                        if h == 12:
                            values(b + 1, 1 - s)
                    pe.wait_ge(o_normed, b + 1)
                    pe.wait_ge(o_stored, b)
                    for m in range(DH):
                        mm = pe.transpose(ot_ps[:, m * L:(m + 1) * L], o_sb[:, s, m * P:(m + 1) * P], g.ident[0:L, 0:L])
                    mm.then_inc(o_turned, 1)

                pe.wait_ge(kv_loaded, 32)
                k_half(0, 0, 0)
                k_half(0, 0, 1)
                values(0, 0)
                with loop(pe, B, 2) as b:
                    for s in range(2):
                        batch(b + s, s)

            @block.vector
            def _(dve):
                def keys(b, s, m):
                    dve.wait_ge(kproj_ready, DH * b + m + 1)
                    dve.scalar_tensor_tensor(turn[:, 0, m], kv_ps[:, 0, 0:S2], bk[:, m:m + 1], k_cos, ALU.add, ALU.mult).then_inc(k_cosed, 1)
                    dve.scalar_tensor_tensor(turn[:, 1, m], kv_ps[:, 1, 0:S2], bk[:, DH + m:DH + m + 1], k_sin, ALU.add, ALU.mult).then_inc(k_read, 1)
                    dve.wait_ge(k_cosed, DH * b + m + 1)
                    dve.wait_ge(k_read, DH * b + m + 1)
                    dve.tensor_tensor(kT[:, s, m], turn[:, 0, m], turn[:, 1, m], ALU.add).then_inc(k_summed, 1)

                def bias_scores(b, s, h):
                    dve.wait_ge(s_ready, NHEAD * b + h + 1)
                    dve.wait_ge(p_ready, NHEAD * b + h - 1) if h >= 2 else dve.wait_ge(p_ready, NHEAD * b)
                    after_wait(dve, g)
                    dve.tensor_tensor_reduce(sm[:, h % 2], s_ps[0:L, h % 2, 0:S2], mask[:, s], -SCALE, BIG, ALU.add, ALU.min, least[:, s, h:h + 1]).then_inc(biased, 1)

                def copy_probs(b, h):
                    dve.wait_ge(t_ready, NHEAD * b + h + 1)
                    dve.wait_ge(pv_done, NHEAD * b + h - 1) if h >= 2 else dve.wait_ge(pv_done, NHEAD * b)
                    dve.tensor_copy(pt[:, 0], pt_ps[0:KC, 0, 0:CK * L].rearrange("p (c l) -> p c l", l=L)).then_inc(pt_ready[0], 1)

                dve.memset(sm[:, :, 0:1], 0.0).then_inc(biased, 2)
                dve.wait_ge(biased, 2)
                for m in range(DH):
                    keys(0, 0, m)
                with loop(dve, B, 2) as b0:
                    for s in range(2):
                        b = b0 + s
                        dve.tensor_scalar(mask[:, s], keep[:, chunk(b, S2)], -1.0, BIG, ALU.add, ALU.mult).then_inc(mask_ready, 1)
                        dve.wait_ge(mask_ready, b + 1)
                        for h in range(NHEAD + 2):
                            if h < NHEAD:
                                bias_scores(b, s, h)
                            if h >= 2 and h % 2 == 0:
                                copy_probs(b, h - 2)
                            if h in (7, 10):
                                keys(b + 1, 1 - s, (h - 7) // 3)
                        dve.wait_ge(p_ready, NHEAD * (b + 1))
                        dve.reciprocal(total[:, s], total[:, s]).then_inc(inverted, 1)
                        dve.wait_ge(inverted, b + 1)
                        dve.wait_ge(pv_done, NHEAD * (b + 1))
                        dve.tensor_tensor(o_sb[:, s].rearrange("p (n d) -> p n d", d=HD), o_ps[0:L, 0:D].rearrange("p (n d) -> p n d", d=HD),
                                          total[:, s].unsqueeze(2).to_broadcast([L, NHEAD, HD]), ALU.mult).then_inc(o_normed, 1)

            @block.scalar
            def _(act):
                def copy_values(b, s):
                    act.wait_ge(v_ready, b + 1)
                    for c in range(CK):
                        last = act.activation(v[:, s, c], kv_ps[0:KC, c // 2, (c % 2) * D:(c % 2 + 1) * D], ACT.Copy)
                    last.then_inc(v_read, 1)

                def exponentiate(b, s, h):
                    act.wait_ge(biased, NHEAD * b + h + 3)
                    act.wait_ge(t_ready, NHEAD * b + h - 1) if h >= 2 else act.wait_ge(t_ready, NHEAD * b)
                    act.activation(prob[:, h % 2], sm[:, h % 2], ACT.Exp, bias=least[:, s, h:h + 1], scale=-1.0, accum_out=total[:, s, h:h + 1]).then_inc(p_ready, 1)

                def copy_probs(b, h):
                    act.wait_ge(t_ready, NHEAD * b + h + 1)
                    act.wait_ge(pv_done, NHEAD * b + h - 1) if h >= 2 else act.wait_ge(pv_done, NHEAD * b)
                    act.activation(pt[:, 1], pt_ps[0:KC, 1, 0:CK * L].rearrange("p (c l) -> p c l", l=L), ACT.Copy).then_inc(pt_ready[1], 1)

                copy_values(0, 0)
                with loop(act, B, 2) as b0:
                    for s in range(2):
                        b = b0 + s
                        for h in range(NHEAD + 2):
                            if h < NHEAD:
                                exponentiate(b, s, h)
                            if h >= 3 and h % 2 == 1:
                                copy_probs(b, h - 2)
                            if h == 14:
                                act.wait_ge(pv_done, NHEAD * b)
                                copy_values(b + 1, 1 - s)
                        act.wait_ge(o_turned, b + 1)
                        for m in range(DH):
                            last = act.activation(merged[:, m, chunk(b, L)], ot_view[:, m], ACT.Identity, bias=bv[:, m:m + 1])
                        last.then_inc(o_stored, 1)

        add_projection(k, g, "xattn_wo", ins["xattn_w_o"], merged, DH, bo)


def min_gru(k, g, ins, norm):
    nc = k.nc
    norm(g, g.x, g.xn)
    loaded = k.sem("gru_loaded")
    hidden_ready, gate_ready, z_done, forget_done = k.sem("gru_hidden_ready"), k.sem("gru_gate_ready"), k.sem("gru_z_done"), k.sem("gru_forget_done")
    raised, fed_done, scanned, cleared = k.sem("gru_raised"), k.sem("gru_fed_done"), k.sem("gru_scanned"), k.sem("gru_cleared")
    out_ready, added = k.sem("gru_out_ready"), k.sem("gru_added")
    with ExitStack() as ctx:
        w = k.sb(ctx, "gru_w", [P, DH, 2 * DI])
        w_out = k.sb(ctx, "gru_w_out", [P, DIC, D])
        z = k.sb(ctx, "gru_z", [P, DIC, CW])
        forget = k.sb(ctx, "gru_forget", [P, DIC, CW])
        fed = k.sb(ctx, "gru_fed", [P, DIC, CW])
        state = k.sb(ctx, "gru_state", [P, DIC, CW])
        hid = k.ps(ctx, "gru_hid", [P, 2, 512])
        gat = k.ps(ctx, "gru_gat", [P, 2, 512])
        acc = k.ps(ctx, "gru_acc", [P, DH, 512])
        block = ctx.enter_context(nc.Block())

        @block.sync
        def _(sp):
            sp.dma_start(w[:], ins["gru_w"].rearrange("(h p) n -> p h n", p=P)).then_inc(loaded, 16)
            sp.dma_start(w_out[:], ins["gru_w_out"].rearrange("(c p) n -> p c n", p=P)).then_inc(loaded, 16)

        @block.tensor
        def _(pe):
            pe.wait_ge(loaded, 32)
            with loop(pe, NCH) as j:
                for c in range(DIC):
                    pe.wait_ge(raised, DIC * j + c - 1) if c >= 2 else pe.wait_ge(raised, DIC * j)
                    for h in range(DH):
                        mm = pe.matmul(hid[:, c % 2, 0:CW], w[:, h, c * P:(c + 1) * P], g.xn[:, h, chunk(j, CW)], start=(h == 0), stop=(h == DH - 1))
                    mm.then_inc(hidden_ready, 1)
                    pe.wait_ge(forget_done, DIC * j + c - 1) if c >= 2 else pe.wait_ge(forget_done, DIC * j)
                    for h in range(DH):
                        mm = pe.matmul(gat[:, c % 2, 0:CW], w[:, h, DI + c * P:DI + (c + 1) * P], g.xn[:, h, chunk(j, CW)], start=(h == 0), stop=(h == DH - 1))
                    mm.then_inc(gate_ready, 1)
                pe.wait_ge(added, DH * j)
                pe.wait_ge(scanned, DIC * (j + 1))
                for m in range(DH):
                    for c in range(DIC):
                        mm = pe.matmul(acc[:, m, 0:CW], w_out[:, c, m * P:(m + 1) * P], state[:, c], start=(c == 0), stop=(c == DIC - 1))
                    mm.then_inc(out_ready, 1)

        @block.scalar
        def _(act):
            act.wait_ge(cleared, 1)
            with loop(act, NCH) as j:
                for c in range(DIC):
                    act.wait_ge(gate_ready, DIC * j + c + 1)
                    act.wait_ge(scanned, DIC * j)
                    act.activation(z[:, c], gat[:, c % 2, 0:CW], ACT.Sigmoid).then_inc(z_done, 1)
                    src = gat[:, c % 2, 0:CW].rearrange("p (b l) -> p b l", l=L)
                    dst = forget[:, c].rearrange("p (b l) -> p b l", l=L)
                    act.activation(dst[:, :, 1:], src[:, :, 1:], ACT.Sigmoid, scale=-1.0).then_inc(forget_done, 1)

        @block.vector
        def _(dve):
            dve.memset(forget[:].rearrange("p c (b l) -> p (c b) l", l=L)[:, :, 0:1], 0.0).then_inc(cleared, 1)
            with loop(dve, NCH) as j:
                dve.wait_ge(out_ready, DH * j)
                for c in range(DIC):
                    n = DIC * j + c + 1
                    dve.wait_ge(hidden_ready, n)
                    dve.tensor_scalar(fed[:, c], hid[:, c % 2, 0:CW], 0.0, 0.5, ALU.max, ALU.add).then_inc(raised, 1)
                    dve.wait_ge(raised, n)
                    dve.wait_ge(z_done, n)
                    dve.tensor_tensor(fed[:, c], fed[:, c], z[:, c], ALU.mult).then_inc(fed_done, 1)
                    dve.wait_ge(fed_done, n)
                    dve.wait_ge(forget_done, n)
                    dve.tensor_tensor_scan(state[:, c], forget[:, c], fed[:, c], 0.0, ALU.mult, ALU.add).then_inc(scanned, 1)
                for m in range(DH):
                    dve.wait_ge(out_ready, DH * j + m + 1)
                    x = g.x[:, m, chunk(j, CW)]
                    dve.tensor_tensor(x, acc[:, m, 0:CW], x, ALU.add).then_inc(added, 1)


def delay_attention(k, g, ins, norm):
    nc = k.nc
    norm(g, g.x, g.xn)
    twice = k.dram("delay_weights", [B, 2 * L])
    w_loaded = k.sem("delay_w_loaded")
    with ExitStack() as ctx:
        values = k.sb(ctx, "delay_values", [L, B, D])
        spectrum = k.sb(ctx, "delay_spectrum", [L, B])
        circ = k.sb(ctx, "delay_circ", [L, B, L])
        merged = k.sb(ctx, "delay_merged", [P, DH, T])
        bias = k.sb(ctx, "delay_bias", [P, 2 * DH])
        dft = k.sb(ctx, "delay_dft", [L, L])
        idft = k.sb(ctx, "delay_idft", [L, L])

        ctx_loaded = k.sems("delay_ctx_loaded", 2)
        staged, proj_ready, v_ready, qk_copied, v_copied = k.sem("delay_staged"), k.sem("delay_proj_ready"), k.sem("delay_v_ready"), k.sem("delay_qk_copied"), k.sem("delay_v_copied")
        dft_ready, kf_copied, crossed, summed = k.sem("delay_dft_ready"), k.sem("delay_kf_copied"), k.sem("delay_crossed"), k.sem("delay_summed")
        with ExitStack() as c2:
            w = k.sb(c2, "delay_w", [P, DH, 3 * D])
            b_qk = k.sb(c2, "delay_b_qk", [1, 2 * D])
            xq = k.sb(c2, "delay_xq", [P, 2, DH, L])
            xk = k.sb(c2, "delay_xk", [P, 2, DH, L])
            qk = k.sb(c2, "delay_qk", [L, 2, 2 * D])
            kf = k.sb(c2, "delay_kf", [L, 2, D])
            cross = k.sb(c2, "delay_cross", [L, 2, D])
            qk_ps = k.ps(c2, "delay_qk_ps", [P, 2, 512])
            v_ps = k.ps(c2, "delay_v_ps", [P, 2, 512])
            f_ps = k.ps(c2, "delay_f_ps", [P, 2, 512])
            block = c2.enter_context(nc.Block())

            @block.sync
            def _(sp):
                def load(b, s):
                    sp.dma_start(xk[:, s], ins["ctxT"][ds(b, 1), :, 0:L].rearrange("b (h p) t -> p (b h) t", p=P)).then_inc(ctx_loaded[s], 16)

                sp.dma_start(w[:], ins["delay_w"].rearrange("(h p) n -> p h n", p=P)).then_inc(w_loaded, 16)
                sp.dma_start(b_qk[:], ins["delay_b_qk"]).then_inc(w_loaded, 16)
                sp.dma_start(dft[:], ins["delay_dft"]).then_inc(w_loaded, 16)
                sp.dma_start(idft[:], ins["delay_idft"]).then_inc(w_loaded, 16)
                sp.dma_start(bias[:], ins["delay_bias"]).then_inc(w_loaded, 16)
                for s in range(2):
                    load(s, s)
                with loop(sp, B - 2, 2) as b:
                    for s in range(2):
                        sp.wait_ge(v_ready, b + s + 1)
                        load(b + s + 2, s)
                sp.wait_ge(w_loaded, 80)

            @block.gpsimd
            def _(pool):
                def stage(b, s):
                    pool.tensor_copy(xq[:, s], g.xn[:, :, chunk(b, L)]).then_inc(staged, 1)

                for s in range(2):
                    stage(s, s)
                with loop(pool, B - 2, 2) as b:
                    for s in range(2):
                        pool.wait_ge(proj_ready, b + s + 1)
                        stage(b + s + 2, s)

            @block.tensor
            def _(pe):
                pe.wait_ge(w_loaded, 80)

                def project(b, s):
                    pe.wait_ge(qk_copied, b)
                    pe.wait_ge(staged, b + 1 + s)
                    pe.wait_ge(ctx_loaded[s], 8 * b + 16)
                    pe.matmul(qk_ps[0:L, s], g.ones[0:1, 0:L], b_qk[:], start=True, stop=False, skip_group_check=True)
                    for n, src in enumerate((xq, xk)):
                        for h in range(DH):
                            mm = pe.matmul(qk_ps[0:L, s, n * D:(n + 1) * D], src[:, s, h], w[:, h, n * D:(n + 1) * D], start=False, stop=(h == DH - 1), skip_group_check=True)
                    mm.then_inc(proj_ready, 1)
                    pe.wait_ge(v_copied, b)
                    for h in range(DH):
                        mm = pe.matmul(v_ps[0:L, s, 0:D], xk[:, s, h], w[:, h, 2 * D:], start=(h == 0), stop=(h == DH - 1))
                    mm.then_inc(v_ready, 1)

                def transform(b, s):
                    pe.wait_ge(qk_copied, b + s + 1)
                    pe.wait_ge(crossed, b)
                    pe.matmul(f_ps[0:L, s], dft[:], qk[:, s], start=True, stop=True).then_inc(dft_ready, 1)

                with loop(pe, B, 2) as b:
                    for s in range(2):
                        project(b, s)
                    for s in range(2):
                        transform(b, s)

            @block.scalar
            def _(act):
                with loop(act, B, 2) as b:
                    act.wait_ge(dft_ready, b)
                    for s in range(2):
                        act.wait_ge(proj_ready, b + s + 1)
                        act.activation(qk[:, s], qk_ps[0:L, s], ACT.Copy).then_inc(qk_copied, 1)
                    act.wait_ge(crossed, b)
                    for s in range(2):
                        act.wait_ge(dft_ready, b + s + 1)
                        act.activation(kf[:, s], f_ps[0:L, s, D:], ACT.Copy).then_inc(kf_copied, 1)

            @block.vector
            def _(dve):
                with loop(dve, B, 2) as b:
                    for s in range(2):
                        dve.wait_ge(v_ready, b + s + 1)
                        dve.tensor_copy(values[:, ds(b + s, 1)].rearrange("p b d -> p (b d)"), v_ps[0:L, s, 0:D]).then_inc(v_copied, 1)
                    dve.wait_ge(summed, b)
                    for s in range(2):
                        dve.wait_ge(kf_copied, b + s + 1)
                        dve.tensor_tensor(cross[:, s], f_ps[0:L, s, 0:D], kf[:, s], ALU.mult).then_inc(crossed, 1)
                    for s in range(2):
                        dve.wait_ge(crossed, b + s + 1)
                        dve.tensor_reduce(spectrum[:, ds(b + s, 1)], cross[:, s], AX, ALU.add).then_inc(summed, 1)
                dve.wait_ge(summed, B)

        corr_ready, picked = k.sem("delay_corr_ready"), k.sem("delay_picked")
        weights_ready, exp_ready, stored, circ_loaded = k.sem("delay_weights_ready"), k.sem("delay_exp_ready"), k.sem("delay_stored"), k.sem("delay_circ_loaded")
        with ExitStack() as c2:
            corr = k.sb(c2, "delay_corr", [B, L])
            rest = k.sb(c2, "delay_rest", [B, L])
            rest2 = k.sb(c2, "delay_rest2", [B, L])
            top = k.sb(c2, "delay_top", [B, 8])
            ninth = k.sb(c2, "delay_ninth", [B, 8])
            shift = k.sb(c2, "delay_shift", [B, 1])
            chosen = k.sb(c2, "delay_chosen", [B, L])
            power = k.sb(c2, "delay_power", [B, L])
            share = k.sb(c2, "delay_share", [B, 1])
            weight2 = k.sb(c2, "delay_weight2", [B, 2, L])
            corr_ps = k.ps(c2, "delay_corr_ps", [P, 512])
            block = c2.enter_context(nc.Block())

            @block.tensor
            def _(pe):
                pe.matmul(corr_ps[0:B, 0:L], spectrum[:], idft[:], start=True, stop=True).then_inc(corr_ready, 1)

            @block.vector
            def _(dve):
                pick = Steps(dve, picked)

                def then(ins):
                    pick.did(ins)
                    pick.wait()

                dve.wait_ge(corr_ready, 1)
                then(dve.tensor_copy(corr[:], corr_ps[0:B, 0:L]))
                then(dve.max(top[:], corr[:]))
                then(dve.match_replace(rest[:], top[:], corr[:], -BIG))
                then(dve.max(ninth[:], rest[:]))
                then(dve.memset(ninth[:, 1:], -BIG))
                then(dve.match_replace(rest2[:], ninth[:], rest[:], -BIG))
                then(dve.tensor_scalar(chosen[:], rest2[:], -BIG, None, ALU.is_equal))
                then(dve.tensor_scalar(shift[:], top[:, 0:1], -1.0, None, ALU.mult))
                dve.wait_ge(exp_ready, 1)
                then(dve.tensor_tensor(chosen[:], chosen[:], power[:], ALU.mult))
                then(dve.tensor_reduce(share[:], chosen[:], AX, ALU.add))
                then(dve.reciprocal(share[:], share[:]))
                for n in range(2):
                    dve.tensor_scalar(weight2[:, n], chosen[:], share[:, 0:1], None, ALU.mult).then_inc(weights_ready, 1)

            @block.scalar
            def _(act):
                act.wait_ge(picked, 8)
                act.activation(power[:], corr[:], ACT.Exp, bias=shift[:]).then_inc(exp_ready, 1)

            @block.sync
            def _(sp):
                sp.wait_ge(weights_ready, 2)
                sp.dma_start(twice, weight2[:].rearrange("b n l -> b (n l)")).then_inc(stored, 16)
                sp.wait_ge(stored, 16)
                for b in range(B):
                    window = bass.AP(twice.tensor, b * 2 * L + 1, [[1, L], [1, L]])
                    sp.dma_start(circ[:, b], window).then_inc(circ_loaded, 16)
                sp.wait_ge(circ_loaded, 16 * B)

        shifted, kept = k.sem("delay_shifted"), k.sem("delay_kept")
        with ExitStack() as c2:
            agg = k.ps(c2, "delay_agg", [P, 2, DH, 512])
            block = c2.enter_context(nc.Block())

            @block.tensor
            def _(pe):
                for b in range(B):
                    if b >= 2:
                        pe.wait_ge(kept, b - 1)
                    for m in range(DH):
                        mm = pe.matmul(agg[:, b % 2, m, 0:L], values[:, b, m * P:(m + 1) * P], circ[:, b], start=True, stop=True)
                    mm.then_inc(shifted, 1)

            @block.vector
            def _(dve):
                for b in range(B):
                    dve.wait_ge(shifted, b + 1)
                    for m in range(DH):
                        last = dve.tensor_scalar(merged[:, m, b * L:(b + 1) * L], agg[:, b % 2, m, 0:L][:, ::-1], bias[:, m:m + 1], None, ALU.add)
                    last.then_inc(kept, 1)

        add_projection(k, g, "delay_wo", ins["delay_w_o"], merged, DH, bias[:, DH:])


def token_tiles(k, g, name, tok):
    nc = k.nc
    staged, turned, copied = k.sem(f"{name}_staged"), k.sem(f"{name}_turned"), k.sem(f"{name}_copied")
    with ExitStack() as ctx:
        stage = k.sb(ctx, f"{name}_stage", [P, 2, DH, P])
        ps = k.ps(ctx, f"{name}_ps", [P, 2, 512])
        block = ctx.enter_context(nc.Block())

        @block.gpsimd
        def _(pool):
            with loop(pool, TT, 2) as t:
                pool.wait_ge(turned, t)
                for s in range(2):
                    pool.tensor_copy(stage[:, s], g.xn[:, :, chunk(t + s, P)]).then_inc(staged, 1)

        @block.tensor
        def _(pe):
            with loop(pe, TT, 2) as t:
                pe.wait_ge(copied, t)
                for s in range(2):
                    pe.wait_ge(staged, t + s + 1)
                    for h in range(DH):
                        mm = pe.transpose(ps[:, s, h * P:(h + 1) * P], stage[:, s, h], g.ident[:])
                    mm.then_inc(turned, 1)

        @block.vector
        def _(dve):
            with loop(dve, TT, 2) as t:
                for s in range(2):
                    dve.wait_ge(turned, t + s + 1)
                    dve.tensor_copy(tok[:, ds(t + s, 1)].rearrange("p a d -> p (a d)"), ps[:, s, 0:D]).then_inc(copied, 1)
            dve.wait_ge(copied, TT)


def soft_experts(k, g, ins, norm):
    nc = k.nc
    norm(g, g.x, g.xn)
    HN = NP_ // 2
    NC = NP_ // P
    y_dram = k.dram("soft_y", [PS, NE, D])
    with ExitStack() as ctx:
        xt = k.sb(ctx, "soft_xt", [P, NC, D])

        with ExitStack() as c1:
            tok = k.sb(c1, "soft_tok", [P, TT, D])
            token_tiles(k, g, "soft_tiles", tok)

            loaded, staged = k.sem("soft_d_loaded"), k.sem("soft_d_staged")
            lg_ready, biased, maxed, lowered, exped = k.sem("soft_d_lg_ready"), k.sem("soft_d_biased"), k.sem("soft_d_maxed"), k.sem("soft_d_lowered"), k.sem("soft_d_exped")
            summed, inverted, shared, mixed = k.sem("soft_d_summed"), k.sem("soft_d_inverted"), k.sem("soft_d_shared"), k.sem("soft_d_mixed")
            cleared, mix_ready, clipped = k.sem("soft_d_cleared"), k.sem("soft_d_mix_ready"), k.sem("soft_d_clipped")
            GN = HN // PS
            with ExitStack() as c2:
                phi = k.sb(c2, "soft_phi", [P, DH, NP_])
                phi_b = k.sb(c2, "soft_phi_b", [P, NP_])
                stage = k.sb(c2, "soft_stage", [P, 2, DH, P])
                logit = k.sb(c2, "soft_logit", [P, 2, HN])
                share = k.sb(c2, "soft_share", [P, 2, HN])
                high = k.sb(c2, "soft_high", [P, 2, GN])
                total = k.sb(c2, "soft_total", [P, 2, GN])
                zero = k.sb(c2, "soft_zero", [1, 512])
                lg = k.ps(c2, "soft_lg", [P, 2, HN])
                mix = k.ps(c2, "soft_mix", [P, HN // P, D])
                block = c2.enter_context(nc.Block())

                def groups(tile, s):
                    return tile[:, s].rearrange("p (n q) -> p n q", q=PS)

                @block.sync
                def _(sp):
                    sp.dma_start(phi[:], ins["soft_phi"].rearrange("(h p) n -> p h n", p=P)).then_inc(loaded, 16)
                    sp.dma_start(phi_b[:], ins["soft_phi_b"].partition_broadcast(P)).then_inc(loaded, 16)

                @block.tensor
                def _(pe):
                    def logits(a, t, s):
                        pe.wait_ge(staged, a * TT + t + 1)
                        for w in range(HN // 512):
                            at = a * HN + w * 512
                            for h in range(DH):
                                mm = pe.matmul(lg[:, s, w * 512:(w + 1) * 512], stage[:, s, h], phi[:, h, at:at + 512], start=(h == 0), stop=(h == DH - 1))
                        mm.then_inc(lg_ready, 1)

                    def mixtures(a, t, s):
                        pe.wait_ge(shared, a * TT + t + 1)
                        for c in range(HN // P):
                            mm = pe.matmul(mix[:, c], share[:, s, c * P:(c + 1) * P], tok[:, ds(t, 1)].rearrange("p a d -> p (a d)"), start=False, stop=False, skip_group_check=True)
                        mm.then_inc(mixed, 1)

                    pe.wait_ge(loaded, 32)
                    pe.wait_ge(cleared, 1)
                    for a in range(2):
                        if a:
                            pe.wait_ge(clipped, a)
                        for w in range(HN // P * D // 512):
                            pe.matmul(mix[:].rearrange("p c d -> p (c d)")[:, w * 512:(w + 1) * 512], zero[:, 0:P], zero[:], start=True, stop=False, skip_group_check=True)
                        for s in range(2):
                            if a:
                                pe.wait_ge(biased, a * TT)
                            logits(a, s, s)
                        with loop(pe, TT - 2, 2) as t:
                            for s in range(2):
                                pe.wait_ge(biased, a * TT + t + s + 1)
                                logits(a, t + s + 2, s)
                                mixtures(a, t + s, s)
                        for s in range(2):
                            mixtures(a, TT - 2 + s, s)
                        pe.matmul(lg[0:1, 0, 0:1], zero[:, 0:1], zero[:, 0:1], start=True, stop=True, skip_group_check=True).then_inc(mix_ready, 1)

                @block.vector
                def _(dve):
                    def lower(a, t, s):
                        n = a * TT + t + 1
                        dve.wait_ge(lg_ready, n)
                        dve.wait_ge(shared, a * TT + t - 1) if not isinstance(t, int) or t >= 2 or a else None
                        dve.tensor_tensor(logit[:, s], lg[:, s], phi_b[:, a * HN:(a + 1) * HN], ALU.add).then_inc(biased, 1)
                        dve.wait_ge(biased, n)
                        dve.tensor_reduce(high[:, s], groups(logit, s), AX, ALU.max).then_inc(maxed, 1)
                        dve.wait_ge(maxed, n)
                        dve.tensor_tensor(groups(logit, s), groups(logit, s), high[:, s].unsqueeze(2).to_broadcast([P, GN, PS]), ALU.subtract).then_inc(lowered, 1)

                    def invert(a, t, s):
                        n = a * TT + t + 1
                        dve.wait_ge(exped, n)
                        dve.tensor_reduce(total[:, s], groups(logit, s), AX, ALU.add).then_inc(summed, 1)
                        dve.wait_ge(summed, n)
                        dve.reciprocal(total[:, s], total[:, s]).then_inc(inverted, 1)

                    dve.memset(zero[:], 0.0).then_inc(cleared, 1)
                    dve.wait_ge(loaded, 32)
                    for a in range(2):
                        lower(a, 0, 0)
                        lower(a, 1, 1)
                        with loop(dve, TT - 2, 2) as t:
                            for s in range(2):
                                invert(a, t + s, s)
                                lower(a, t + s + 2, s)
                        for s in range(2):
                            invert(a, TT - 2 + s, s)
                        dve.wait_ge(mix_ready, a + 1)
                        for c in range(HN // P):
                            last = dve.tensor_scalar(xt[:, a * (HN // P) + c], mix[:, c], -33000.0, 65000.0, ALU.max, ALU.min)
                        last.then_inc(clipped, 1)
                    dve.wait_ge(clipped, 2)

                @block.scalar
                def _(act):
                    for a in range(2):
                        with loop(act, TT, 2) as t:
                            for s in range(2):
                                act.wait_ge(lowered, a * TT + t + s + 1)
                                act.activation(logit[:, s], logit[:, s], ACT.Exp).then_inc(exped, 1)

                @block.gpsimd
                def _(pool):
                    def stage_tile(t, s):
                        pool.tensor_copy(stage[:, s], g.xn[:, :, chunk(t, P)]).then_inc(staged, 1)

                    def normalise(a, t, s):
                        pool.wait_ge(inverted, a * TT + t + 1)
                        pool.wait_ge(mixed, a * TT + t - 1) if not isinstance(t, int) or t >= 2 or a else None
                        pool.tensor_tensor(groups(share, s), groups(logit, s), total[:, s].unsqueeze(2).to_broadcast([P, GN, PS]), ALU.mult).then_inc(shared, 1)

                    for a in range(2):
                        for s in range(2):
                            if a:
                                pool.wait_ge(lg_ready, a * TT)
                            stage_tile(s, s)
                        for s in range(2):
                            pool.wait_ge(lg_ready, a * TT + s + 1)
                            stage_tile(2 + s, s)
                        for s in range(2):
                            normalise(a, s, s)
                        with loop(pool, TT - 4, 2) as t:
                            for s in range(2):
                                pool.wait_ge(lg_ready, a * TT + t + s + 3)
                                stage_tile(t + s + 4, s)
                                normalise(a, t + s + 2, s)
                        for s in range(2):
                            normalise(a, TT - 2 + s, s)

        stats, var_ready, std_ready, rstd_ready = k.sem("soft_e_stats"), k.sem("soft_e_var_ready"), k.sem("soft_e_std_ready"), k.sem("soft_e_rstd_ready")
        e_loaded = k.sems("soft_e_loaded", 2)
        normed, bent, turned, copied = k.sem("soft_e_normed"), k.sem("soft_e_bent"), k.sem("soft_e_turned"), k.sem("soft_e_copied")
        y_ready, y_copied, y_stored = k.sem("soft_e_y_ready"), k.sem("soft_e_y_copied"), k.sems("soft_e_y_stored", 2)
        EC = P // PS
        with ExitStack() as c2:
            stat = k.sb(c2, "soft_stat", [P, 2, 6])
            moments = k.sb(c2, "soft_moments", [P, NC, 2])
            rstd = k.sb(c2, "soft_rstd", [P, NC])
            w = k.sb(c2, "soft_w", [P, 2, EC, DH, D])
            w_b = k.sb(c2, "soft_w_b", [1, 2, EC * D])
            xa = k.sb(c2, "soft_xa", [P, 2, D])
            xh = k.sb(c2, "soft_xh", [P, 2, D])
            xhT = k.sb(c2, "soft_xhT", [P, 2, DH, P])
            y_sb = k.sb(c2, "soft_y_sb", [PS, 2, EC * D])
            tp = k.ps(c2, "soft_tp", [P, 2, 512])
            yp = k.ps(c2, "soft_yp", [P, 2, EC * D])
            block = c2.enter_context(nc.Block())

            @block.sync
            def _(sp):
                def load(c, s):
                    sp.dma_start(w[:, s], ins["soft_w"][ds(c * EC, EC)].rearrange("n (h p) d -> p n h d", p=P)).then_inc(e_loaded[s], 16)
                    sp.dma_start(w_b[:, s], ins["soft_w_b"][ds(c, 1)]).then_inc(e_loaded[s], 16)

                def store(c, s):
                    sp.wait_ge(y_copied, c + s + 1)
                    sp.dma_start(y_dram[:, ds((c + s) * EC, EC), :].rearrange("q n d -> q (n d)"), y_sb[:, s]).then_inc(y_stored[s], 16)

                for s in range(2):
                    load(s, s)
                with loop(sp, NC - 2, 2) as c:
                    for s in range(2):
                        sp.wait_ge(y_ready, c + s + 1)
                        load(c + s + 2, s)
                        store(c, s)
                for s in range(2):
                    store(NC - 2, s)
                for s in range(2):
                    sp.wait_ge(y_stored[s], 8 * NC)

            @block.vector
            def _(dve):
                st = Steps(dve, stats)
                for c in range(NC):
                    st.did(dve.bn_stats(stat[:, c % 2], xt[:, c]))
                    st.wait()
                    dve.bn_aggr(moments[:, c], stat[:, c % 2]).then_inc(var_ready, 1)
                dve.wait_ge(std_ready, 1)
                dve.reciprocal(rstd[:], rstd[:]).then_inc(rstd_ready, 1)
                dve.wait_ge(rstd_ready, 1)
                dve.wait_ge(var_ready, NC)

                def normalise(c, s):
                    one = lambda tile: tile[:, ds(c, 1)] if isinstance(c, int) else tile[:, ds(c, 1)]
                    dve.tensor_scalar(xa[:, s], xt[:, ds(c, 1)].rearrange("p a d -> p (a d)"), moments[:, ds(c, 1), 0], rstd[:, ds(c, 1)], ALU.subtract, ALU.mult).then_inc(normed, 1)

                def copy(c, s):
                    dve.wait_ge(turned, c + 1)
                    dve.wait_ge(y_ready, c - s)
                    dve.tensor_copy(xhT[:, s], tp[:, s, 0:D].rearrange("p (h q) -> p h q", h=DH)).then_inc(copied, 1)

                for s in range(2):
                    normalise(s, s)
                with loop(dve, NC - 2, 2) as c:
                    for s in range(2):
                        copy(c + s, s)
                        dve.wait_ge(bent, c + s + 1)
                        normalise(c + s + 2, s)
                for s in range(2):
                    copy(NC - 2 + s, s)

            @block.scalar
            def _(act):
                act.wait_ge(var_ready, NC)
                act.activation(rstd[:], moments[:, :, 1], ACT.Sqrt, bias=g.eps[:]).then_inc(std_ready, 1)
                with loop(act, NC, 2) as c:
                    for s in range(2):
                        act.wait_ge(normed, c + s + 1)
                        act.wait_ge(turned, c)
                        act.activation(xh[:, s], xa[:, s], ACT.Tanh).then_inc(bent, 1)
                    for s in range(2):
                        act.wait_ge(y_ready, c + s + 1)
                        act.wait_ge(y_stored[s], 8 * c)
                        act.activation(y_sb[:, s], yp[0:PS, s], ACT.Copy).then_inc(y_copied, 1)

            @block.tensor
            def _(pe):
                with loop(pe, NC, 2) as c:
                    for s in range(2):
                        pe.wait_ge(bent, c + s + 1)
                        pe.wait_ge(copied, c)
                        for h in range(DH):
                            mm = pe.transpose(tp[:, s, h * P:(h + 1) * P], xh[:, s, h * P:(h + 1) * P], g.ident[:])
                        mm.then_inc(turned, 1)
                    for s in range(2):
                        pe.wait_ge(e_loaded[s], 16 * c + 32)
                        pe.wait_ge(copied, c + s + 1)
                        pe.wait_ge(y_copied, c)
                        after_wait(pe, g)
                        for i in range(EC):
                            out = yp[0:PS, s, i * D:(i + 1) * D]
                            pe.matmul(out, g.ones[:, 0:PS], w_b[:, s, i * D:(i + 1) * D], start=True, stop=False, skip_group_check=True)
                            for h in range(DH):
                                mm = pe.matmul(out, xhT[:, s, h, i * PS:(i + 1) * PS], w[:, s, i, h], start=False, stop=(h == DH - 1), skip_group_check=True)
                        mm.then_inc(y_ready, 1)

        loaded, staged = k.sem("soft_c_loaded"), k.sem("soft_c_staged")
        lg_ready, biased, maxed, lowered, exped = k.sem("soft_c_lg_ready"), k.sem("soft_c_biased"), k.sem("soft_c_maxed"), k.sem("soft_c_lowered"), k.sem("soft_c_exped")
        summed, inverted, shared = k.sem("soft_c_summed"), k.sem("soft_c_inverted"), k.sem("soft_c_shared")
        turned, copied, y_ready, added = k.sem("soft_c_turned"), k.sem("soft_c_copied"), k.sem("soft_c_y_ready"), k.sem("soft_c_added")
        HC = HN // P
        GN = HN // NE
        with ExitStack() as c2:
            phi = k.sb(c2, "soft_phi2", [P, DH, NP_])
            phi_b = k.sb(c2, "soft_phi2_b", [P, NP_])
            y = k.sb(c2, "soft_yt", [P, NC, D])
            stage = k.sb(c2, "soft_stage2", [P, 2, DH, P])
            logit = k.sb(c2, "soft_logit2", [P, 2, HN])
            share = k.sb(c2, "soft_share2", [P, 2, HN])
            shareT = k.sb(c2, "soft_shareT", [P, 2, HN])
            high = k.sb(c2, "soft_high2", [P, 2, GN])
            total = k.sb(c2, "soft_total2", [P, 2, GN])
            lg = k.ps(c2, "soft_lg2", [P, 2, HN])
            ct = k.ps(c2, "soft_ct", [P, HN])
            acc = k.ps(c2, "soft_acc", [P, 2, 512])
            block = c2.enter_context(nc.Block())

            def groups(tile, a):
                return tile[:, a].rearrange("p (q n) -> p q n", n=NE)

            @block.sync
            def _(sp):
                sp.dma_start(phi[:], ins["soft_phi2"].rearrange("(h p) n -> p h n", p=P)).then_inc(loaded, 16)
                sp.dma_start(phi_b[:], ins["soft_phi2_b"].partition_broadcast(P)).then_inc(loaded, 16)
                sp.dma_start(y[:], y_dram.rearrange("q n d -> (q n) d").rearrange("(c p) d -> p c d", p=P)).then_inc(loaded, 16)

            @block.gpsimd
            def _(pool):
                def stage_tile(t, s):
                    pool.tensor_copy(stage[:, s], g.xn[:, :, chunk(t, P)]).then_inc(staged, 1)

                def normalise(t, a, first=False):
                    pool.wait_ge(inverted, 2 * t + a + 1)
                    if not first:
                        pool.wait_ge(turned, 2 * t + a - 1)
                    pool.tensor_tensor(groups(share, a), groups(logit, a), total[:, a].unsqueeze(2).to_broadcast([P, GN, NE]), ALU.mult).then_inc(shared, 1)

                for s in range(2):
                    stage_tile(s, s)
                for a in range(2):
                    normalise(0, a, True)
                with loop(pool, TT - 2, 2) as t:
                    for s in range(2):
                        pool.wait_ge(lg_ready, 2 * (t + s) + 2)
                        stage_tile(t + s + 2, s)
                        for a in range(2):
                            normalise(t + s + 1, a)
                for a in range(2):
                    normalise(TT - 1, a)

            @block.tensor
            def _(pe):
                def logits(t, s, a):
                    if a == 0:
                        pe.wait_ge(staged, t + 1)
                    for w in range(HN // 512):
                        at = a * HN + w * 512
                        for h in range(DH):
                            mm = pe.matmul(lg[:, a, w * 512:(w + 1) * 512], stage[:, s, h], phi[:, h, at:at + 512], start=(h == 0), stop=(h == DH - 1))
                    mm.then_inc(lg_ready, 1)

                def turn(t, a):
                    pe.wait_ge(shared, 2 * t + a + 1)
                    pe.wait_ge(copied, 2 * t + a)
                    for c in range(HC):
                        mm = pe.transpose(ct[:, c * P:(c + 1) * P], share[:, a, c * P:(c + 1) * P], g.ident[:])
                    mm.then_inc(turned, 1)

                def combine(t, s, a):
                    pe.wait_ge(copied, 2 * t + a + 1)
                    for m in range(DH):
                        for c in range(HC):
                            mm = pe.matmul(acc[:, s, m * P:(m + 1) * P], y[:, a * HC + c, m * P:(m + 1) * P], shareT[:, a, c * P:(c + 1) * P],
                                           start=(a == 0 and m == 0 and c == 0), stop=(a == 1 and c == HC - 1), skip_group_check=True)
                    if a:
                        mm.then_inc(y_ready, 1)

                def tile(t, s, last=False):
                    for a in range(2):
                        turn(t, a)
                        if not last:
                            pe.wait_ge(biased, 2 * t + a + 1)
                            logits(t + 1, 1 - s, a)
                        if a == 0:
                            pe.wait_ge(added, t)
                        combine(t, s, a)

                pe.wait_ge(loaded, 48)
                for a in range(2):
                    logits(0, 0, a)
                with loop(pe, TT - 2, 2) as t:
                    for s in range(2):
                        tile(t + s, s)
                for s in range(2):
                    tile(TT - 2 + s, s, s == 1)

            @block.vector
            def _(dve):
                def lower(t, a, first=False):
                    n = 2 * t + a + 1
                    dve.wait_ge(lg_ready, n)
                    if not first:
                        dve.wait_ge(shared, 2 * t + a - 1)
                    dve.tensor_tensor(logit[:, a], lg[:, a], phi_b[:, a * HN:(a + 1) * HN], ALU.add).then_inc(biased, 1)
                    dve.wait_ge(biased, n)
                    dve.tensor_reduce(high[:, a], groups(logit, a), AX, ALU.max).then_inc(maxed, 1)
                    dve.wait_ge(maxed, n)
                    dve.tensor_tensor(groups(logit, a), groups(logit, a), high[:, a].unsqueeze(2).to_broadcast([P, GN, NE]), ALU.subtract).then_inc(lowered, 1)

                def invert(t, a):
                    n = 2 * t + a + 1
                    dve.wait_ge(exped, n)
                    dve.tensor_reduce(total[:, a], groups(logit, a), AX, ALU.add).then_inc(summed, 1)
                    dve.wait_ge(summed, n)
                    dve.reciprocal(total[:, a], total[:, a]).then_inc(inverted, 1)

                def add(t, s):
                    dve.wait_ge(y_ready, t + 1)
                    x = g.x[:, :, chunk(t, P)]
                    dve.tensor_tensor(x, acc[:, s, 0:D].rearrange("p (h q) -> p h q", h=DH), x, ALU.add).then_inc(added, 1)

                dve.memset(high[:, :, 0:1], 0.0).then_inc(added, 1)
                dve.wait_ge(added, 1)
                dve.wait_ge(loaded, 48)
                for a in range(2):
                    lower(0, a, True)
                for a in range(2):
                    invert(0, a)
                    lower(1, a)
                with loop(dve, TT - 2, 2) as t:
                    for s in range(2):
                        for a in range(2):
                            invert(t + s + 1, a)
                            lower(t + s + 2, a)
                        add(t + s, s)
                for a in range(2):
                    invert(TT - 1, a)
                for s in range(2):
                    add(TT - 2 + s, s)

            @block.scalar
            def _(act):
                def exponentiate(t, a):
                    act.wait_ge(lowered, 2 * t + a + 1)
                    act.activation(logit[:, a], logit[:, a], ACT.Exp).then_inc(exped, 1)

                def copy(t, a):
                    act.wait_ge(turned, 2 * t + a + 1)
                    act.wait_ge(y_ready, t)
                    act.activation(shareT[:, a], ct[:], ACT.Copy).then_inc(copied, 1)

                for a in range(2):
                    exponentiate(0, a)
                with loop(act, TT - 1) as t:
                    for a in range(2):
                        exponentiate(t + 1, a)
                        copy(t, a)
                for a in range(2):
                    copy(TT - 1, a)


def pipelined(eng, n, ring, steps):
    lag = len(steps) - 1

    def at(time, slot):
        for behind, step in enumerate(steps):
            tile = time - behind
            if not isinstance(tile, int) or 0 <= tile < n:
                step(tile, (slot - behind) % ring)

    first = -(-(ring + lag) // ring) * ring
    rounds = (n - first) // ring
    for time in range(first):
        at(time, time % ring)
    if rounds > 0:
        with eng.Fori(0, rounds) as r:
            for slot in range(ring):
                at(r * ring + (first + slot), slot)
    for time in range(first + max(rounds, 0) * ring, n + lag):
        at(time, time % ring)


def after_wait(eng, g):
    eng.sem_inc(g.waits_passed, 1)


def wait(eng, sem, value):
    if not isinstance(value, int) or value > 0:
        eng.wait_ge(sem, value)


def routed_experts(k, g, ins, norm):
    nc = k.nc
    norm(g, g.x, g.xn)
    tok_dram = k.dram("moe_tok", [T, D])
    list_dram = k.dram("moe_list", [NSLOT, 1], I32)
    expert_dram = k.dram("moe_expert", [2 * P], I32)
    y_dram = k.dram("moe_y", [NSLOT, D])
    with ExitStack() as ctx:
        slot = k.sb(ctx, "moe_slot", [P, TT, TOPK], I32)
        place = k.sb(ctx, "moe_place", [P, TT * TOPK], I32)
        weight = k.sb(ctx, "moe_weight", [P, TT, TOPK])
        token = k.sb(ctx, "moe_token", [P, TT], I32)
        loaded = k.sem("moe_loaded")
        tok_stored, list_cleared, expert_stored = k.sem("moe_tok_stored"), k.sem("moe_list_cleared"), k.sem("moe_expert_stored")

        with ExitStack() as c1:
            tok = k.sb(c1, "moe_tok_sb", [P, TT, D])
            token_tiles(k, g, "moe_tiles", tok)

            lt_ready, lt_copied, lg_ready, score_ready = k.sem("moe_lt_ready"), k.sem("moe_lt_copied"), k.sem("moe_lg_ready"), k.sem("moe_score_ready")
            stepped, chosen_ready, cum_ready, rank_ready, id_ready = k.sem("moe_stepped"), k.sem("moe_chosen_ready"), k.sem("moe_cum_ready"), k.sem("moe_rank_ready"), k.sem("moe_id_ready")
            with ExitStack() as c2:
                def sb(name, shape, dt=F32):
                    return k.sb(c2, f"moe_{name}", shape, dt)

                gate_w = sb("gate_w", [P, DH, E])
                gate_b = sb("gate_b", [P, E])
                before = sb("before", [P, P])
                all_ones = sb("all_ones", [P, P])
                tri = sb("tri", [P, NG, NG])
                tile_id = sb("tile_id", [P, 2])
                logitT = sb("logitT", [E, T])
                score = sb("score", [P, TT, E])
                choice = sb("choice", [P, TT, E])
                pair = sb("pair", [P, TT * NG, EG])
                pair_best = sb("pair_best", [P, EG - 1, TT * NG])
                group = sb("group", [P, TT * NG])
                larger = sb("larger", [P, TT, NG, NG])
                equal = sb("equal", [P, TT, NG, NG])
                ahead = sb("ahead", [P, TT * NG])
                masked = sb("masked", [P, TT, E])
                best = sb("best", [P, TT, TOPK])
                marked = sb("marked", [P, TT, E])
                chosen = sb("chosen", [P, TT, E])
                share = sb("share", [P, TT, E])
                total = sb("total", [P, TT])
                cum = sb("cum", [P, TT + 1, E])
                count = sb("count", [P, E])
                count_i = sb("count_i", [P, E], I32)
                tiles_i = sb("tiles_i", [P, E], I32)
                tiles = sb("tiles", [P, E])
                ends = sb("ends", [P, E])
                base = sb("base", [P, E])
                one_row = sb("one_row", [P, E])
                key = sb("key", [P, TT, E])
                key8 = sb("key8", [P, TT, TOPK])
                match = sb("match", [P, TOPK, E])
                low_i = sb("low_i", [P, TT * TOPK], I32)
                high_i = sb("high_i", [P, TT * TOPK], I32)
                low = sb("low", [P, TT * TOPK])
                ended = sb("ended", [P, 2, E])
                expert_f = sb("expert_f", [P, 2])
                expert = sb("expert", [P, 2], I32)
                zeros = sb("zeros", [P, SLOT_TILES], I32)
                lt_ps = k.ps(c2, "moe_lt_ps", [P, 2, 512])
                lg_ps = k.ps(c2, "moe_lg_ps", [P, 2, 512])
                rank_ps = k.ps(c2, "moe_rank_ps", [P, 2, 512])
                count_ps = k.ps(c2, "moe_count_ps", [P, 512])
                block = c2.enter_context(nc.Block())
                HT = TT // 2

                @block.sync
                def _(sp):
                    sp.dma_start(gate_w[:], ins["moe_gate_w"].rearrange("(h p) e -> p h e", p=P)).then_inc(loaded, 16)
                    sp.dma_start(gate_b[:], ins["moe_gate_b"].partition_broadcast(P)).then_inc(loaded, 16)
                    sp.dma_start(before[:], ins["moe_before"]).then_inc(loaded, 16)
                    sp.dma_start(tri[:], ins["moe_tri"].partition_broadcast(P)).then_inc(loaded, 16)
                    sp.dma_start(tile_id[:], ins["moe_tile_id"]).then_inc(loaded, 16)
                    sp.dma_start(token[:], ins["moe_token"]).then_inc(loaded, 16)
                    sp.dma_start(tok_dram.rearrange("(t p) d -> p t d", p=P), tok[:]).then_inc(tok_stored, 16)
                    sp.wait_ge(chosen_ready, 1)
                    sp.dma_start(list_dram.rearrange("(p i) n -> p (i n)", p=P), zeros[:]).then_inc(list_cleared, 16)
                    sp.wait_ge(id_ready, 1)
                    with nc.allow_non_contiguous_dma(reason="one word for each tile of slots"):
                        sp.dma_start(expert_dram.rearrange("(j p) -> p j", p=P), expert[:]).then_inc(expert_stored, 16)
                    sp.wait_ge(tok_stored, 16)
                    sp.wait_ge(list_cleared, 16)
                    sp.wait_ge(expert_stored, 16)

                @block.tensor
                def _(pe):
                    pe.wait_ge(loaded, 96)
                    for j in range(NCH):
                        if j >= 2:
                            pe.wait_ge(lt_copied, j - 1)
                        for h in range(DH):
                            mm = pe.matmul(lt_ps[0:E, j % 2, 0:CW], gate_w[:, h], g.xn[:, h, j * CW:(j + 1) * CW], start=(h == 0), stop=(h == DH - 1))
                        mm.then_inc(lt_ready, 1)
                    pe.wait_ge(lt_copied, NCH)
                    for t in range(TT):
                        mm = pe.transpose(lg_ps[:, t // HT, t % HT * E:(t % HT + 1) * E], logitT[:, t * P:(t + 1) * P], g.ident[0:E, 0:E])
                    mm.then_inc(lg_ready, 1)
                    pe.wait_ge(cum_ready, 1)
                    for w in range(2):
                        part = slice(w * HT, (w + 1) * HT)
                        pe.matmul(rank_ps[:, w, 0:HT * E], before[:], chosen[:, part].rearrange("p t e -> p (t e)"), start=True, stop=False)
                        pe.matmul(rank_ps[:, w, 0:HT * E], all_ones[:], cum[:, part].rearrange("p t e -> p (t e)"), start=False, stop=True)
                    pe.matmul(count_ps[:, 0:E], all_ones[:], cum[:, TT], start=True, stop=True).then_inc(rank_ready, 1)

                @block.scalar
                def _(act):
                    for j in range(NCH):
                        act.wait_ge(lt_ready, j + 1)
                        act.activation(logitT[:, j * CW:(j + 1) * CW], lt_ps[0:E, j % 2, 0:CW], ACT.Copy).then_inc(lt_copied, 1)
                    act.wait_ge(lg_ready, 1)
                    act.activation(score[:].rearrange("p (w t) e -> p w (t e)", w=2), lg_ps[:, :, 0:HT * E], ACT.Sigmoid).then_inc(score_ready, 1)

                @block.vector
                def _(dve):
                    steps = Steps(dve, stepped)

                    def then(ins):
                        steps.did(ins)
                        steps.wait()

                    dve.memset(zeros[:], 0)
                    dve.memset(all_ones[:], 1.0)
                    dve.memset(one_row[:], 1.0)
                    dve.memset(cum[:, 0], 0.0).then_inc(chosen_ready, 1)
                    dve.wait_ge(loaded, 96)
                    dve.wait_ge(score_ready, 1)
                    then(dve.tensor_tensor(choice[:], score[:], gate_b[:].unsqueeze(1).to_broadcast([P, TT, E]), ALU.add))
                    by_group = choice[:].rearrange("p t (a b) -> p (t a) b", b=EG)
                    for d in range(1, EG):
                        then(dve.tensor_tensor(pair[:, :, :EG - d], by_group[:, :, :EG - d], by_group[:, :, d:], ALU.add))
                        then(dve.tensor_reduce(pair_best[:, d - 1], pair[:, :, :EG - d], AX, ALU.max))
                    then(dve.tensor_reduce(group[:], pair_best[:].rearrange("p d a -> p a d"), AX, ALU.max))
                    own = group[:].rearrange("p (t a) -> p t a", a=NG)
                    mine = own.unsqueeze(3).to_broadcast([P, TT, NG, NG])
                    other = own.unsqueeze(2).to_broadcast([P, TT, NG, NG])
                    then(dve.tensor_tensor(larger[:], other, mine, ALU.is_gt))
                    then(dve.tensor_tensor(equal[:], other, mine, ALU.is_equal))
                    flat = lambda a: a[:].rearrange("p t a b -> p t (a b)")
                    then(dve.tensor_tensor(flat(equal), flat(equal), tri[:].rearrange("p a b -> p (a b)").unsqueeze(1).to_broadcast([P, TT, NG * NG]), ALU.mult))
                    then(dve.tensor_tensor(larger[:], larger[:], equal[:], ALU.add))
                    then(dve.tensor_reduce(ahead[:], larger[:].rearrange("p t a b -> p (t a) b"), AX, ALU.add))
                    then(dve.tensor_scalar(ahead[:], ahead[:], TOPG - 0.5, None, ALU.is_lt))
                    then(dve.tensor_tensor(masked[:].rearrange("p t (a b) -> p (t a) b", b=EG), by_group, ahead[:].unsqueeze(2).to_broadcast([P, TT * NG, EG]), ALU.mult))
                    for t in range(TT):
                        last = dve.max(best[:, t], masked[:, t])
                    then(last)
                    for t in range(TT):
                        last = dve.match_replace(marked[:, t], best[:, t], masked[:, t], -BIG)
                    then(last)
                    then(dve.tensor_scalar(chosen[:], marked[:], -BIG, None, ALU.is_equal))
                    for t in range(TT):
                        add = dve.tensor_tensor(cum[:, t + 1], cum[:, t], chosen[:, t], ALU.add)
                        if t < TT - 1:
                            then(add)
                    add.then_inc(cum_ready, 1)
                    then(dve.tensor_tensor(share[:], score[:], chosen[:], ALU.mult))
                    then(dve.tensor_reduce(total[:], share[:], AX, ALU.add))
                    then(dve.tensor_scalar(total[:], total[:], 1e-20, None, ALU.add))
                    then(dve.reciprocal(total[:], total[:]))
                    then(dve.tensor_tensor(share[:], share[:], total[:].unsqueeze(2).to_broadcast([P, TT, E]), ALU.mult))
                    then(dve.tensor_scalar(share[:], share[:], 2.5, None, ALU.mult))
                    dve.wait_ge(rank_ready, 1)
                    then(dve.tensor_scalar(count_i[:], count_ps[:, 0:E], P - 1.0, None, ALU.add))
                    then(dve.tensor_scalar(tiles_i[:], count_i[:], P.bit_length() - 1, None, ALU.arith_shift_right))
                    then(dve.tensor_copy(tiles[:], tiles_i[:]))
                    then(dve.tensor_tensor_scan(ends[:], one_row[:], tiles[:], 0.0, ALU.mult, ALU.add))
                    then(dve.tensor_tensor(base[:], ends[:], tiles[:], ALU.subtract))
                    then(dve.tensor_scalar(base[:], base[:], float(P), 1.0, ALU.mult, ALU.add))
                    for w in range(2):
                        part = slice(w * HT, (w + 1) * HT)
                        last = dve.tensor_tensor(key[:, part], rank_ps[:, w, 0:HT * E].rearrange("p (t e) -> p t e", e=E), base[:].unsqueeze(1).to_broadcast([P, HT, E]), ALU.add)
                    then(last)
                    then(dve.tensor_tensor(key[:], key[:], chosen[:], ALU.mult))
                    for t in range(TT):
                        last = dve.max(key8[:, t], key[:, t])
                    then(last)
                    then(dve.tensor_scalar(slot[:], key8[:], -1.0, None, ALU.add))
                    flat_slot = slot[:].rearrange("p t n -> p (t n)")
                    then(dve.tensor_scalar(low_i[:], flat_slot, P - 1, None, ALU.bitwise_and))
                    then(dve.tensor_scalar(high_i[:], flat_slot, P.bit_length() - 1, None, ALU.arith_shift_right))
                    then(dve.tensor_scalar(low[:], low_i[:], float(SLOT_TILES), None, ALU.mult))
                    then(dve.tensor_tensor(place[:], low[:], high_i[:], ALU.add))
                    for t in range(TT):
                        then(dve.tensor_tensor(match[:], key[:, t].unsqueeze(1).to_broadcast([P, TOPK, E]), key8[:, t].unsqueeze(2).to_broadcast([P, TOPK, E]), ALU.is_equal))
                        then(dve.tensor_tensor(match[:], match[:], share[:, t].unsqueeze(1).to_broadcast([P, TOPK, E]), ALU.mult))
                        then(dve.tensor_reduce(weight[:, t], match[:], AX, ALU.add))
                    for j in range(2):
                        last = dve.tensor_scalar(ended[:, j], ends[:], tile_id[:, j:j + 1], None, ALU.is_le)
                    then(last)
                    then(dve.tensor_reduce(expert_f[:], ended[:], AX, ALU.add))
                    dve.tensor_scalar(expert[:], expert_f[:], E - 1.0, None, ALU.min).then_inc(id_ready, 1)

        listed = k.sem("moe_listed")
        s_loaded, up_ready, silu_done, gated, down_ready, added = k.sem("moe_s_loaded"), k.sem("moe_s_up_ready"), k.sem("moe_s_silu_done"), k.sem("moe_s_gated"), k.sem("moe_s_down_ready"), k.sem("moe_s_added")
        with ExitStack() as c2:
            SC = -(-SI // P)
            rows = [min(P, SI - c * P) for c in range(SC)]
            w_up = k.sb(c2, "moe_s_w_up", [P, DH, 2 * SI])
            w_down = k.sb(c2, "moe_s_w_down", [P, SC, D])
            act_g = k.sb(c2, "moe_s_act", [P, SC, CW])
            hid = k.sb(c2, "moe_s_hid", [P, SC, CW])
            up = k.ps(c2, "moe_s_up", [P, SC, 2, 512])
            acc = k.ps(c2, "moe_s_acc", [P, DH, 512])
            block = c2.enter_context(nc.Block())

            @block.gpsimd
            def _(pool):
                for t in range(TT):
                    for n in range(TOPK):
                        at = t * TOPK + n
                        pool.indirect_dma_start(list_dram, bass.IndirectOffsetOnAxis(ap=place[:, at:at + 1], axis=0), token[:, t:t + 1], None).then_inc(listed, 16)
                pool.wait_ge(listed, 16 * TT * TOPK)

            @block.sync
            def _(sp):
                sp.dma_start(w_up[:], ins["moe_s_up"].rearrange("(h p) n -> p h n", p=P)).then_inc(s_loaded, 16)
                sp.dma_start(w_down[:], ins["moe_s_down"].rearrange("(c p) n -> p c n", p=P)).then_inc(s_loaded, 16)

            @block.tensor
            def _(pe):
                pe.wait_ge(s_loaded, 32)
                with loop(pe, NCH) as j:
                    pe.wait_ge(gated, SC * j)
                    for c in range(SC):
                        for n in range(2):
                            at = n * SI + c * P
                            for h in range(DH):
                                mm = pe.matmul(up[0:rows[c], c, n, 0:CW], w_up[:, h, at:at + rows[c]], g.xn[:, h, chunk(j, CW)], start=(h == 0), stop=(h == DH - 1))
                        mm.then_inc(up_ready, 1)
                    pe.wait_ge(gated, SC * (j + 1))
                    pe.wait_ge(added, DH * j)
                    for m in range(DH):
                        for c in range(SC):
                            mm = pe.matmul(acc[:, m, 0:CW], w_down[0:rows[c], c, m * P:(m + 1) * P], hid[0:rows[c], c], start=(c == 0), stop=(c == SC - 1))
                        mm.then_inc(down_ready, 1)

            @block.scalar
            def _(act):
                with loop(act, NCH) as j:
                    act.wait_ge(gated, SC * j)
                    for c in range(SC):
                        act.wait_ge(up_ready, SC * j + c + 1)
                        act.activation(act_g[0:rows[c], c], up[0:rows[c], c, 0, 0:CW], ACT.Silu).then_inc(silu_done, 1)

            @block.vector
            def _(dve):
                with loop(dve, NCH) as j:
                    dve.wait_ge(down_ready, DH * j)
                    for c in range(SC):
                        dve.wait_ge(silu_done, SC * j + c + 1)
                        dve.tensor_tensor(hid[0:rows[c], c], act_g[0:rows[c], c], up[0:rows[c], c, 1, 0:CW], ALU.mult).then_inc(gated, 1)
                    for m in range(DH):
                        dve.wait_ge(down_ready, DH * j + m + 1)
                        x = g.x[:, m, chunk(j, CW)]
                        dve.tensor_tensor(x, acc[:, m, 0:CW], x, ALU.add).then_inc(added, 1)

        RING = 4
        I2 = I - P
        WN = 4 * I + 2 * D
        list_loaded = k.sem("moe_list_loaded")
        staged, gathered, w_loaded = k.sem("moe_staged"), k.sems("moe_gathered", RING), k.sems("moe_w_loaded", RING)
        x_turned, x_copied, up_ready, silu_done, gated = k.sem("moe_x_turned"), k.sem("moe_x_copied"), k.sem("moe_up_ready"), k.sem("moe_silu_done"), k.sem("moe_gated")
        h_turned, h_copied, y_ready, y_copied, y_stored = k.sem("moe_h_turned"), k.sem("moe_h_copied"), k.sem("moe_y_ready"), k.sem("moe_y_copied"), k.sems("moe_y_stored", RING)
        with ExitStack() as c2:
            slot_token = k.sb(c2, "moe_slot_token", [P, SLOT_TILES], I32)
            index = k.sb(c2, "moe_index", [P, RING], I32)
            w = k.sb(c2, "moe_w", [P, RING, WN])
            xg = k.sb(c2, "moe_xg", [P, RING, D])
            xT = k.sb(c2, "moe_xT", [P, RING, D])
            act_g = k.sb(c2, "moe_act", [P, RING, I])
            hid = k.sb(c2, "moe_hid", [P, RING, I])
            hT = k.sb(c2, "moe_hT", [P, RING, 2 * P])
            y_sb = k.sb(c2, "moe_y_sb", [P, RING, D])
            x_ps = k.ps(c2, "moe_x_ps", [P, 2, 512])
            up_ps = k.ps(c2, "moe_up_ps", [P, 2, 512])
            h_ps = k.ps(c2, "moe_h_ps", [P, 2, 512])
            y_ps = k.ps(c2, "moe_y_ps", [P, 2, 512])
            block = c2.enter_context(nc.Block())
            uses = lambda t, s: (t - s) * (16 // RING)

            @block.gpsimd
            def _(pool):
                def gather(t, s):
                    wait(pool, x_turned, t - RING + 1)
                    pool.tensor_copy(index[:, s:s + 1], slot_token[:, ds(t, 1)]).then_inc(staged, 1)
                    pool.wait_ge(staged, t + 1)
                    after_wait(pool, g)
                    pool.indirect_dma_start(xg[:, s], None, tok_dram, bass.IndirectOffsetOnAxis(ap=index[:, s:s + 1], axis=0)).then_inc(gathered[s], 16)

                pool.wait_ge(list_loaded, 16)
                pipelined(pool, SLOT_TILES, RING, [gather])

            @block.sync
            def _(sp):
                def load(t, s):
                    wait(sp, y_ready, t - RING + 1)
                    after_wait(sp, g)
                    e = sp.value_load(expert_dram[ds(t, 1)].unsqueeze(0), min_val=0, max_val=E - 1)
                    sp.dma_start(w[:, s], ins["moe_w"][ds(e, 1)].rearrange("e p n -> p (e n)")).then_inc(w_loaded[s], 16)

                sp.dma_start(slot_token[:], list_dram.rearrange("(p i) n -> p (i n)", p=P)).then_inc(list_loaded, 16)
                pipelined(sp, SLOT_TILES, RING, [load])

            @block.tensor
            def _(pe):
                def turn(t, s):
                    pe.wait_ge(gathered[s], uses(t, s) + 16)
                    wait(pe, x_copied, t - 1)
                    for h in range(DH):
                        mm = pe.transpose(x_ps[:, s % 2, h * P:(h + 1) * P], xg[:, s, h * P:(h + 1) * P], g.ident[:])
                    mm.then_inc(x_turned, 1)

                def up(t, s):
                    pe.wait_ge(w_loaded[s], uses(t, s) + 16)
                    pe.wait_ge(x_copied, t + 1)
                    wait(pe, gated, t - 1)
                    for h in range(DH):
                        mm = pe.matmul(up_ps[:, s % 2, 0:2 * I], xT[:, s, h * P:(h + 1) * P], w[:, s, h * 2 * I:(h + 1) * 2 * I], start=(h == 0), stop=(h == DH - 1))
                    mm.then_inc(up_ready, 1)

                def turn_hidden(t, s):
                    pe.wait_ge(gated, t + 1)
                    wait(pe, h_copied, t - 1)
                    pe.transpose(h_ps[:, s % 2, 0:P], hid[:, s, 0:P], g.ident[:])
                    pe.transpose(h_ps[0:I2, s % 2, P:2 * P], hid[:, s, P:I], g.ident[:]).then_inc(h_turned, 1)

                def down(t, s):
                    pe.wait_ge(h_copied, t + 1)
                    wait(pe, y_copied, t - 1)
                    pe.matmul(y_ps[:, s % 2, 0:D], hT[:, s, 0:P], w[:, s, 4 * I:4 * I + D], start=True, stop=False)
                    pe.matmul(y_ps[:, s % 2, 0:D], hT[0:I2, s, P:2 * P], w[0:I2, s, 4 * I + D:4 * I + 2 * D], start=False, stop=True).then_inc(y_ready, 1)

                pipelined(pe, SLOT_TILES, RING, [turn, up, turn_hidden, down])

            @block.vector
            def _(dve):
                def copy_x(t, s):
                    dve.wait_ge(x_turned, t + 1)
                    wait(dve, up_ready, t - RING + 1)
                    dve.tensor_copy(xT[:, s], x_ps[:, s % 2, 0:D]).then_inc(x_copied, 1)

                def gate(t, s):
                    dve.wait_ge(silu_done, t + 1)
                    wait(dve, h_turned, t - RING + 1)
                    dve.tensor_tensor(hid[:, s], act_g[:, s], up_ps[:, s % 2, I:2 * I], ALU.mult).then_inc(gated, 1)

                def copy_y(t, s):
                    dve.wait_ge(y_ready, t + 1)
                    wait(dve, y_stored[s], uses(t, s))
                    dve.tensor_copy(y_sb[:, s], y_ps[:, s % 2, 0:D]).then_inc(y_copied, 1)

                pipelined(dve, SLOT_TILES, RING, [copy_x, gate, lambda t, s: None, copy_y])

            @block.scalar
            def _(act):
                def silu(t, s):
                    act.wait_ge(up_ready, t + 1)
                    wait(act, gated, t - RING + 1)
                    act.activation(act_g[:, s], up_ps[:, s % 2, 0:I], ACT.Silu).then_inc(silu_done, 1)

                def copy_hidden(t, s):
                    act.wait_ge(h_turned, t + 1)
                    wait(act, y_ready, t - RING + 1)
                    act.activation(hT[:, s, 0:P], h_ps[:, s % 2, 0:P], ACT.Copy)
                    act.activation(hT[0:I2, s, P:2 * P], h_ps[0:I2, s % 2, P:2 * P], ACT.Copy).then_inc(h_copied, 1)

                def store(t, s):
                    act.wait_ge(y_copied, t + 1)
                    act.dma_start(y_dram[ds(t * P, P), :], y_sb[:, s]).then_inc(y_stored[s], 16)

                pipelined(act, SLOT_TILES, RING, [silu, copy_hidden, store])
                for s in range(RING):
                    act.wait_ge(y_stored[s], SLOT_TILES // RING * 16)

        staged, fetched, diag_ready = k.sem("moe_f_staged"), k.sems("moe_f_fetched", 2), k.sem("moe_f_diag_ready")
        sum_ready, sum_added = k.sem("moe_f_sum_ready"), k.sem("moe_f_sum_added")
        with ExitStack() as c2:
            index = k.sb(c2, "moe_f_index", [P, 2, TOPK], I32)
            part = k.sb(c2, "moe_f_part", [P, 2, TOPK, D])
            diag = k.sb(c2, "moe_f_diag", [P, 2, TOPK, P])
            acc = k.ps(c2, "moe_f_acc", [P, 2, DH, 512])
            block = c2.enter_context(nc.Block())

            @block.gpsimd
            def _(pool):
                def fetch(t, s):
                    wait(pool, sum_ready, t - 1)
                    pool.tensor_copy(index[:, s].unsqueeze(1), slot[:, ds(t, 1)]).then_inc(staged, 1)
                    pool.wait_ge(staged, t + 1)
                    after_wait(pool, g)
                    for n in range(TOPK):
                        pool.indirect_dma_start(part[:, s, n], None, y_dram, bass.IndirectOffsetOnAxis(ap=index[:, s, n:n + 1], axis=0)).then_inc(fetched[s], 16)

                pipelined(pool, TT, 2, [fetch])

            @block.vector
            def _(dve):
                def weigh(t, s):
                    wait(dve, sum_ready, t - 1)
                    for n in range(TOPK):
                        last = dve.tensor_scalar(diag[:, s, n], g.ident[:], weight[:, ds(t, 1), n], None, ALU.mult)
                    last.then_inc(diag_ready, 1)

                def add(t, s):
                    dve.wait_ge(sum_ready, t + 1)
                    x = g.x[:, :, chunk(t, P)]
                    dve.tensor_tensor(x, acc[:, s, :, 0:P], x, ALU.add).then_inc(sum_added, 1)

                pipelined(dve, TT, 2, [weigh, add])

            @block.tensor
            def _(pe):
                def total(t, s):
                    pe.wait_ge(diag_ready, t + 1)
                    pe.wait_ge(fetched[s], (t - s) * (8 * TOPK) + 16 * TOPK)
                    wait(pe, sum_added, t - 1)
                    for m in range(DH):
                        for n in range(TOPK):
                            mm = pe.matmul(acc[:, s, m, 0:P], part[:, s, n, m * P:(m + 1) * P], diag[:, s, n], start=(n == 0), stop=(n == TOPK - 1))
                    mm.then_inc(sum_ready, 1)

                pipelined(pe, TT, 2, [total])


class State:
    pass


STAGES = [mamba, cross_attention, routed_experts, min_gru, delay_attention, soft_experts]


def decoder(nc, ins, out):
    with ExitStack() as outer:
        k = Kit(nc, outer)
        g = State()
        g.x = k.sb(outer, "x", [P, DH, T])
        g.xn = k.sb(outer, "xn", [P, DH, T])
        g.ident = k.sb(outer, "ident", [P, P])
        g.mean_w = k.sb(outer, "mean_w", [P, P])
        g.ones = k.sb(outer, "ones", [1, P])
        g.eps = k.sb(outer, "eps", [P, 1])
        g.waits_passed = k.kept_sem("waits_passed")
        load_constants(k, g, ins)
        norm = LayerNorm(k)
        for stage in STAGES:
            stage(k, g, ins, norm)
            k.end_stage()
        stored = k.sem("x_stored")
        with nc.Block() as block:
            @block.sync
            def _(sp):
                sp.dma_start(out.rearrange("(h p) t -> p h t", p=P), g.x[:]).then_inc(stored, 16)
                sp.wait_ge(stored, 16)




def by_partition(v):
    return np.ascontiguousarray(v.reshape(-1, P).T)


def rotary(n):
    freq = np.float32(1.0) / np.float32(10000.0) ** (np.arange(0, HD, 2, dtype=np.float32) / np.float32(HD))
    pos = np.float32(10.0) * (np.arange(n, dtype=np.float32) / np.float32(n))
    angle = (pos[:, None] * freq).astype(np.float32)
    row = np.arange(P) % HD
    sign = np.where(row % 2 == 0, -1.0, 1.0)[:, None]
    return (np.cos(angle).T[row // 2].astype(np.float32), (sign * np.sin(angle).T[row // 2]).astype(np.float32))


def transforms():
    t = np.arange(L)
    f_cos, f_sin = np.arange(NF + 1), np.arange(1, NF)
    turn = lambda f: 2 * np.pi * ((t[:, None] * f[None, :]) % L) / L
    there = np.concatenate([np.cos(turn(f_cos)), np.sin(turn(f_sin))], axis=1)
    times = np.where((f_cos == 0) | (f_cos == NF), 1.0, 2.0)
    times = np.concatenate([times, np.full(NF - 1, 2.0)]) / (L * D)
    return there.astype(np.float32), np.ascontiguousarray((there * times).T).astype(np.float32)


def host_layout(a):
    f = {}
    c = np.ascontiguousarray
    f["xT"] = c(a["x"].reshape(T, D).T)
    f["ident"] = np.eye(P, dtype=np.float32)
    f["mamba_small"] = c(np.concatenate([
        a["L0_attn_conv_w"], a["L0_attn_conv_b"][:, None], a["L0_attn_dt_w"][:, None], a["L0_attn_dt_b"][:, None],
        a["L0_attn_D"][:, None], a["L0_attn_A_log"]], axis=1))
    f["mamba_norm"] = c(np.stack([by_partition(a["L0_attn_norm_w"]), by_partition(a["L0_attn_norm_b"])], axis=1))
    f["mamba_w_in"] = c(a["L0_attn_W_in"])
    f["mamba_xp_w"] = c(a["L0_attn_x_proj_w"][:, 1:])
    f["mamba_dt_rep"] = c(np.repeat(a["L0_attn_x_proj_w"][:, 0:1], P, axis=1))
    f["mamba_w_out"] = c(a["L0_attn_W_out"])

    def swapped(w):
        return w.reshape(*w.shape[:-1], -1, 2)[..., ::-1].reshape(w.shape)

    w_k, w_v = a["L0_xattn_Wkv"][:, :D], a["L0_xattn_Wkv"][:, D:]
    b_k, b_v = a["L0_xattn_bkv"][:D], a["L0_xattn_bkv"][D:]
    f["xattn_w_q"] = c(np.concatenate([a["L0_xattn_Wq"], swapped(a["L0_xattn_Wq"])], axis=1))
    f["xattn_w_kv"] = c(np.concatenate([w_k, swapped(w_k), w_v], axis=1))
    f["xattn_w_o"] = c(a["L0_xattn_Wo"])
    f["xattn_bias"] = c(np.concatenate([by_partition(v) for v in (
        a["L0_xattn_bq"], swapped(a["L0_xattn_bq"]), b_k, swapped(b_k), b_v, a["L0_xattn_bo"])], axis=1))
    f["xattn_rope"] = c(np.concatenate([*rotary(L), *rotary(S2)], axis=1))
    f["xattn_own_head"] = (np.arange(P)[:, None] // HD == np.arange(HPT)).astype(np.float32)
    f["xattn_keep"] = c(a["mask_BxS2_bf1"]).reshape(B * S2).view(np.uint8)
    f["ctxT"] = np.zeros((B + 1, D, S2), np.float32)
    f["ctxT"][:B] = a["ctx_1024"].transpose(0, 2, 1)
    f["gru_w"] = c(a["L1_attn_W_hg"])
    f["gru_w_out"] = c(a["L1_attn_W_out"])
    f["delay_w"] = c(np.concatenate([a["L1_xattn_Wq"], a["L1_xattn_Wk"], a["L1_xattn_Wv"]], axis=1))
    f["delay_b_qk"] = c(np.concatenate([a["L1_xattn_bq"], a["L1_xattn_bk"]])[None])
    f["delay_w_o"] = c(a["L1_xattn_Wo"])
    f["delay_bias"] = c(np.concatenate([by_partition(a["L1_xattn_bv"]), by_partition(a["L1_xattn_bo"])], axis=1))
    f["delay_dft"], f["delay_idft"] = transforms()
    phi = a["L1_ffn_phi_w"]
    by_slot = phi.reshape(NE, PS, D).transpose(1, 0, 2).reshape(NP_, D)
    f["soft_phi"], f["soft_phi2"] = c(phi.T), c(by_slot.T)
    f["soft_phi_b"] = c(a["L1_ffn_phi_b"])
    f["soft_phi2_b"] = c(a["L1_ffn_phi_b"].reshape(NE, PS).T).reshape(-1)
    f["soft_w"] = c(a["L1_ffn_expert_w"])
    f["soft_w_b"] = c(a["L1_ffn_expert_b"]).reshape(NP_ // P, P // PS * D)
    f["moe_gate_w"], f["moe_gate_b"] = c(a["L0_ffn_gate_w"].T), c(a["L0_ffn_gate_bias"])
    f["moe_before"] = (np.arange(P)[:, None] < np.arange(P)).astype(np.float32)
    f["moe_tri"] = (np.arange(NG)[:, None] > np.arange(NG)).astype(np.float32)
    f["moe_tile_id"] = np.arange(2 * P).reshape(2, P).T.astype(np.float32)
    f["moe_token"] = c(np.arange(T).reshape(TT, P).T.astype(np.int32))
    f["moe_s_up"] = c(np.concatenate([a["L0_ffn_Sg"], a["L0_ffn_Su"]]).T)
    s_down = np.zeros((-(-SI // P) * P, D), np.float32)
    s_down[:SI] = a["L0_ffn_Sd"].T
    f["moe_s_down"] = s_down
    up = np.concatenate([a["L0_ffn_Wg"], a["L0_ffn_Wu"]], axis=1).transpose(0, 2, 1)
    f["moe_w"] = np.zeros((E, P, 4 * I + 2 * D), np.float32)
    for h in range(DH):
        f["moe_w"][:, :, h * 2 * I:(h + 1) * 2 * I] = up[:, h * P:(h + 1) * P]
    down = a["L0_ffn_Wd"].transpose(0, 2, 1)
    f["moe_w"][:, :, 4 * I:4 * I + D] = down[:, :P]
    f["moe_w"][:, :I - P, 4 * I + D:] = down[:, P:]
    return f


def kernel(**inputs):
    import concourse.bacc as bacc
    from concourse.bass_utils import run_bass_kernel_spmd

    arrays = host_layout({name: np.asarray(v) for name, v in inputs.items()})
    nc = bacc.Bacc("TRN2", target_bir_lowering=False, num_devices=1)
    ins = {name: nc.dram_tensor(name, v.shape, mybir.dt.from_np(v.dtype), kind="ExternalInput").ap() for name, v in arrays.items()}
    out = nc.dram_tensor("out", [D, T], F32, kind="ExternalOutput").ap()
    decoder(nc, ins, out)
    got = run_bass_kernel_spmd(nc, [arrays], core_ids=[0]).results[0]["out"]
    return np.ascontiguousarray(got.T.reshape(B, L, D))
```

```python
from contextlib import ExitStack, contextmanager

import numpy as np

import concourse.bass as bass
from concourse import mybir

F32 = mybir.dt.float32
I32 = mybir.dt.int32
U8 = mybir.dt.uint8
ALU = mybir.AluOpType
ACT = mybir.ActivationFunctionType
AX = mybir.AxisListType.X
ds = bass.ds

P = 128
B, L, D = 16, 112, 256
T = B * L
DH = D // P
CW = 448
NCH = T // CW
BPC = CW // L
EPS = 1e-5
DI, DIC, NST, TAPS = 512, 4, 16, 4
HW = T // 2
BPH = HW // L
S2, NHEAD, HD, KC = 375, 16, 16, 125
HPT = P // HD
SCALE = 64 ** -0.5
BIG = 3.0e38
E, I, NG, TOPG, TOPK = 64, 176, 8, 4, 8
EG = E // NG
TT = T // P
SLOT_TILES = 176
NSLOT = SLOT_TILES * P
SI = 2 * I
NF = L // 2
TOPD = 9
NE, PS = 64, 32
NP_ = NE * PS


def chunk(i, size):
    return ds(i * size, size)


@contextmanager
def loop(eng, n, step=1):
    with eng.Fori(0, n // step) as i:
        yield i * step if step > 1 else i


class Kit:

    def __init__(self, nc, outer):
        self.nc, self.outer, self.n = nc, outer, 0
        self.stage_sems = []

    def sem(self, name):
        self.stage_sems.append(self.nc.alloc_semaphore(name=name))
        return self.stage_sems[-1]

    def end_stage(self):
        self.nc.clear_and_free_semaphores(self.stage_sems)
        self.nc.all_engine_barrier()
        self.stage_sems = []

    def kept_sem(self, name):
        return self.outer.enter_context(self.nc.semaphore(name))

    def sems(self, name, n):
        return [self.sem(f"{name}{i}") for i in range(n)]

    def sb(self, ctx, name, shape, dt=F32):
        self.n += 1
        return ctx.enter_context(self.nc.sbuf_tensor(f"{name}_{self.n}", shape, dt))

    def ps(self, ctx, name, shape):
        self.n += 1
        return ctx.enter_context(self.nc.psum_tensor(f"{name}_{self.n}", shape, F32))

    def dram(self, name, shape, dt=F32):
        return self.nc.dram_tensor(name, shape, dt).ap()


class Steps:

    def __init__(self, eng, sem, base=0):
        self.eng, self.sem, self.base, self.n = eng, sem, base, 0

    def did(self, ins):
        self.n += 1
        ins.then_inc(self.sem, 1)

    def wait(self):
        self.eng.wait_ge(self.sem, self.base + self.n)


def pipelined(eng, n, ring, steps):
    lag = len(steps) - 1

    def at(time, slot):
        for behind, step in enumerate(steps):
            tile = time - behind
            if not isinstance(tile, int) or 0 <= tile < n:
                step(tile, (slot - behind) % ring)

    first = -(-(ring + lag) // ring) * ring
    rounds = (n - first) // ring
    for time in range(first):
        at(time, time % ring)
    if rounds > 0:
        with eng.Fori(0, rounds) as r:
            for slot in range(ring):
                at(r * ring + (first + slot), slot)
    for time in range(first + max(rounds, 0) * ring, n + lag):
        at(time, time % ring)


def after_wait(eng, g):
    eng.sem_inc(g.waits_passed, 1)


def wait(eng, sem, value):
    if not isinstance(value, int) or value > 0:
        eng.wait_ge(sem, value)


def load_constants(k, g, ins):
    nc = k.nc
    loaded = k.sem("constants_loaded")
    filled = k.sem("constants_filled")
    with nc.Block() as block:
        @block.sync
        def _(sp):
            sp.dma_start(g.x[:], ins["xT"].rearrange("(h p) t -> p h t", p=P)).then_inc(loaded, 16)
            sp.dma_start(g.ident[:], ins["ident"]).then_inc(loaded, 16)
            sp.wait_ge(loaded, 32)

        @block.gpsimd
        def _(pool):
            pool.memset(g.mean_w[:], 1.0 / D)
            pool.memset(g.ones[:], 1.0)
            pool.memset(g.eps[:], EPS).then_inc(filled, 1)
            pool.wait_ge(filled, 1)


class LayerNorm:
    ROWS = P // NCH

    def __init__(self, k):
        self.k, self.calls = k, 0
        self.mean_ready, self.centred, self.squared = k.kept_sem("ln_mean_ready"), k.kept_sem("ln_centred"), k.kept_sem("ln_squared")
        self.var_ready, self.std_ready, self.rstd_ready = k.kept_sem("ln_var_ready"), k.kept_sem("ln_std_ready"), k.kept_sem("ln_rstd_ready")
        self.spread, self.normed, self.done = k.kept_sem("ln_spread"), k.kept_sem("ln_normed"), k.kept_sem("ln_done")

    def __call__(self, g, src, dst, weight=None, bias=None, prefetch=None):
        k, nc, base, rows = self.k, self.k.nc, NCH * self.calls, self.ROWS
        self.calls += 1
        with ExitStack() as ctx:
            xc = k.sb(ctx, "ln_xc", [P, NCH, DH, CW])
            sq = k.sb(ctx, "ln_sq", [P, NCH, DH, CW])
            rstd = k.sb(ctx, "ln_rstd", [P, CW])
            mean = k.ps(ctx, "ln_mean", [P, NCH, 512])
            var = k.ps(ctx, "ln_var", [P, 512])
            block = ctx.enter_context(nc.Block())
            if prefetch:
                block.sync(prefetch)

            @block.tensor
            def _(pe):
                for i in range(NCH):
                    for h in range(DH):
                        mm = pe.matmul(mean[:, i, 0:CW], g.mean_w[:], src[:, h, i * CW:(i + 1) * CW], start=(h == 0), stop=(h == DH - 1))
                    mm.then_inc(self.mean_ready, 1)
                for i in range(NCH):
                    pe.wait_ge(self.squared, base + i + 1)
                    for h in range(DH):
                        mm = pe.matmul(var[i * rows:(i + 1) * rows, 0:CW], g.mean_w[:, 0:rows], sq[:, i, h], start=(h == 0), stop=(h == DH - 1), tile_position=(0, i * rows))
                    mm.then_inc(self.var_ready, 1)
                pe.wait_ge(self.rstd_ready, self.calls)
                for i in range(NCH):
                    at = slice(i * rows, i * rows + 1)
                    pe.matmul(mean[:, i, 0:CW], g.ones[at], rstd[at], start=True, stop=True, tile_position=(i * rows, 0)).then_inc(self.spread, 1)

            @block.vector
            def _(dve):
                for i in range(NCH):
                    dve.wait_ge(self.mean_ready, base + i + 1)
                    m = mean[:, i, 0:CW].unsqueeze(1).to_broadcast([P, DH, CW])
                    dve.tensor_tensor(xc[:, i], src[:, :, i * CW:(i + 1) * CW], m, ALU.subtract).then_inc(self.centred, 1)
                dve.wait_ge(self.std_ready, self.calls)
                dve.reciprocal(rstd[:], rstd[:]).then_inc(self.rstd_ready, 1)
                for i in range(NCH):
                    dve.wait_ge(self.spread, base + i + 1)
                    r = mean[:, i, 0:CW].unsqueeze(1).to_broadcast([P, DH, CW])
                    if weight is None:
                        dve.tensor_tensor(dst[:, :, i * CW:(i + 1) * CW], xc[:, i], r, ALU.mult).then_inc(self.done, 1)
                        continue
                    dve.tensor_tensor(sq[:, i], xc[:, i], r, ALU.mult).then_inc(self.normed, 1)
                    dve.wait_ge(self.normed, i + 1)
                    for h in range(DH):
                        last = dve.tensor_scalar(dst[:, h, i * CW:(i + 1) * CW], sq[:, i, h], weight[:, h:h + 1], bias[:, h:h + 1], ALU.mult, ALU.add)
                    last.then_inc(self.done, 1)

            @block.scalar
            def _(act):
                for i in range(NCH):
                    act.wait_ge(self.centred, base + i + 1)
                    act.activation(sq[:, i], xc[:, i], ACT.Square).then_inc(self.squared, 1)
                act.wait_ge(self.var_ready, base + NCH)
                act.activation(rstd[:], var[:, 0:CW], ACT.Sqrt, bias=g.eps[:]).then_inc(self.std_ready, 1)


def mamba(k, g, ins, norm):
    nc = k.nc
    b_dram = k.dram("mamba_b", [2 * NST, HW])
    c_dram = k.dram("mamba_c", [2 * NST, HW])
    small_loaded = k.sem("mamba_small_loaded")
    w_in_loaded = k.sem("mamba_w_in_loaded")
    with ExitStack() as ctx:
        xs = k.sb(ctx, "mamba_xs", [P, DIC, T])
        gate = k.sb(ctx, "mamba_gate", [P, DIC, T])
        small = k.sb(ctx, "mamba_small", [P, DIC, TAPS + 4 + NST])
        conv_w, conv_b = small[:, :, 0:TAPS], small[:, :, TAPS]
        dt_w, dt_b, skip = small[:, :, TAPS + 1], small[:, :, TAPS + 2], small[:, :, TAPS + 3]
        a_neg = small[:, :, TAPS + 4:]
        norm_wb = k.sb(ctx, "mamba_norm_wb", [P, 2, DH])
        xp_w = k.sb(ctx, "mamba_xp_w", [P, DIC, 2 * NST])
        dt_rep = k.sb(ctx, "mamba_dt_rep", [P, DIC, P])

        with ExitStack() as c1:
            xn1 = k.sb(c1, "mamba_xn1", [P, DH, T])
            w_in = k.sb(c1, "mamba_w_in", [P, DH, 2 * DI])
            a_exp, a_sign = k.sem("mamba_a_exp"), k.sem("mamba_a_sign")
            with nc.Block() as block:
                @block.sync
                def _(sp):
                    sp.dma_start(small[:], ins["mamba_small"].rearrange("(c p) n -> p c n", p=P)).then_inc(small_loaded, 16)
                    sp.dma_start(norm_wb[:], ins["mamba_norm"]).then_inc(small_loaded, 16)
                    sp.dma_start(xp_w[:], ins["mamba_xp_w"].rearrange("(c p) n -> p c n", p=P)).then_inc(small_loaded, 16)
                    sp.dma_start(dt_rep[:], ins["mamba_dt_rep"].rearrange("(c p) n -> p c n", p=P)).then_inc(small_loaded, 16)
                    sp.dma_start(w_in[:], ins["mamba_w_in"].rearrange("(h p) n -> p h n", p=P)).then_inc(w_in_loaded, 16)
                    sp.wait_ge(small_loaded, 64)

                @block.scalar
                def _(act):
                    act.wait_ge(small_loaded, 64)
                    act.activation(a_neg, a_neg, ACT.Exp).then_inc(a_exp, 1)

                @block.vector
                def _(dve):
                    dve.wait_ge(a_exp, 1)
                    dve.tensor_scalar(a_neg, a_neg, -1.0, None, ALU.mult).then_inc(a_sign, 1)
                    dve.wait_ge(a_sign, 1)
            norm(g, g.x, xn1)
            norm(g, xn1, g.xn, norm_wb[:, 0], norm_wb[:, 1])

            proj_ready = k.sem("mamba_proj_ready")
            tap_done, conv_done = k.sem("mamba_tap_done"), k.sem("mamba_conv_done")
            silu_done, gate_done = k.sem("mamba_silu_done"), k.sem("mamba_gate_done")
            res_done = k.sem("mamba_res_done")
            with ExitStack() as c2:
                xz = k.ps(c2, "mamba_xz", [P, 2 * DIC, 512])
                pre = k.sb(c2, "mamba_pre", [P, DIC, CW])
                block = c2.enter_context(nc.Block())

                @block.tensor
                def _(pe):
                    pe.wait_ge(w_in_loaded, 16)
                    with loop(pe, NCH) as j:
                        for m in range(2 * DIC):
                            pe.wait_ge(*((conv_done, DIC * j) if m < DIC else (gate_done, DIC * j)))
                            for h in range(DH):
                                mm = pe.matmul(xz[:, m, 0:CW], w_in[:, h, m * P:(m + 1) * P], g.xn[:, h, chunk(j, CW)], start=(h == 0), stop=(h == DH - 1))
                            mm.then_inc(proj_ready, 1)

                @block.vector
                def _(dve):
                    with loop(dve, NCH) as j:
                        dve.wait_ge(silu_done, DIC * j)
                        taps = Steps(dve, tap_done, DIC * (TAPS - 1) * j)
                        for c in range(DIC):
                            dve.wait_ge(proj_ready, 2 * DIC * j + c + 1)
                            taps.did(dve.tensor_scalar(pre[:, c], xz[:, c, 0:CW], conv_w[:, c, TAPS - 1:TAPS], conv_b[:, c:c + 1], ALU.mult, ALU.add))
                            src = xz[:, c, 0:CW].rearrange("p (b l) -> p b l", l=L)
                            dst = pre[:, c].rearrange("p (b l) -> p b l", l=L)
                            for lag in range(1, TAPS):
                                taps.wait()
                                tap = dve.scalar_tensor_tensor(dst[:, :, lag:], src[:, :, :L - lag], conv_w[:, c, TAPS - 1 - lag:TAPS - lag], dst[:, :, lag:], ALU.mult, ALU.add)
                                if lag < TAPS - 1:
                                    taps.did(tap)
                                else:
                                    tap.then_inc(conv_done, 1)

                @block.scalar
                def _(act):
                    with loop(act, NCH) as j:
                        for c in range(DIC):
                            act.wait_ge(proj_ready, 2 * DIC * j + DIC + c + 1)
                            act.activation(gate[:, c, chunk(j, CW)], xz[:, DIC + c, 0:CW], ACT.Silu).then_inc(gate_done, 1)
                        for c in range(DIC):
                            act.wait_ge(conv_done, DIC * j + c + 1)
                            act.activation(xs[:, c, chunk(j, CW)], pre[:, c], ACT.Silu).then_inc(silu_done, 1)

                @block.gpsimd
                def _(pool):
                    for h in range(DH):
                        pool.tensor_tensor(g.x[:, h], g.x[:, h], xn1[:, h], ALU.add).then_inc(res_done, 1)
                    pool.wait_ge(res_done, DH)

        with ExitStack() as c3:
            dt = k.sb(c3, "mamba_dt", [P, DIC, T])
            u = k.sb(c3, "mamba_u", [P, DIC, T])

            raw_ready, bc_ready = k.sem("mamba_raw_ready"), k.sem("mamba_bc_ready")
            raw_used, bc_used = k.sem("mamba_raw_used"), k.sem("mamba_bc_used")
            abs_done, exp_done, ln_done, relu_done = k.sem("mamba_abs_done"), k.sem("mamba_exp_done"), k.sem("mamba_ln_done"), k.sem("mamba_relu_done")
            dt_done, u_done, bc_stored = k.sem("mamba_dt_done"), k.sem("mamba_u_done"), k.sem("mamba_bc_stored")
            with ExitStack() as c2:
                raw = k.ps(c2, "mamba_raw", [P, 512])
                bc = k.ps(c2, "mamba_bc", [2 * NST, 512])
                bc_sb = k.sb(c2, "mamba_bc_sb", [2 * NST, T])
                soft = k.sb(c2, "mamba_soft", [P, DIC, CW])
                relu = k.sb(c2, "mamba_relu", [P, DIC, CW])
                block = c2.enter_context(nc.Block())

                @block.tensor
                def _(pe):
                    with loop(pe, NCH) as j:
                        pe.wait_ge(raw_used, DIC * j)
                        for c in range(DIC):
                            mm = pe.matmul(raw[:, 0:CW], dt_rep[:, c], xs[:, c, chunk(j, CW)], start=(c == 0), stop=(c == DIC - 1))
                        mm.then_inc(raw_ready, 1)
                        pe.wait_ge(bc_used, j)
                        after_wait(pe, g)
                        for c in range(DIC):
                            mm = pe.matmul(bc[:, 0:CW], xp_w[:, c], xs[:, c, chunk(j, CW)], start=(c == 0), stop=(c == DIC - 1))
                        mm.then_inc(bc_ready, 1)

                @block.scalar
                def _(act):
                    with loop(act, NCH) as j:
                        act.wait_ge(raw_ready, j + 1)
                        act.wait_ge(dt_done, DIC * j)
                        for c in range(DIC):
                            act.activation(soft[:, c], raw[:, 0:CW], ACT.Abs, bias=dt_b[:, c:c + 1], scale=dt_w[:, c:c + 1]).then_inc(abs_done, 1)
                            act.activation(relu[:, c], raw[:, 0:CW], ACT.Relu, bias=dt_b[:, c:c + 1], scale=dt_w[:, c:c + 1]).then_inc(raw_used, 1)
                        act.wait_ge(abs_done, DIC * j + DIC)
                        act.activation(soft[:], soft[:], ACT.Exp, scale=-1.0).then_inc(exp_done, 1)
                        act.wait_ge(exp_done, j + 1)
                        act.activation(soft[:], soft[:], ACT.Ln, bias=1.0).then_inc(ln_done, 1)

                @block.vector
                def _(dve):
                    with loop(dve, NCH) as j:
                        dve.wait_ge(bc_ready, j + 1)
                        dve.tensor_copy(bc_sb[:, chunk(j, CW)], bc[:, 0:CW]).then_inc(bc_used, 1)
                        dve.wait_ge(ln_done, j + 1)
                        dve.wait_ge(raw_used, DIC * j + DIC)
                        for c in range(DIC):
                            dve.tensor_tensor(dt[:, c, chunk(j, CW)], soft[:, c], relu[:, c], ALU.add).then_inc(dt_done, 1)
                        for c in range(DIC):
                            dve.wait_ge(dt_done, DIC * j + c + 1)
                            dve.tensor_tensor(u[:, c, chunk(j, CW)], dt[:, c, chunk(j, CW)], xs[:, c, chunk(j, CW)], ALU.mult)

                @block.sync
                def _(sp):
                    sp.wait_ge(bc_used, NCH)
                    for hh in range(2):
                        sp.dma_start(b_dram[hh * NST:(hh + 1) * NST, :], bc_sb[0:NST, hh * HW:(hh + 1) * HW]).then_inc(bc_stored, 16)
                        sp.dma_start(c_dram[hh * NST:(hh + 1) * NST, :], bc_sb[NST:2 * NST, hh * HW:(hh + 1) * HW]).then_inc(bc_stored, 16)
                    sp.wait_ge(bc_stored, 64)

            b_loaded, c_loaded = k.sems("mamba_b_loaded", 2), k.sems("mamba_c_loaded", 2)
            skip_ready = k.sem("mamba_skip_ready")
            decay_ready, input_ready = k.sem("mamba_decay_ready"), k.sem("mamba_input_ready")
            state_ready, out_ready, summed = k.sem("mamba_state_ready"), k.sem("mamba_out_ready"), k.sem("mamba_summed")
            y_ready, y_done = k.sem("mamba_y_ready"), k.sem("mamba_y_done")
            QH = NST * DIC
            with ExitStack() as c2:
                b_all = k.sb(c2, "mamba_b_all", [P, 2, HW])
                c_all = k.sb(c2, "mamba_c_all", [P, 2, HW])
                decay = k.sb(c2, "mamba_decay", [P, 2, HW])
                fed = k.sb(c2, "mamba_fed", [P, 2, HW])
                state = k.sb(c2, "mamba_state", [P, 2, HW])
                read = k.sb(c2, "mamba_read", [P, 2, HW])
                skip_diag = k.sb(c2, "mamba_skip_diag", [P, DIC, P])
                y = k.ps(c2, "mamba_y", [P, DIC, 2, 512])
                block = c2.enter_context(nc.Block())
                by_batch = [decay[:, s].rearrange("p (b l) -> p b l", l=L) for s in range(2)]

                def load(sp, n, s):
                    sp.dma_start(b_all[:, s], b_dram[ds(n, 1), :].partition_broadcast(P)).then_inc(b_loaded[s], 16)
                    sp.dma_start(c_all[:, s], c_dram[ds(n, 1), :].partition_broadcast(P)).then_inc(c_loaded[s], 16)

                @block.sync
                def _(sp):
                    for s in range(2):
                        load(sp, s, s)
                    with loop(sp, 2 * NST - 2, 2) as n:
                        for s in range(2):
                            sp.wait_ge(out_ready, 2 + DIC * (n + s + 1))
                            after_wait(sp, g)
                            load(sp, n + s + 2, s)

                @block.scalar
                def _(act):
                    for hh in range(2):
                        tok = slice(hh * HW, (hh + 1) * HW)
                        with loop(act, NST, 2) as n:
                            for s in range(2):
                                for c in range(DIC):
                                    act.wait_ge(state_ready, hh * QH + DIC * (n + s) + c + 1)
                                    src = dt[:, c, tok].rearrange("p (b l) -> p b l", l=L)
                                    act.activation(by_batch[c % 2][:, :, 1:], src[:, :, 1:], ACT.Exp, scale=a_neg[:, c, ds(n + s, 1)]).then_inc(decay_ready, 1)

                @block.gpsimd
                def _(pool):
                    for hh in range(2):
                        tok = slice(hh * HW, (hh + 1) * HW)
                        with loop(pool, NST, 2) as n:
                            for s in range(2):
                                pool.wait_ge(b_loaded[s], 8 * NST * hh + 8 * n + 16)
                                for c in range(DIC):
                                    pool.wait_ge(state_ready, hh * QH + DIC * (n + s) + c + 1)
                                    pool.tensor_tensor(fed[:, c % 2], u[:, c, tok], b_all[:, s], ALU.mult).then_inc(input_ready, 1)

                @block.vector
                def _(dve):
                    for c in range(DIC):
                        diag = dve.tensor_scalar(skip_diag[:, c], g.ident[:], skip[:, c:c + 1], None, ALU.mult)
                    diag.then_inc(skip_ready, 1)
                    for s in range(2):
                        zeros = dve.memset(by_batch[s][:, :, 0:1], 0.0)
                    zeros.then_inc(state_ready, 2)
                    dve.memset(read[:, :, 0:1], 0.0).then_inc(out_ready, 2)
                    for hh in range(2):
                        tok = slice(hh * HW, (hh + 1) * HW)
                        with loop(dve, NST, 2) as n:
                            q0 = hh * QH + DIC * n

                            def scan(q):
                                dve.wait_ge(decay_ready, q0 + q + 1)
                                dve.wait_ge(input_ready, q0 + q + 1)
                                dve.wait_ge(out_ready, q0 + q + 1)
                                dve.tensor_tensor_scan(state[:, q % 2], decay[:, q % 2], fed[:, q % 2], 0.0, ALU.mult, ALU.add).then_inc(state_ready, 1)

                            def read_out(q):
                                if q % DIC == 0:
                                    dve.wait_ge(c_loaded[q // DIC], 8 * NST * hh + 8 * n + 16)
                                dve.wait_ge(state_ready, q0 + q + 3)
                                dve.wait_ge(summed, q0 + q + 1)
                                dve.tensor_tensor(read[:, q % 2], state[:, q % 2], c_all[:, q // DIC], ALU.mult).then_inc(out_ready, 1)

                            scan(0)
                            for q in range(1, 2 * DIC):
                                scan(q)
                                read_out(q - 1)
                            read_out(2 * DIC - 1)
                        dve.wait_ge(y_ready, hh + 1)
                        for c in range(DIC):
                            for w in range(2):
                                part = slice(hh * HW + w * CW, hh * HW + (w + 1) * CW)
                                dve.tensor_tensor(xs[:, c, part], y[:, c, w, 0:CW], gate[:, c, part], ALU.mult).then_inc(y_done, 1)

                @block.tensor
                def _(pe):
                    pe.wait_ge(skip_ready, 1)
                    for hh in range(2):
                        if hh:
                            pe.wait_ge(y_done, 2 * DIC * hh)
                        for c in range(DIC):
                            for w in range(2):
                                part = slice(hh * HW + w * CW, hh * HW + (w + 1) * CW)
                                mm = pe.matmul(y[:, c, w, 0:CW], skip_diag[:, c], xs[:, c, part], start=True, stop=False, skip_group_check=True)
                        if hh == 0:
                            mm.then_inc(summed, 2)
                        with loop(pe, NST, 2) as n:
                            for q in range(2 * DIC):
                                pe.wait_ge(out_ready, hh * QH + DIC * n + q + 3)
                                for w in range(2):
                                    mm = pe.matmul(y[:, q % DIC, w, 0:CW], g.ident[:], read[:, q % 2, w * CW:(w + 1) * CW], start=False, stop=False, skip_group_check=True)
                                mm.then_inc(summed, 1)
                        pe.matmul(y[0:1, 0, 0, 510:511], g.ident[:, 0:1], g.ident[:, 0:1], start=True, stop=True, skip_group_check=True).then_inc(y_ready, 1)

        add_projection(k, g, "mamba_wout", ins["mamba_w_out"], xs, DIC)


def add_projection(k, g, name, w_dram, src, kc, bias=None):
    nc = k.nc
    loaded, ready, added = k.sem(f"{name}_loaded"), k.sem(f"{name}_ready"), k.sem(f"{name}_added")
    with ExitStack() as ctx:
        w = k.sb(ctx, f"{name}_w", [P, kc, D])
        acc = k.ps(ctx, f"{name}_acc", [P, 2, DH, 512])
        block = ctx.enter_context(nc.Block())

        @block.sync
        def _(sp):
            sp.dma_start(w[:], w_dram.rearrange("(c p) n -> p c n", p=P)).then_inc(loaded, 16)

        @block.tensor
        def _(pe):
            pe.wait_ge(loaded, 16)
            with loop(pe, NCH, 2) as j:
                pe.wait_ge(added, DH * j)
                for s in range(2):
                    for m in range(DH):
                        for c in range(kc):
                            mm = pe.matmul(acc[:, s, m, 0:CW], w[:, c, m * P:(m + 1) * P], src[:, c, chunk(j + s, CW)], start=(c == 0), stop=(c == kc - 1))
                        mm.then_inc(ready, 1)

        @block.vector
        def _(dve):
            with loop(dve, NCH, 2) as j:
                for s in range(2):
                    for m in range(DH):
                        dve.wait_ge(ready, DH * (j + s) + m + 1)
                        x = g.x[:, m, chunk(j + s, CW)]
                        if bias is None:
                            dve.tensor_tensor(x, acc[:, s, m, 0:CW], x, ALU.add).then_inc(added, 1)
                        else:
                            dve.scalar_tensor_tensor(x, acc[:, s, m, 0:CW], bias[:, m:m + 1], x, ALU.add, ALU.add).then_inc(added, 1)


def cross_attention(k, g, ins, norm):
    nc = k.nc
    norm(g, g.x, g.xn)
    with ExitStack() as ctx:
        q = k.sb(ctx, "xattn_q", [P, DH, T])
        merged = k.sb(ctx, "xattn_merged", [P, DH, T])
        bias = k.sb(ctx, "xattn_bias", [P, 2 * DH + 2 * DH + DH + DH])
        bq, bk, bv, bo = bias[:, 0:4], bias[:, 4:8], bias[:, 8:10], bias[:, 10:12]
        rope = k.sb(ctx, "xattn_rope", [P, 2 * (L + S2)])
        q_cos, q_sin = rope[:, 0:L], rope[:, L:2 * L]
        k_cos, k_sin = rope[:, 2 * L:2 * L + S2], rope[:, 2 * L + S2:]
        w_kv = k.sb(ctx, "xattn_w_kv", [P, DH, 3 * D])
        own_head = k.sb(ctx, "xattn_own_head", [P, HPT])
        keep = k.sb(ctx, "xattn_keep", [L, B * S2], U8)
        small_loaded, kv_loaded = k.sem("xattn_small_loaded"), k.sem("xattn_kv_loaded")

        q_ready, q_cosed, q_sined, q_done = k.sem("xattn_q_ready"), k.sem("xattn_q_cosed"), k.sem("xattn_q_sined"), k.sem("xattn_q_done")
        with ExitStack() as c2:
            w_q = k.sb(c2, "xattn_w_q", [P, DH, 2 * D])
            tmp = k.sb(c2, "xattn_q_tmp", [P, 2, DH, CW])
            qp = k.ps(c2, "xattn_qp", [P, 2, DH, 512])
            block = c2.enter_context(nc.Block())

            @block.sync
            def _(sp):
                sp.dma_start(w_q[:], ins["xattn_w_q"].rearrange("(h p) n -> p h n", p=P)).then_inc(small_loaded, 16)
                sp.dma_start(bias[:], ins["xattn_bias"]).then_inc(small_loaded, 16)
                sp.dma_start(rope[:], ins["xattn_rope"]).then_inc(small_loaded, 16)
                sp.dma_start(own_head[:], ins["xattn_own_head"]).then_inc(small_loaded, 16)
                sp.dma_start(w_kv[:], ins["xattn_w_kv"].rearrange("(h p) n -> p h n", p=P)).then_inc(kv_loaded, 16)
                sp.dma_start(keep[:], ins["xattn_keep"].partition_broadcast(L)).then_inc(kv_loaded, 16)
                sp.wait_ge(kv_loaded, 32)

            @block.tensor
            def _(pe):
                pe.wait_ge(small_loaded, 64)
                with loop(pe, NCH) as j:
                    pe.wait_ge(q_sined, DH * j)
                    for m in range(DH):
                        for swap in range(2):
                            at = (swap * DH + m) * P
                            for h in range(DH):
                                mm = pe.matmul(qp[:, swap, m, 0:CW], w_q[:, h, at:at + P], g.xn[:, h, chunk(j, CW)], start=(h == 0), stop=(h == DH - 1))
                        mm.then_inc(q_ready, 1)

            @block.vector
            def _(dve):
                dve.wait_ge(small_loaded, 64)

                def turned(out, m, swap, table):
                    src = qp[:, swap, m, 0:CW].rearrange("p (b l) -> p b l", l=L)
                    table = table.unsqueeze(1).to_broadcast([P, BPC, L])
                    return dve.scalar_tensor_tensor(out.rearrange("p (b l) -> p b l", l=L), src, bq[:, swap * DH + m:swap * DH + m + 1], table, ALU.add, ALU.mult)

                with loop(dve, NCH) as j:
                    dve.wait_ge(q_done, DH * j)
                    for m in range(DH):
                        dve.wait_ge(q_ready, DH * j + m + 1)
                        turned(tmp[:, 0, m], m, 0, q_cos).then_inc(q_cosed, 1)
                        turned(tmp[:, 1, m], m, 1, q_sin).then_inc(q_sined, 1)

            @block.gpsimd
            def _(pool):
                with loop(pool, NCH) as j:
                    for m in range(DH):
                        pool.wait_ge(q_cosed, DH * j + m + 1)
                        pool.wait_ge(q_sined, DH * j + m + 1)
                        pool.tensor_tensor(q[:, m, chunk(j, CW)], tmp[:, 0, m], tmp[:, 1, m], ALU.add).then_inc(q_done, 1)

        ctx_loaded = k.sems("xattn_ctx_loaded", 2)
        kproj_ready, k_read, k_summed = k.sem("xattn_kproj_ready"), k.sem("xattn_k_read"), k.sem("xattn_k_summed")
        k_cosed, v_ready, v_read = k.sem("xattn_k_cosed"), k.sem("xattn_v_ready"), k.sem("xattn_v_read")
        blocked, mask_ready = k.sem("xattn_blocked"), k.sem("xattn_mask_ready")
        s_ready, biased, p_ready, t_ready = k.sem("xattn_s_ready"), k.sem("xattn_biased"), k.sem("xattn_p_ready"), k.sem("xattn_t_ready")
        pt_ready, pv_done = k.sems("xattn_pt_ready", 2), k.sem("xattn_pv_done")
        inverted, o_normed, o_turned, o_stored = k.sem("xattn_inverted"), k.sem("xattn_o_normed"), k.sem("xattn_o_turned"), k.sem("xattn_o_stored")
        CK = S2 // KC
        RING = 4
        with ExitStack() as c2:
            context = k.sb(c2, "xattn_context", [P, 2, DH, S2])
            kT = k.sb(c2, "xattn_kT", [P, 2, DH, S2])
            turn = k.sb(c2, "xattn_turn", [P, 2, DH, S2])
            v = k.sb(c2, "xattn_v", [KC, 2, CK, D])
            qb = k.sb(c2, "xattn_qb", [P, 2, DH, HPT, L])
            mask = k.sb(c2, "xattn_mask", [L, 2, S2])
            sm = k.sb(c2, "xattn_sm", [L, RING, S2])
            least = k.sb(c2, "xattn_least", [L, 2, NHEAD])
            prob = k.sb(c2, "xattn_prob", [L, RING, S2])
            total = k.sb(c2, "xattn_total", [L, 2, NHEAD])
            pt = k.sb(c2, "xattn_pt", [KC, RING, CK, L])
            o_sb = k.sb(c2, "xattn_o_sb", [L, 2, D])
            kv_ps = k.ps(c2, "xattn_kv_ps", [P, 2, 512])
            s_ps = k.ps(c2, "xattn_s_ps", [P, 2, 512])
            pt_ps = k.ps(c2, "xattn_pt_ps", [P, 2, 512])
            o_ps = k.ps(c2, "xattn_o_ps", [P, 2, 512])
            block = c2.enter_context(nc.Block())

            def turned_probs(n):
                return pt_ps[0:KC, n % 2, 0:CK * L].rearrange("p (c l) -> p c l", l=L)

            def sums_turned(s):
                return o_ps[:, s, D:D + DH * L].rearrange("p (h l) -> p h l", h=DH)

            def batches(eng, batch):
                batch(0, 0)
                with loop(eng, B - 2, 2) as b:
                    for s in range(2):
                        batch(b + (1 + s), 1 - s)
                batch(B - 1, 1)

            def follows(b):
                return not isinstance(b, int) or b < B - 1

            def precedes(b):
                return not isinstance(b, int) or b > 0

            def ahead(b, s, h, step):
                if h < NHEAD:
                    step(b, s, h)
                elif follows(b):
                    step(b + 1, 1 - s, h - NHEAD)

            @block.sync
            def _(sp):
                def load(b, s):
                    sp.dma_start(context[:, s], ins["ctxT"][ds(b, 1)].rearrange("b (h p) t -> p (b h) t", p=P)).then_inc(ctx_loaded[s], 16)

                for s in range(2):
                    load(s, s)
                with loop(sp, B - 2, 2) as b:
                    for s in range(2):
                        sp.wait_ge(v_ready, b + s + 1)
                        load(b + s + 2, s)

            @block.gpsimd
            def _(pool):
                def spread(b, s):
                    for m in range(DH):
                        src = q[:, m, chunk(b, L)].unsqueeze(1).to_broadcast([P, HPT, L])
                        own = own_head[:].unsqueeze(2).to_broadcast([P, HPT, L])
                        pool.tensor_tensor(qb[:, s, m], src, own, ALU.mult).then_inc(blocked, 1)

                for s in range(2):
                    spread(s, s)
                with loop(pool, B - 2, 2) as b:
                    for s in range(2):
                        pool.wait_ge(s_ready, NHEAD * (b + s + 1))
                        spread(b + s + 2, s)

            @block.tensor
            def _(pe):
                def k_half(b, s, m):
                    if m == 0:
                        pe.wait_ge(ctx_loaded[s], 8 * (b - s) + 16)
                        wait(pe, v_read, b)
                    else:
                        pe.wait_ge(k_read, DH * b + 1)
                    for swap in range(2):
                        at = (swap * DH + m) * P
                        for h in range(DH):
                            mm = pe.matmul(kv_ps[:, swap, 0:S2], w_kv[:, h, at:at + P], context[:, s, h], start=(h == 0), stop=(h == DH - 1))
                    mm.then_inc(kproj_ready, 1)

                def values(b, s):
                    pe.wait_ge(k_read, DH * b + 2)
                    for c in range(CK):
                        for h in range(DH):
                            mm = pe.matmul(kv_ps[0:KC, c // 2, (c % 2) * D:(c % 2 + 1) * D], context[:, s, h, c * KC:(c + 1) * KC], w_kv[:, h, 2 * D:], start=(h == 0), stop=(h == DH - 1))
                    mm.then_inc(v_ready, 1)

                def scores(b, s, h):
                    if h % HPT == 0:
                        pe.wait_ge(blocked, DH * b + h // HPT + 1)
                        pe.wait_ge(k_summed, DH * b + h // HPT + 1)
                    wait(pe, biased, NHEAD * b + h - 1)
                    pe.matmul(s_ps[0:L, h % 2, 0:S2], qb[:, s, h // HPT, h % HPT], kT[:, s, h // HPT], start=True, stop=True).then_inc(s_ready, 1)

                def turn_probs(b, s, h):
                    pe.wait_ge(p_ready, NHEAD * b + h + 1)
                    wait(pe, pt_ready[h % 2], NHEAD // 2 * b + h // 2)
                    for c in range(CK):
                        mm = pe.transpose(turned_probs(h)[:, c], prob[:, h % RING, c * KC:(c + 1) * KC], g.ident[0:L, 0:L])
                    mm.then_inc(t_ready, 1)

                def weigh(b, s, h):
                    if h == 0:
                        pe.wait_ge(v_read, b + 1)
                    pe.wait_ge(pt_ready[h % 2], NHEAD // 2 * b + h // 2 + 1)
                    for c in range(CK):
                        mm = pe.matmul(o_ps[0:L, s, h * HD:(h + 1) * HD], pt[:, h % RING, c], v[:, s, c, h * HD:(h + 1) * HD], start=(c == 0), stop=(c == CK - 1))
                    mm.then_inc(pv_done, 1)

                def turn_sums(b, s):
                    pe.wait_ge(o_normed, b + 1)
                    for m in range(DH):
                        mm = pe.transpose(sums_turned(s)[:, m], o_sb[:, s, m * P:(m + 1) * P], g.ident[0:L, 0:L])
                    mm.then_inc(o_turned, 1)

                def batch(b, s):
                    for h in range(NHEAD):
                        ahead(b, s, h + 4, scores)
                        ahead(b, s, h + 2, turn_probs)
                        weigh(b, s, h)
                        if follows(b) and h in (2, 5):
                            k_half(b + 1, 1 - s, (h - 2) // 3)
                        if follows(b) and h == 8:
                            values(b + 1, 1 - s)
                        if h == 4 and precedes(b):
                            turn_sums(b - 1, 1 - s)

                pe.wait_ge(kv_loaded, 32)
                k_half(0, 0, 0)
                k_half(0, 0, 1)
                values(0, 0)
                for h in range(4):
                    scores(0, 0, h)
                for h in range(2):
                    turn_probs(0, 0, h)
                batches(pe, batch)
                turn_sums(B - 1, 1)

            @block.vector
            def _(dve):
                def keys(b, s, m):
                    dve.wait_ge(kproj_ready, DH * b + m + 1)
                    dve.scalar_tensor_tensor(turn[:, 0, m], kv_ps[:, 0, 0:S2], bk[:, m:m + 1], k_cos, ALU.add, ALU.mult).then_inc(k_cosed, 1)
                    dve.scalar_tensor_tensor(turn[:, 1, m], kv_ps[:, 1, 0:S2], bk[:, DH + m:DH + m + 1], k_sin, ALU.add, ALU.mult).then_inc(k_read, 1)
                    dve.wait_ge(k_cosed, DH * b + m + 1)
                    dve.wait_ge(k_read, DH * b + m + 1)
                    dve.tensor_tensor(kT[:, s, m], turn[:, 0, m], turn[:, 1, m], ALU.add).then_inc(k_summed, 1)

                def bias_scores(b, s, h):
                    if h == 0:
                        dve.tensor_scalar(mask[:, s], keep[:, chunk(b, S2)], -1.0, BIG, ALU.add, ALU.mult).then_inc(mask_ready, 1)
                        dve.wait_ge(mask_ready, b + 1)
                    wait(dve, p_ready, NHEAD * b + h + 1 - RING)
                    dve.wait_ge(s_ready, NHEAD * b + h + 1)
                    after_wait(dve, g)
                    dve.tensor_tensor_reduce(sm[:, h % RING], s_ps[0:L, h % 2, 0:S2], mask[:, s], -SCALE, BIG, ALU.add, ALU.min, least[:, s, h:h + 1]).then_inc(biased, 1)

                def copy_probs(b, s, h):
                    wait(dve, pv_done, NHEAD * b + h + 1 - RING)
                    dve.wait_ge(t_ready, NHEAD * b + h + 1)
                    dve.tensor_copy(pt[:, h % RING], turned_probs(h)).then_inc(pt_ready[0], 1)

                def norm_sums(b, s):
                    dve.wait_ge(p_ready, NHEAD * (b + 1))
                    dve.reciprocal(total[:, s], total[:, s]).then_inc(inverted, 1)
                    dve.wait_ge(inverted, b + 1)
                    dve.wait_ge(pv_done, NHEAD * (b + 1))
                    dve.tensor_tensor(o_sb[:, s].rearrange("p (n d) -> p n d", d=HD), o_ps[0:L, s, 0:D].rearrange("p (n d) -> p n d", d=HD),
                                      total[:, s].unsqueeze(2).to_broadcast([L, NHEAD, HD]), ALU.mult).then_inc(o_normed, 1)

                def batch(b, s):
                    for h in range(NHEAD):
                        ahead(b, s, h + 3, bias_scores)
                        if h % 2 == 1:
                            ahead(b, s, h + 1, copy_probs)
                        if h == 1 and precedes(b):
                            norm_sums(b - 1, 1 - s)
                        if follows(b) and h in (4, 7):
                            keys(b + 1, 1 - s, (h - 4) // 3)

                for m in range(DH):
                    keys(0, 0, m)
                for h in range(3):
                    bias_scores(0, 0, h)
                copy_probs(0, 0, 0)
                batches(dve, batch)
                norm_sums(B - 1, 1)

            @block.scalar
            def _(act):
                def copy_values(b, s):
                    wait(act, pv_done, NHEAD * (b - 1))
                    act.wait_ge(v_ready, b + 1)
                    for c in range(CK):
                        last = act.activation(v[:, s, c], kv_ps[0:KC, c // 2, (c % 2) * D:(c % 2 + 1) * D], ACT.Copy)
                    last.then_inc(v_read, 1)

                def exponentiate(b, s, h):
                    if h == 0:
                        wait(act, o_normed, b - 1)
                    wait(act, t_ready, NHEAD * b + h + 1 - RING)
                    act.wait_ge(biased, NHEAD * b + h + 1)
                    act.activation(prob[:, h % RING], sm[:, h % RING], ACT.Exp, bias=least[:, s, h:h + 1], scale=-1.0, accum_out=total[:, s, h:h + 1]).then_inc(p_ready, 1)

                def copy_probs(b, s, h):
                    wait(act, pv_done, NHEAD * b + h + 1 - RING)
                    act.wait_ge(t_ready, NHEAD * b + h + 1)
                    act.activation(pt[:, h % RING], turned_probs(h), ACT.Copy).then_inc(pt_ready[1], 1)

                def store_sums(b, s):
                    act.wait_ge(o_turned, b + 1)
                    for m in range(DH):
                        last = act.activation(merged[:, m, chunk(b, L)], sums_turned(s)[:, m], ACT.Identity, bias=bv[:, m:m + 1])
                    last.then_inc(o_stored, 1)

                def batch(b, s):
                    for h in range(NHEAD):
                        ahead(b, s, h + 3, exponentiate)
                        if h % 2 == 0:
                            ahead(b, s, h + 1, copy_probs)
                        if h == 5 and precedes(b):
                            store_sums(b - 1, 1 - s)
                        if follows(b) and h == 10:
                            copy_values(b + 1, 1 - s)

                copy_values(0, 0)
                for h in range(3):
                    exponentiate(0, 0, h)
                batches(act, batch)
                store_sums(B - 1, 1)

        add_projection(k, g, "xattn_wo", ins["xattn_w_o"], merged, DH, bo)


def min_gru(k, g, ins, norm):
    nc = k.nc
    norm(g, g.x, g.xn)
    loaded = k.sem("gru_loaded")
    hidden_ready, gate_ready, z_done, forget_done = k.sem("gru_hidden_ready"), k.sem("gru_gate_ready"), k.sem("gru_z_done"), k.sem("gru_forget_done")
    raised, fed_done, scanned, cleared = k.sem("gru_raised"), k.sem("gru_fed_done"), k.sem("gru_scanned"), k.sem("gru_cleared")
    out_ready, added = k.sem("gru_out_ready"), k.sem("gru_added")
    with ExitStack() as ctx:
        w = k.sb(ctx, "gru_w", [P, DH, 2 * DI])
        w_out = k.sb(ctx, "gru_w_out", [P, DIC, D])
        z = k.sb(ctx, "gru_z", [P, DIC, CW])
        forget = k.sb(ctx, "gru_forget", [P, DIC, CW])
        fed = k.sb(ctx, "gru_fed", [P, DIC, CW])
        state = k.sb(ctx, "gru_state", [P, DIC, CW])
        hid = k.ps(ctx, "gru_hid", [P, 2, 512])
        gat = k.ps(ctx, "gru_gat", [P, 2, 512])
        acc = k.ps(ctx, "gru_acc", [P, DH, 512])
        block = ctx.enter_context(nc.Block())

        @block.sync
        def _(sp):
            sp.dma_start(w[:], ins["gru_w"].rearrange("(h p) n -> p h n", p=P)).then_inc(loaded, 16)
            sp.dma_start(w_out[:], ins["gru_w_out"].rearrange("(c p) n -> p c n", p=P)).then_inc(loaded, 16)

        @block.tensor
        def _(pe):
            pe.wait_ge(loaded, 32)
            with loop(pe, NCH) as j:
                for c in range(DIC):
                    pe.wait_ge(raised, DIC * j + c - 1) if c >= 2 else pe.wait_ge(raised, DIC * j)
                    for h in range(DH):
                        mm = pe.matmul(hid[:, c % 2, 0:CW], w[:, h, c * P:(c + 1) * P], g.xn[:, h, chunk(j, CW)], start=(h == 0), stop=(h == DH - 1))
                    mm.then_inc(hidden_ready, 1)
                    pe.wait_ge(forget_done, DIC * j + c - 1) if c >= 2 else pe.wait_ge(forget_done, DIC * j)
                    for h in range(DH):
                        mm = pe.matmul(gat[:, c % 2, 0:CW], w[:, h, DI + c * P:DI + (c + 1) * P], g.xn[:, h, chunk(j, CW)], start=(h == 0), stop=(h == DH - 1))
                    mm.then_inc(gate_ready, 1)
                pe.wait_ge(added, DH * j)
                pe.wait_ge(scanned, DIC * (j + 1))
                for m in range(DH):
                    for c in range(DIC):
                        mm = pe.matmul(acc[:, m, 0:CW], w_out[:, c, m * P:(m + 1) * P], state[:, c], start=(c == 0), stop=(c == DIC - 1))
                    mm.then_inc(out_ready, 1)

        @block.scalar
        def _(act):
            act.wait_ge(cleared, 1)
            with loop(act, NCH) as j:
                for c in range(DIC):
                    act.wait_ge(gate_ready, DIC * j + c + 1)
                    act.wait_ge(scanned, DIC * j)
                    act.activation(z[:, c], gat[:, c % 2, 0:CW], ACT.Sigmoid).then_inc(z_done, 1)
                    src = gat[:, c % 2, 0:CW].rearrange("p (b l) -> p b l", l=L)
                    dst = forget[:, c].rearrange("p (b l) -> p b l", l=L)
                    act.activation(dst[:, :, 1:], src[:, :, 1:], ACT.Sigmoid, scale=-1.0).then_inc(forget_done, 1)

        @block.vector
        def _(dve):
            dve.memset(forget[:].rearrange("p c (b l) -> p (c b) l", l=L)[:, :, 0:1], 0.0).then_inc(cleared, 1)
            with loop(dve, NCH) as j:
                dve.wait_ge(out_ready, DH * j)
                for c in range(DIC):
                    n = DIC * j + c + 1
                    dve.wait_ge(hidden_ready, n)
                    dve.tensor_scalar(fed[:, c], hid[:, c % 2, 0:CW], 0.0, 0.5, ALU.max, ALU.add).then_inc(raised, 1)
                    dve.wait_ge(raised, n)
                    dve.wait_ge(z_done, n)
                    dve.tensor_tensor(fed[:, c], fed[:, c], z[:, c], ALU.mult).then_inc(fed_done, 1)
                    dve.wait_ge(fed_done, n)
                    dve.wait_ge(forget_done, n)
                    dve.tensor_tensor_scan(state[:, c], forget[:, c], fed[:, c], 0.0, ALU.mult, ALU.add).then_inc(scanned, 1)
                for m in range(DH):
                    dve.wait_ge(out_ready, DH * j + m + 1)
                    x = g.x[:, m, chunk(j, CW)]
                    dve.tensor_tensor(x, acc[:, m, 0:CW], x, ALU.add).then_inc(added, 1)


def delay_attention(k, g, ins, norm):
    nc = k.nc
    norm(g, g.x, g.xn)
    twice = k.dram("delay_weights", [B, 2 * L])
    w_loaded = k.sem("delay_w_loaded")
    with ExitStack() as ctx:
        values = k.sb(ctx, "delay_values", [L, B, D])
        spectrum = k.sb(ctx, "delay_spectrum", [L, B])
        circ = k.sb(ctx, "delay_circ", [L, B, L])
        merged = k.sb(ctx, "delay_merged", [P, DH, T])
        bias = k.sb(ctx, "delay_bias", [P, 2 * DH])
        dft = k.sb(ctx, "delay_dft", [L, L])
        idft = k.sb(ctx, "delay_idft", [L, L])

        ctx_loaded = k.sems("delay_ctx_loaded", 2)
        staged, proj_ready, v_ready, qk_copied, v_copied = k.sem("delay_staged"), k.sem("delay_proj_ready"), k.sem("delay_v_ready"), k.sem("delay_qk_copied"), k.sem("delay_v_copied")
        dft_ready, kf_copied, crossed, summed = k.sem("delay_dft_ready"), k.sem("delay_kf_copied"), k.sem("delay_crossed"), k.sem("delay_summed")
        with ExitStack() as c2:
            w = k.sb(c2, "delay_w", [P, DH, 3 * D])
            b_qk = k.sb(c2, "delay_b_qk", [1, 2 * D])
            xq = k.sb(c2, "delay_xq", [P, 2, DH, L])
            xk = k.sb(c2, "delay_xk", [P, 2, DH, L])
            qk = k.sb(c2, "delay_qk", [L, 2, 2 * D])
            kf = k.sb(c2, "delay_kf", [L, 2, D])
            cross = k.sb(c2, "delay_cross", [L, 2, D])
            qk_ps = k.ps(c2, "delay_qk_ps", [P, 2, 512])
            v_ps = k.ps(c2, "delay_v_ps", [P, 2, 512])
            f_ps = k.ps(c2, "delay_f_ps", [P, 2, 512])
            block = c2.enter_context(nc.Block())

            @block.sync
            def _(sp):
                def load(b, s):
                    sp.dma_start(xk[:, s], ins["ctxT"][ds(b, 1), :, 0:L].rearrange("b (h p) t -> p (b h) t", p=P)).then_inc(ctx_loaded[s], 16)

                sp.dma_start(w[:], ins["delay_w"].rearrange("(h p) n -> p h n", p=P)).then_inc(w_loaded, 16)
                sp.dma_start(b_qk[:], ins["delay_b_qk"]).then_inc(w_loaded, 16)
                sp.dma_start(dft[:], ins["delay_dft"]).then_inc(w_loaded, 16)
                sp.dma_start(idft[:], ins["delay_idft"]).then_inc(w_loaded, 16)
                sp.dma_start(bias[:], ins["delay_bias"]).then_inc(w_loaded, 16)
                for s in range(2):
                    load(s, s)
                with loop(sp, B - 2, 2) as b:
                    for s in range(2):
                        sp.wait_ge(v_ready, b + s + 1)
                        load(b + s + 2, s)
                sp.wait_ge(w_loaded, 80)

            @block.gpsimd
            def _(pool):
                def stage(b, s):
                    pool.tensor_copy(xq[:, s], g.xn[:, :, chunk(b, L)]).then_inc(staged, 1)

                for s in range(2):
                    stage(s, s)
                with loop(pool, B - 2, 2) as b:
                    for s in range(2):
                        pool.wait_ge(proj_ready, b + s + 1)
                        stage(b + s + 2, s)

            @block.tensor
            def _(pe):
                pe.wait_ge(w_loaded, 80)

                def project(b, s):
                    pe.wait_ge(qk_copied, b)
                    pe.wait_ge(staged, b + 1 + s)
                    pe.wait_ge(ctx_loaded[s], 8 * b + 16)
                    pe.matmul(qk_ps[0:L, s], g.ones[0:1, 0:L], b_qk[:], start=True, stop=False, skip_group_check=True)
                    for n, src in enumerate((xq, xk)):
                        for h in range(DH):
                            mm = pe.matmul(qk_ps[0:L, s, n * D:(n + 1) * D], src[:, s, h], w[:, h, n * D:(n + 1) * D], start=False, stop=(h == DH - 1), skip_group_check=True)
                    mm.then_inc(proj_ready, 1)
                    pe.wait_ge(v_copied, b)
                    for h in range(DH):
                        mm = pe.matmul(v_ps[0:L, s, 0:D], xk[:, s, h], w[:, h, 2 * D:], start=(h == 0), stop=(h == DH - 1))
                    mm.then_inc(v_ready, 1)

                def transform(b, s):
                    pe.wait_ge(qk_copied, b + s + 1)
                    pe.wait_ge(crossed, b)
                    pe.matmul(f_ps[0:L, s], dft[:], qk[:, s], start=True, stop=True).then_inc(dft_ready, 1)

                with loop(pe, B, 2) as b:
                    for s in range(2):
                        project(b, s)
                    for s in range(2):
                        transform(b, s)

            @block.scalar
            def _(act):
                with loop(act, B, 2) as b:
                    act.wait_ge(dft_ready, b)
                    for s in range(2):
                        act.wait_ge(proj_ready, b + s + 1)
                        act.activation(qk[:, s], qk_ps[0:L, s], ACT.Copy).then_inc(qk_copied, 1)
                    act.wait_ge(crossed, b)
                    for s in range(2):
                        act.wait_ge(dft_ready, b + s + 1)
                        act.activation(kf[:, s], f_ps[0:L, s, D:], ACT.Copy).then_inc(kf_copied, 1)

            @block.vector
            def _(dve):
                with loop(dve, B, 2) as b:
                    for s in range(2):
                        dve.wait_ge(v_ready, b + s + 1)
                        dve.tensor_copy(values[:, ds(b + s, 1)].rearrange("p b d -> p (b d)"), v_ps[0:L, s, 0:D]).then_inc(v_copied, 1)
                    dve.wait_ge(summed, b)
                    for s in range(2):
                        dve.wait_ge(kf_copied, b + s + 1)
                        dve.tensor_tensor(cross[:, s], f_ps[0:L, s, 0:D], kf[:, s], ALU.mult).then_inc(crossed, 1)
                    for s in range(2):
                        dve.wait_ge(crossed, b + s + 1)
                        dve.tensor_reduce(spectrum[:, ds(b + s, 1)], cross[:, s], AX, ALU.add).then_inc(summed, 1)
                dve.wait_ge(summed, B)

        corr_ready, picked = k.sem("delay_corr_ready"), k.sem("delay_picked")
        weights_ready, exp_ready, stored, circ_loaded = k.sem("delay_weights_ready"), k.sem("delay_exp_ready"), k.sem("delay_stored"), k.sem("delay_circ_loaded")
        with ExitStack() as c2:
            corr = k.sb(c2, "delay_corr", [B, L])
            rest = k.sb(c2, "delay_rest", [B, L])
            rest2 = k.sb(c2, "delay_rest2", [B, L])
            top = k.sb(c2, "delay_top", [B, 8])
            ninth = k.sb(c2, "delay_ninth", [B, 8])
            shift = k.sb(c2, "delay_shift", [B, 1])
            chosen = k.sb(c2, "delay_chosen", [B, L])
            power = k.sb(c2, "delay_power", [B, L])
            share = k.sb(c2, "delay_share", [B, 1])
            weight2 = k.sb(c2, "delay_weight2", [B, 2, L])
            corr_ps = k.ps(c2, "delay_corr_ps", [P, 512])
            block = c2.enter_context(nc.Block())

            @block.tensor
            def _(pe):
                pe.matmul(corr_ps[0:B, 0:L], spectrum[:], idft[:], start=True, stop=True).then_inc(corr_ready, 1)

            @block.vector
            def _(dve):
                pick = Steps(dve, picked)

                def then(ins):
                    pick.did(ins)
                    pick.wait()

                dve.wait_ge(corr_ready, 1)
                then(dve.tensor_copy(corr[:], corr_ps[0:B, 0:L]))
                then(dve.max(top[:], corr[:]))
                then(dve.match_replace(rest[:], top[:], corr[:], -BIG))
                then(dve.max(ninth[:], rest[:]))
                then(dve.memset(ninth[:, 1:], -BIG))
                then(dve.match_replace(rest2[:], ninth[:], rest[:], -BIG))
                then(dve.tensor_scalar(chosen[:], rest2[:], -BIG, None, ALU.is_equal))
                then(dve.tensor_scalar(shift[:], top[:, 0:1], -1.0, None, ALU.mult))
                dve.wait_ge(exp_ready, 1)
                then(dve.tensor_tensor(chosen[:], chosen[:], power[:], ALU.mult))
                then(dve.tensor_reduce(share[:], chosen[:], AX, ALU.add))
                then(dve.reciprocal(share[:], share[:]))
                for n in range(2):
                    dve.tensor_scalar(weight2[:, n], chosen[:], share[:, 0:1], None, ALU.mult).then_inc(weights_ready, 1)

            @block.scalar
            def _(act):
                act.wait_ge(picked, 8)
                act.activation(power[:], corr[:], ACT.Exp, bias=shift[:]).then_inc(exp_ready, 1)

            @block.sync
            def _(sp):
                sp.wait_ge(weights_ready, 2)
                sp.dma_start(twice, weight2[:].rearrange("b n l -> b (n l)")).then_inc(stored, 16)
                sp.wait_ge(stored, 16)
                for b in range(B):
                    window = bass.AP(twice.tensor, b * 2 * L + 1, [[1, L], [1, L]])
                    sp.dma_start(circ[:, b], window).then_inc(circ_loaded, 16)
                sp.wait_ge(circ_loaded, 16 * B)

        shifted, kept = k.sem("delay_shifted"), k.sem("delay_kept")
        with ExitStack() as c2:
            agg = k.ps(c2, "delay_agg", [P, 2, DH, 512])
            block = c2.enter_context(nc.Block())

            @block.tensor
            def _(pe):
                for b in range(B):
                    if b >= 2:
                        pe.wait_ge(kept, b - 1)
                    for m in range(DH):
                        mm = pe.matmul(agg[:, b % 2, m, 0:L], values[:, b, m * P:(m + 1) * P], circ[:, b], start=True, stop=True)
                    mm.then_inc(shifted, 1)

            @block.vector
            def _(dve):
                for b in range(B):
                    dve.wait_ge(shifted, b + 1)
                    for m in range(DH):
                        last = dve.tensor_scalar(merged[:, m, b * L:(b + 1) * L], agg[:, b % 2, m, 0:L][:, ::-1], bias[:, m:m + 1], None, ALU.add)
                    last.then_inc(kept, 1)

        add_projection(k, g, "delay_wo", ins["delay_w_o"], merged, DH, bias[:, DH:])


def token_tiles(k, g, name, tok):
    nc = k.nc
    staged, turned, copied = k.sem(f"{name}_staged"), k.sem(f"{name}_turned"), k.sem(f"{name}_copied")
    with ExitStack() as ctx:
        stage = k.sb(ctx, f"{name}_stage", [P, 2, DH, P])
        ps = k.ps(ctx, f"{name}_ps", [P, 2, 512])
        block = ctx.enter_context(nc.Block())

        @block.gpsimd
        def _(pool):
            with loop(pool, TT, 2) as t:
                pool.wait_ge(turned, t)
                for s in range(2):
                    pool.tensor_copy(stage[:, s], g.xn[:, :, chunk(t + s, P)]).then_inc(staged, 1)

        @block.tensor
        def _(pe):
            with loop(pe, TT, 2) as t:
                pe.wait_ge(copied, t)
                for s in range(2):
                    pe.wait_ge(staged, t + s + 1)
                    for h in range(DH):
                        mm = pe.transpose(ps[:, s, h * P:(h + 1) * P], stage[:, s, h], g.ident[:])
                    mm.then_inc(turned, 1)

        @block.vector
        def _(dve):
            with loop(dve, TT, 2) as t:
                for s in range(2):
                    dve.wait_ge(turned, t + s + 1)
                    dve.tensor_copy(tok[:, ds(t + s, 1)].rearrange("p a d -> p (a d)"), ps[:, s, 0:D]).then_inc(copied, 1)
            dve.wait_ge(copied, TT)


def soft_experts(k, g, ins, norm):
    nc = k.nc
    HN = NP_ // 2
    NC = NP_ // P
    EC = P // PS
    WR = 4
    logit_dram = k.dram("soft_logits", [2, T, HN])
    loaded, w_loaded = k.sem("soft_loaded"), k.sems("soft_w_loaded", WR)
    with ExitStack() as ctx:
        xt = k.sb(ctx, "soft_xt", [P, NC, D])
        y = k.sb(ctx, "soft_y", [P, NC, D])
        w = k.sb(ctx, "soft_w", [P, WR, EC, DH, D])
        w_b = k.sb(ctx, "soft_w_b", [P, NC, D])

        def load_experts(sp, c, s):
            sp.dma_start(w[:, s], ins["soft_w"][ds(c * EC, EC)].rearrange("n (h p) d -> p n h d", p=P)).then_inc(w_loaded[s], 16)

        with ExitStack() as c1:
            tok = k.sb(c1, "soft_tok", [P, TT, D])
            phi = k.sb(c1, "soft_phi", [P, DH, NP_])
            phi_b = k.sb(c1, "soft_phi_b", [P, NP_])

            def prefetch(sp):
                sp.dma_start(phi[:], ins["soft_phi"].rearrange("(h p) n -> p h n", p=P)).then_inc(loaded, 16)
                sp.dma_start(phi_b[:], ins["soft_phi_b"].partition_broadcast(P)).then_inc(loaded, 16)
                for n in range(EC):
                    sp.dma_start(w_b[n * PS:(n + 1) * PS], ins["soft_w_b"][n].rearrange("(c d) -> c d", d=D).partition_broadcast(PS)).then_inc(loaded, 16)
                for s in range(WR):
                    load_experts(sp, s, s)

            norm(g, g.x, g.xn, prefetch=prefetch)
            token_tiles(k, g, "soft_tiles", tok)

            staged, lg_ready, biased, maxed, lowered, exped = (k.sem(f"soft_d_{x}") for x in ("staged", "lg_ready", "biased", "maxed", "lowered", "exped"))
            summed, inverted, shared, mixed, cleared, clipped = (k.sem(f"soft_d_{x}") for x in ("summed", "inverted", "shared", "mixed", "cleared", "clipped"))
            stored = k.sems("soft_d_stored", 2)
            GN = HN // PS
            HC = HN // P
            with ExitStack() as c2:
                stage = k.sb(c2, "soft_stage", [P, 2, DH, P])
                logit = k.sb(c2, "soft_logit", [P, 2, HN])
                power = k.sb(c2, "soft_power", [P, 2, HN])
                share = k.sb(c2, "soft_share", [P, 2, HN])
                high = k.sb(c2, "soft_high", [P, 2, GN])
                total = k.sb(c2, "soft_total", [P, 2, GN])
                zero = k.sb(c2, "soft_zero", [1, 512])
                lg = k.ps(c2, "soft_lg", [P, 2, HN])
                mix = k.ps(c2, "soft_mix", [P, HC, D])
                block = c2.enter_context(nc.Block())

                def groups(tile, s):
                    return tile[:, s].rearrange("p (n q) -> p n q", q=PS)

                def none(t, s):
                    pass

                @block.sync
                def _(sp):
                    for a in range(2):
                        def store(t, s):
                            sp.wait_ge(biased, a * TT + t + 1)
                            sp.dma_start(logit_dram[a, ds(t * P, P), :], logit[:, s]).then_inc(stored[s], 16)

                        pipelined(sp, TT, 2, [store])
                    for s in range(2):
                        sp.wait_ge(stored[s], 16 * TT)

                @block.gpsimd
                def _(pool):
                    for a in range(2):
                        def stage_tile(t, s):
                            wait(pool, lg_ready, a * TT + t - 1)
                            pool.tensor_copy(stage[:, s], g.xn[:, :, chunk(t, P)]).then_inc(staged, 1)

                        def normalise(t, s):
                            pool.wait_ge(inverted, a * TT + t + 1)
                            wait(pool, mixed, a * TT + t - 1)
                            pool.tensor_tensor(groups(share, s), groups(power, s), total[:, s].unsqueeze(2).to_broadcast([P, GN, PS]), ALU.mult).then_inc(shared, 1)

                        pipelined(pool, TT, 2, [stage_tile, none, normalise])

                @block.tensor
                def _(pe):
                    pe.wait_ge(loaded, 16 * (2 + EC))
                    pe.wait_ge(cleared, 1)
                    for a in range(2):
                        def logits(t, s):
                            pe.wait_ge(staged, a * TT + t + 1)
                            wait(pe, biased, a * TT + t - 1)
                            for v in range(HN // 512):
                                at = a * HN + v * 512
                                for h in range(DH):
                                    mm = pe.matmul(lg[:, s, v * 512:(v + 1) * 512], stage[:, s, h], phi[:, h, at:at + 512], start=(h == 0), stop=(h == DH - 1))
                            mm.then_inc(lg_ready, 1)

                        def mixtures(t, s):
                            if isinstance(t, int) and t == 0:
                                wait(pe, clipped, a * HC)
                                for v in range(HC * D // 512):
                                    pe.matmul(mix[:].rearrange("p c d -> p (c d)")[:, v * 512:(v + 1) * 512], zero[:, 0:P], zero[:], start=True, stop=False, skip_group_check=True)
                            pe.wait_ge(shared, a * TT + t + 1)
                            for c in range(HC):
                                mm = pe.matmul(mix[:, c], share[:, s, c * P:(c + 1) * P], tok[:, ds(t, 1)].rearrange("p a d -> p (a d)"), start=False, stop=isinstance(t, int) and t == TT - 1, skip_group_check=True)
                            mm.then_inc(mixed, 1)

                        pipelined(pe, TT, 2, [logits, none, mixtures])

                @block.vector
                def _(dve):
                    dve.memset(zero[:], 0.0).then_inc(cleared, 1)
                    dve.wait_ge(loaded, 16 * (2 + EC))
                    for a in range(2):
                        def lower(t, s):
                            n = a * TT + t + 1
                            dve.wait_ge(lg_ready, n)
                            wait(dve, stored[s], 8 * (a * TT + t - s))
                            dve.tensor_tensor(logit[:, s], lg[:, s], phi_b[:, a * HN:(a + 1) * HN], ALU.add).then_inc(biased, 1)
                            dve.wait_ge(biased, n)
                            dve.tensor_reduce(high[:, s], groups(logit, s), AX, ALU.max).then_inc(maxed, 1)
                            dve.wait_ge(maxed, n)
                            wait(dve, shared, n - 2)
                            dve.tensor_tensor(groups(power, s), groups(logit, s), high[:, s].unsqueeze(2).to_broadcast([P, GN, PS]), ALU.subtract).then_inc(lowered, 1)

                        def invert(t, s):
                            n = a * TT + t + 1
                            dve.wait_ge(exped, n)
                            dve.tensor_reduce(total[:, s], groups(power, s), AX, ALU.add).then_inc(summed, 1)
                            dve.wait_ge(summed, n)
                            dve.reciprocal(total[:, s], total[:, s]).then_inc(inverted, 1)

                        pipelined(dve, TT, 2, [lower, invert])
                        dve.wait_ge(mixed, (a + 1) * TT)
                        for c in range(HC):
                            dve.tensor_scalar(xt[:, a * HC + c], mix[:, c], -33000.0, 65000.0, ALU.max, ALU.min).then_inc(clipped, 1)

                @block.scalar
                def _(act):
                    for a in range(2):
                        def exponentiate(t, s):
                            act.wait_ge(lowered, a * TT + t + 1)
                            act.activation(power[:, s], power[:, s], ACT.Exp).then_inc(exped, 1)

                        pipelined(act, TT, 2, [exponentiate])

        stats, var_ready, std_ready, rstd_ready = (k.sem(f"soft_e_{x}") for x in ("stats", "var_ready", "std_ready", "rstd_ready"))
        normed, bent, turned, copied, y_ready, y_added = (k.sem(f"soft_e_{x}") for x in ("normed", "bent", "turned", "copied", "y_ready", "y_added"))
        with ExitStack() as c2:
            stat = k.sb(c2, "soft_stat", [P, NC, 6])
            moments = k.sb(c2, "soft_moments", [P, NC, 2])
            rstd = k.sb(c2, "soft_rstd", [P, NC])
            xa = k.sb(c2, "soft_xa", [P, WR, D])
            xh = k.sb(c2, "soft_xh", [P, WR, D])
            xhT = k.sb(c2, "soft_xhT", [P, WR, DH, P])
            tp = k.ps(c2, "soft_tp", [P, 2, 512])
            yp = k.ps(c2, "soft_yp", [P, 2, 512])
            block = c2.enter_context(nc.Block())

            @block.sync
            def _(sp):
                with loop(sp, NC - WR, WR) as c:
                    for s in range(WR):
                        sp.wait_ge(y_ready, c + s + 1)
                        load_experts(sp, c + s + WR, s)

            @block.vector
            def _(dve):
                for c in range(NC):
                    dve.bn_stats(stat[:, c], xt[:, c]).then_inc(stats, 1)
                for c in range(NC):
                    dve.wait_ge(stats, c + 1)
                    dve.bn_aggr(moments[:, c], stat[:, c]).then_inc(var_ready, 1)
                dve.wait_ge(std_ready, 1)
                dve.reciprocal(rstd[:], rstd[:]).then_inc(rstd_ready, 1)
                dve.wait_ge(rstd_ready, 1)
                dve.wait_ge(var_ready, NC)

                def normalise(c, s):
                    wait(dve, bent, c - WR + 1)
                    dve.tensor_scalar(xa[:, s], xt[:, ds(c, 1)].rearrange("p a d -> p (a d)"), moments[:, ds(c, 1), 0], rstd[:, ds(c, 1)], ALU.subtract, ALU.mult).then_inc(normed, 1)

                def copy(c, s):
                    dve.wait_ge(turned, c + 1)
                    wait(dve, y_ready, c - WR + 1)
                    dve.tensor_copy(xhT[:, s], tp[:, s % 2, 0:D].rearrange("p (h q) -> p h q", h=DH)).then_inc(copied, 1)

                def add_bias(c, s):
                    dve.wait_ge(y_ready, c + 1)
                    dve.tensor_tensor(y[:, ds(c, 1)].rearrange("p a d -> p (a d)"), yp[:, s % 2, 0:D], w_b[:, ds(c, 1)].rearrange("p a d -> p (a d)"), ALU.add).then_inc(y_added, 1)

                pipelined(dve, NC, WR, [normalise, copy, add_bias])

            @block.scalar
            def _(act):
                act.wait_ge(var_ready, NC)
                act.activation(rstd[:], moments[:, :, 1], ACT.Sqrt, bias=g.eps[:]).then_inc(std_ready, 1)

                def bend(c, s):
                    act.wait_ge(normed, c + 1)
                    wait(act, turned, c - WR + 1)
                    act.activation(xh[:, s], xa[:, s], ACT.Tanh).then_inc(bent, 1)

                pipelined(act, NC, WR, [bend])

            @block.tensor
            def _(pe):
                def turn(c, s):
                    pe.wait_ge(bent, c + 1)
                    wait(pe, copied, c - 1)
                    for h in range(DH):
                        mm = pe.transpose(tp[:, s % 2, h * P:(h + 1) * P], xh[:, s, h * P:(h + 1) * P], g.ident[:])
                    mm.then_inc(turned, 1)

                def product(c, s):
                    pe.wait_ge(w_loaded[s], (c - s) * (16 // WR) + 16)
                    pe.wait_ge(copied, c + 1)
                    wait(pe, y_added, c - 1)
                    for n in range(EC):
                        rows = slice(n * PS, (n + 1) * PS)
                        for h in range(DH):
                            mm = pe.matmul(yp[rows, s % 2, 0:D], xhT[:, s, h, rows], w[:, s, n, h], start=(h == 0), stop=(h == DH - 1), tile_position=(0, n * PS))
                    mm.then_inc(y_ready, 1)

                pipelined(pe, NC, WR, [turn, product])

        maxed, lowered, exped, summed, inverted, shared = (k.sem(f"soft_c_{x}") for x in ("maxed", "lowered", "exped", "summed", "inverted", "shared"))
        turned, copied, y_ready, added = (k.sem(f"soft_c_{x}") for x in ("turned", "copied", "y_ready", "added"))
        lc_loaded = k.sems("soft_c_loaded", 2)
        GT = 512 // P
        GC = NP_ // 512
        with ExitStack() as c2:
            logit = k.sb(c2, "soft_logit2", [P, 2, NP_])
            power = k.sb(c2, "soft_power2", [P, 2, NP_])
            share = k.sb(c2, "soft_share2", [P, 2, NP_])
            shareT = k.sb(c2, "soft_shareT", [P, 2, NP_])
            high = k.sb(c2, "soft_high2", [P, 2, PS])
            total = k.sb(c2, "soft_total2", [P, 2, PS])
            ct = k.ps(c2, "soft_ct", [P, GC, 512])
            acc = k.ps(c2, "soft_acc", [P, 2, 512])
            block = c2.enter_context(nc.Block())

            def by_number(tile, s):
                return tile[:, s].rearrange("p (n q) -> p q n", q=PS)

            def over_experts(v, s):
                return v[:, s].unsqueeze(2).to_broadcast([P, PS, NE])

            def none(t, s):
                pass

            @block.sync
            def _(sp):
                def load(t, s):
                    wait(sp, lowered, t - 1)
                    sp.dma_start(logit[:, s].rearrange("p (a n) -> p a n", a=2), logit_dram[:, ds(t * P, P), :].rearrange("a p n -> p a n")).then_inc(lc_loaded[s], 16)

                pipelined(sp, TT, 2, [load])

            @block.vector
            def _(dve):
                def lower(t, s):
                    dve.wait_ge(lc_loaded[s], 8 * (t - s) + 16)
                    dve.tensor_reduce(high[:, s], by_number(logit, s), AX, ALU.max).then_inc(maxed, 1)
                    dve.wait_ge(maxed, t + 1)
                    wait(dve, shared, t - 1)
                    dve.tensor_tensor(by_number(power, s), by_number(logit, s), over_experts(high, s), ALU.subtract).then_inc(lowered, 1)

                def invert(t, s):
                    dve.wait_ge(exped, t + 1)
                    dve.tensor_reduce(total[:, s], by_number(power, s), AX, ALU.add).then_inc(summed, 1)
                    dve.wait_ge(summed, t + 1)
                    dve.reciprocal(total[:, s], total[:, s]).then_inc(inverted, 1)

                def add(t, s):
                    dve.wait_ge(y_ready, t + 1)
                    x = g.x[:, :, chunk(t, P)]
                    dve.tensor_tensor(x, acc[:, s, 0:D].rearrange("p (h q) -> p h q", h=DH), x, ALU.add).then_inc(added, 1)

                pipelined(dve, TT, 2, [lower, invert, none, none, add])

            @block.scalar
            def _(act):
                def exponentiate(t, s):
                    act.wait_ge(lowered, t + 1)
                    act.activation(power[:, s], power[:, s], ACT.Exp).then_inc(exped, 1)

                def copy(t, s):
                    wait(act, y_ready, t - 1)
                    for b in range(GC):
                        act.wait_ge(turned, GC * t + b + 1)
                        act.activation(shareT[:, s, b * 512:(b + 1) * 512], ct[:, b], ACT.Copy).then_inc(copied, 1)

                pipelined(act, TT, 2, [exponentiate, none, copy])

            @block.gpsimd
            def _(pool):
                def normalise(t, s):
                    pool.wait_ge(inverted, t + 1)
                    wait(pool, turned, GC * (t - 1))
                    pool.tensor_tensor(by_number(share, s), by_number(power, s), over_experts(total, s), ALU.mult).then_inc(shared, 1)

                pipelined(pool, TT, 2, [normalise])

            @block.tensor
            def _(pe):
                def turn(t, s):
                    pe.wait_ge(shared, t + 1)
                    for b in range(GC):
                        wait(pe, copied, GC * (t - 1) + b + 1)
                        for c in range(GT):
                            mm = pe.transpose(ct[:, b, c * P:(c + 1) * P], share[:, s, (b * GT + c) * P:(b * GT + c + 1) * P], g.ident[:])
                        mm.then_inc(turned, 1)

                def combine(t, s):
                    pe.wait_ge(copied, GC * (t + 1))
                    wait(pe, added, t - 1)
                    for m in range(DH):
                        for c in range(NC):
                            mm = pe.matmul(acc[:, s, m * P:(m + 1) * P], y[:, c, m * P:(m + 1) * P], shareT[:, s, c * P:(c + 1) * P], start=(c == 0), stop=(c == NC - 1))
                    mm.then_inc(y_ready, 1)

                pipelined(pe, TT, 2, [turn, combine])


def routed_experts(k, g, ins, norm):
    nc = k.nc
    norm(g, g.x, g.xn)
    tok_dram = k.dram("moe_tok", [T, D])
    list_dram = k.dram("moe_list", [NSLOT, 1], I32)
    expert_dram = k.dram("moe_expert", [2 * P], I32)
    y_dram = k.dram("moe_y", [NSLOT, D])
    with ExitStack() as ctx:
        slot = k.sb(ctx, "moe_slot", [P, TT, TOPK], I32)
        place = k.sb(ctx, "moe_place", [P, TT * TOPK], I32)
        weight = k.sb(ctx, "moe_weight", [P, TT, TOPK])
        token = k.sb(ctx, "moe_token", [P, TT], I32)
        loaded = k.sem("moe_loaded")
        tok_stored, list_cleared, expert_stored = k.sem("moe_tok_stored"), k.sem("moe_list_cleared"), k.sem("moe_expert_stored")

        with ExitStack() as c1:
            tok = k.sb(c1, "moe_tok_sb", [P, TT, D])
            token_tiles(k, g, "moe_tiles", tok)

            lt_ready, lt_copied, lg_ready, score_ready = k.sem("moe_lt_ready"), k.sem("moe_lt_copied"), k.sem("moe_lg_ready"), k.sem("moe_score_ready")
            stepped, chosen_ready, cum_ready, rank_ready, id_ready = k.sem("moe_stepped"), k.sem("moe_chosen_ready"), k.sem("moe_cum_ready"), k.sem("moe_rank_ready"), k.sem("moe_id_ready")
            with ExitStack() as c2:
                def sb(name, shape, dt=F32):
                    return k.sb(c2, f"moe_{name}", shape, dt)

                gate_w = sb("gate_w", [P, DH, E])
                gate_b = sb("gate_b", [P, E])
                before = sb("before", [P, P])
                all_ones = sb("all_ones", [P, P])
                tri = sb("tri", [P, NG, NG])
                tile_id = sb("tile_id", [P, 2])
                logitT = sb("logitT", [E, T])
                score = sb("score", [P, TT, E])
                choice = sb("choice", [P, TT, E])
                pair = sb("pair", [P, TT * NG, EG])
                pair_best = sb("pair_best", [P, EG - 1, TT * NG])
                group = sb("group", [P, TT * NG])
                larger = sb("larger", [P, TT, NG, NG])
                equal = sb("equal", [P, TT, NG, NG])
                ahead = sb("ahead", [P, TT * NG])
                masked = sb("masked", [P, TT, E])
                best = sb("best", [P, TT, TOPK])
                marked = sb("marked", [P, TT, E])
                chosen = sb("chosen", [P, TT, E])
                share = sb("share", [P, TT, E])
                total = sb("total", [P, TT])
                cum = sb("cum", [P, TT + 1, E])
                count = sb("count", [P, E])
                count_i = sb("count_i", [P, E], I32)
                tiles_i = sb("tiles_i", [P, E], I32)
                tiles = sb("tiles", [P, E])
                ends = sb("ends", [P, E])
                base = sb("base", [P, E])
                one_row = sb("one_row", [P, E])
                key = sb("key", [P, TT, E])
                key8 = sb("key8", [P, TT, TOPK])
                match = sb("match", [P, TOPK, E])
                low_i = sb("low_i", [P, TT * TOPK], I32)
                high_i = sb("high_i", [P, TT * TOPK], I32)
                low = sb("low", [P, TT * TOPK])
                ended = sb("ended", [P, 2, E])
                expert_f = sb("expert_f", [P, 2])
                expert = sb("expert", [P, 2], I32)
                zeros = sb("zeros", [P, SLOT_TILES], I32)
                lt_ps = k.ps(c2, "moe_lt_ps", [P, 2, 512])
                lg_ps = k.ps(c2, "moe_lg_ps", [P, 2, 512])
                rank_ps = k.ps(c2, "moe_rank_ps", [P, 2, 512])
                count_ps = k.ps(c2, "moe_count_ps", [P, 512])
                block = c2.enter_context(nc.Block())
                HT = TT // 2

                @block.sync
                def _(sp):
                    sp.dma_start(gate_w[:], ins["moe_gate_w"].rearrange("(h p) e -> p h e", p=P)).then_inc(loaded, 16)
                    sp.dma_start(gate_b[:], ins["moe_gate_b"].partition_broadcast(P)).then_inc(loaded, 16)
                    sp.dma_start(before[:], ins["moe_before"]).then_inc(loaded, 16)
                    sp.dma_start(tri[:], ins["moe_tri"].partition_broadcast(P)).then_inc(loaded, 16)
                    sp.dma_start(tile_id[:], ins["moe_tile_id"]).then_inc(loaded, 16)
                    sp.dma_start(token[:], ins["moe_token"]).then_inc(loaded, 16)
                    sp.dma_start(tok_dram.rearrange("(t p) d -> p t d", p=P), tok[:]).then_inc(tok_stored, 16)
                    sp.wait_ge(chosen_ready, 1)
                    sp.dma_start(list_dram.rearrange("(p i) n -> p (i n)", p=P), zeros[:]).then_inc(list_cleared, 16)
                    sp.wait_ge(id_ready, 1)
                    with nc.allow_non_contiguous_dma(reason="one word for each tile of slots"):
                        sp.dma_start(expert_dram.rearrange("(j p) -> p j", p=P), expert[:]).then_inc(expert_stored, 16)
                    sp.wait_ge(tok_stored, 16)
                    sp.wait_ge(list_cleared, 16)
                    sp.wait_ge(expert_stored, 16)

                @block.tensor
                def _(pe):
                    pe.wait_ge(loaded, 96)
                    for j in range(NCH):
                        if j >= 2:
                            pe.wait_ge(lt_copied, j - 1)
                        for h in range(DH):
                            mm = pe.matmul(lt_ps[0:E, j % 2, 0:CW], gate_w[:, h], g.xn[:, h, j * CW:(j + 1) * CW], start=(h == 0), stop=(h == DH - 1))
                        mm.then_inc(lt_ready, 1)
                    pe.wait_ge(lt_copied, NCH)
                    for t in range(TT):
                        mm = pe.transpose(lg_ps[:, t // HT, t % HT * E:(t % HT + 1) * E], logitT[:, t * P:(t + 1) * P], g.ident[0:E, 0:E])
                    mm.then_inc(lg_ready, 1)
                    pe.wait_ge(cum_ready, 1)
                    for w in range(2):
                        part = slice(w * HT, (w + 1) * HT)
                        pe.matmul(rank_ps[:, w, 0:HT * E], before[:], chosen[:, part].rearrange("p t e -> p (t e)"), start=True, stop=False)
                        pe.matmul(rank_ps[:, w, 0:HT * E], all_ones[:], cum[:, part].rearrange("p t e -> p (t e)"), start=False, stop=True)
                    pe.matmul(count_ps[:, 0:E], all_ones[:], cum[:, TT], start=True, stop=True).then_inc(rank_ready, 1)

                @block.scalar
                def _(act):
                    for j in range(NCH):
                        act.wait_ge(lt_ready, j + 1)
                        act.activation(logitT[:, j * CW:(j + 1) * CW], lt_ps[0:E, j % 2, 0:CW], ACT.Copy).then_inc(lt_copied, 1)
                    act.wait_ge(lg_ready, 1)
                    act.activation(score[:].rearrange("p (w t) e -> p w (t e)", w=2), lg_ps[:, :, 0:HT * E], ACT.Sigmoid).then_inc(score_ready, 1)

                @block.vector
                def _(dve):
                    steps = Steps(dve, stepped)

                    def then(ins):
                        steps.did(ins)
                        steps.wait()

                    dve.memset(zeros[:], 0)
                    dve.memset(all_ones[:], 1.0)
                    dve.memset(one_row[:], 1.0)
                    dve.memset(cum[:, 0], 0.0).then_inc(chosen_ready, 1)
                    dve.wait_ge(loaded, 96)
                    dve.wait_ge(score_ready, 1)
                    then(dve.tensor_tensor(choice[:], score[:], gate_b[:].unsqueeze(1).to_broadcast([P, TT, E]), ALU.add))
                    by_group = choice[:].rearrange("p t (a b) -> p (t a) b", b=EG)
                    for d in range(1, EG):
                        then(dve.tensor_tensor(pair[:, :, :EG - d], by_group[:, :, :EG - d], by_group[:, :, d:], ALU.add))
                        then(dve.tensor_reduce(pair_best[:, d - 1], pair[:, :, :EG - d], AX, ALU.max))
                    then(dve.tensor_reduce(group[:], pair_best[:].rearrange("p d a -> p a d"), AX, ALU.max))
                    own = group[:].rearrange("p (t a) -> p t a", a=NG)
                    mine = own.unsqueeze(3).to_broadcast([P, TT, NG, NG])
                    other = own.unsqueeze(2).to_broadcast([P, TT, NG, NG])
                    then(dve.tensor_tensor(larger[:], other, mine, ALU.is_gt))
                    then(dve.tensor_tensor(equal[:], other, mine, ALU.is_equal))
                    flat = lambda a: a[:].rearrange("p t a b -> p t (a b)")
                    then(dve.tensor_tensor(flat(equal), flat(equal), tri[:].rearrange("p a b -> p (a b)").unsqueeze(1).to_broadcast([P, TT, NG * NG]), ALU.mult))
                    then(dve.tensor_tensor(larger[:], larger[:], equal[:], ALU.add))
                    then(dve.tensor_reduce(ahead[:], larger[:].rearrange("p t a b -> p (t a) b"), AX, ALU.add))
                    then(dve.tensor_scalar(ahead[:], ahead[:], TOPG - 0.5, None, ALU.is_lt))
                    then(dve.tensor_tensor(masked[:].rearrange("p t (a b) -> p (t a) b", b=EG), by_group, ahead[:].unsqueeze(2).to_broadcast([P, TT * NG, EG]), ALU.mult))
                    for t in range(TT):
                        last = dve.max(best[:, t], masked[:, t])
                    then(last)
                    for t in range(TT):
                        last = dve.match_replace(marked[:, t], best[:, t], masked[:, t], -BIG)
                    then(last)
                    then(dve.tensor_scalar(chosen[:], marked[:], -BIG, None, ALU.is_equal))
                    for t in range(TT):
                        add = dve.tensor_tensor(cum[:, t + 1], cum[:, t], chosen[:, t], ALU.add)
                        if t < TT - 1:
                            then(add)
                    add.then_inc(cum_ready, 1)
                    then(dve.tensor_tensor(share[:], score[:], chosen[:], ALU.mult))
                    then(dve.tensor_reduce(total[:], share[:], AX, ALU.add))
                    then(dve.tensor_scalar(total[:], total[:], 1e-20, None, ALU.add))
                    then(dve.reciprocal(total[:], total[:]))
                    then(dve.tensor_tensor(share[:], share[:], total[:].unsqueeze(2).to_broadcast([P, TT, E]), ALU.mult))
                    then(dve.tensor_scalar(share[:], share[:], 2.5, None, ALU.mult))
                    dve.wait_ge(rank_ready, 1)
                    then(dve.tensor_scalar(count_i[:], count_ps[:, 0:E], P - 1.0, None, ALU.add))
                    then(dve.tensor_scalar(tiles_i[:], count_i[:], P.bit_length() - 1, None, ALU.arith_shift_right))
                    then(dve.tensor_copy(tiles[:], tiles_i[:]))
                    then(dve.tensor_tensor_scan(ends[:], one_row[:], tiles[:], 0.0, ALU.mult, ALU.add))
                    then(dve.tensor_tensor(base[:], ends[:], tiles[:], ALU.subtract))
                    then(dve.tensor_scalar(base[:], base[:], float(P), 1.0, ALU.mult, ALU.add))
                    for w in range(2):
                        part = slice(w * HT, (w + 1) * HT)
                        last = dve.tensor_tensor(key[:, part], rank_ps[:, w, 0:HT * E].rearrange("p (t e) -> p t e", e=E), base[:].unsqueeze(1).to_broadcast([P, HT, E]), ALU.add)
                    then(last)
                    then(dve.tensor_tensor(key[:], key[:], chosen[:], ALU.mult))
                    for t in range(TT):
                        last = dve.max(key8[:, t], key[:, t])
                    then(last)
                    then(dve.tensor_scalar(slot[:], key8[:], -1.0, None, ALU.add))
                    flat_slot = slot[:].rearrange("p t n -> p (t n)")
                    then(dve.tensor_scalar(low_i[:], flat_slot, P - 1, None, ALU.bitwise_and))
                    then(dve.tensor_scalar(high_i[:], flat_slot, P.bit_length() - 1, None, ALU.arith_shift_right))
                    then(dve.tensor_scalar(low[:], low_i[:], float(SLOT_TILES), None, ALU.mult))
                    then(dve.tensor_tensor(place[:], low[:], high_i[:], ALU.add))
                    for t in range(TT):
                        then(dve.tensor_tensor(match[:], key[:, t].unsqueeze(1).to_broadcast([P, TOPK, E]), key8[:, t].unsqueeze(2).to_broadcast([P, TOPK, E]), ALU.is_equal))
                        then(dve.tensor_tensor(match[:], match[:], share[:, t].unsqueeze(1).to_broadcast([P, TOPK, E]), ALU.mult))
                        then(dve.tensor_reduce(weight[:, t], match[:], AX, ALU.add))
                    for j in range(2):
                        last = dve.tensor_scalar(ended[:, j], ends[:], tile_id[:, j:j + 1], None, ALU.is_le)
                    then(last)
                    then(dve.tensor_reduce(expert_f[:], ended[:], AX, ALU.add))
                    dve.tensor_scalar(expert[:], expert_f[:], E - 1.0, None, ALU.min).then_inc(id_ready, 1)

        listed = k.sem("moe_listed")
        s_loaded, up_ready, silu_done, gated, down_ready, added = k.sem("moe_s_loaded"), k.sem("moe_s_up_ready"), k.sem("moe_s_silu_done"), k.sem("moe_s_gated"), k.sem("moe_s_down_ready"), k.sem("moe_s_added")
        with ExitStack() as c2:
            SC = -(-SI // P)
            rows = [min(P, SI - c * P) for c in range(SC)]
            w_up = k.sb(c2, "moe_s_w_up", [P, DH, 2 * SI])
            w_down = k.sb(c2, "moe_s_w_down", [P, SC, D])
            act_g = k.sb(c2, "moe_s_act", [P, SC, CW])
            hid = k.sb(c2, "moe_s_hid", [P, SC, CW])
            up = k.ps(c2, "moe_s_up", [P, SC, 2, 512])
            acc = k.ps(c2, "moe_s_acc", [P, DH, 512])
            block = c2.enter_context(nc.Block())

            @block.gpsimd
            def _(pool):
                for t in range(TT):
                    for n in range(TOPK):
                        at = t * TOPK + n
                        pool.indirect_dma_start(list_dram, bass.IndirectOffsetOnAxis(ap=place[:, at:at + 1], axis=0), token[:, t:t + 1], None).then_inc(listed, 16)
                pool.wait_ge(listed, 16 * TT * TOPK)

            @block.sync
            def _(sp):
                sp.dma_start(w_up[:], ins["moe_s_up"].rearrange("(h p) n -> p h n", p=P)).then_inc(s_loaded, 16)
                sp.dma_start(w_down[:], ins["moe_s_down"].rearrange("(c p) n -> p c n", p=P)).then_inc(s_loaded, 16)

            @block.tensor
            def _(pe):
                pe.wait_ge(s_loaded, 32)
                with loop(pe, NCH) as j:
                    pe.wait_ge(gated, SC * j)
                    for c in range(SC):
                        for n in range(2):
                            at = n * SI + c * P
                            for h in range(DH):
                                mm = pe.matmul(up[0:rows[c], c, n, 0:CW], w_up[:, h, at:at + rows[c]], g.xn[:, h, chunk(j, CW)], start=(h == 0), stop=(h == DH - 1))
                        mm.then_inc(up_ready, 1)
                    pe.wait_ge(gated, SC * (j + 1))
                    pe.wait_ge(added, DH * j)
                    for m in range(DH):
                        for c in range(SC):
                            mm = pe.matmul(acc[:, m, 0:CW], w_down[0:rows[c], c, m * P:(m + 1) * P], hid[0:rows[c], c], start=(c == 0), stop=(c == SC - 1))
                        mm.then_inc(down_ready, 1)

            @block.scalar
            def _(act):
                with loop(act, NCH) as j:
                    act.wait_ge(gated, SC * j)
                    for c in range(SC):
                        act.wait_ge(up_ready, SC * j + c + 1)
                        act.activation(act_g[0:rows[c], c], up[0:rows[c], c, 0, 0:CW], ACT.Silu).then_inc(silu_done, 1)

            @block.vector
            def _(dve):
                with loop(dve, NCH) as j:
                    dve.wait_ge(down_ready, DH * j)
                    for c in range(SC):
                        dve.wait_ge(silu_done, SC * j + c + 1)
                        dve.tensor_tensor(hid[0:rows[c], c], act_g[0:rows[c], c], up[0:rows[c], c, 1, 0:CW], ALU.mult).then_inc(gated, 1)
                    for m in range(DH):
                        dve.wait_ge(down_ready, DH * j + m + 1)
                        x = g.x[:, m, chunk(j, CW)]
                        dve.tensor_tensor(x, acc[:, m, 0:CW], x, ALU.add).then_inc(added, 1)

        RING = 8
        I2 = I - P
        WN = 4 * I + 2 * D
        list_loaded, expert_loaded = k.sem("moe_list_loaded"), k.sem("moe_expert_loaded")
        staged, gathered, w_loaded = k.sem("moe_staged"), k.sems("moe_gathered", RING), k.sems("moe_w_loaded", RING)
        x_turned, x_copied, up_ready, silu_done, gated = k.sem("moe_x_turned"), k.sem("moe_x_copied"), k.sem("moe_up_ready"), k.sem("moe_silu_done"), k.sem("moe_gated")
        h_turned, h_copied, y_ready, y_copied, y_stored = k.sem("moe_h_turned"), k.sem("moe_h_copied"), k.sem("moe_y_ready"), k.sem("moe_y_copied"), k.sems("moe_y_stored", RING)
        with ExitStack() as c2:
            slot_token = k.sb(c2, "moe_slot_token", [P, SLOT_TILES], I32)
            expert_row = k.sb(c2, "moe_expert_row", [1, 2 * P], I32)
            index = k.sb(c2, "moe_index", [P, RING], I32)
            w = k.sb(c2, "moe_w", [P, RING, WN])
            xg = k.sb(c2, "moe_xg", [P, RING, D])
            xT = k.sb(c2, "moe_xT", [P, RING, D])
            act_g = k.sb(c2, "moe_act", [P, RING, I])
            hid = k.sb(c2, "moe_hid", [P, RING, I])
            hT = k.sb(c2, "moe_hT", [P, RING, 2 * P])
            y_sb = k.sb(c2, "moe_y_sb", [P, RING, D])
            x_ps = k.ps(c2, "moe_x_ps", [P, 2, 512])
            up_ps = k.ps(c2, "moe_up_ps", [P, 2, 512])
            h_ps = k.ps(c2, "moe_h_ps", [P, 2, 512])
            y_ps = k.ps(c2, "moe_y_ps", [P, 2, 512])
            block = c2.enter_context(nc.Block())
            uses = lambda t, s: (t - s) * (16 // RING)

            @block.gpsimd
            def _(pool):
                def gather(t, s):
                    wait(pool, x_turned, t - RING + 1)
                    pool.tensor_copy(index[:, s:s + 1], slot_token[:, ds(t, 1)]).then_inc(staged, 1)
                    pool.wait_ge(staged, t + 1)
                    after_wait(pool, g)
                    pool.indirect_dma_start(xg[:, s], None, tok_dram, bass.IndirectOffsetOnAxis(ap=index[:, s:s + 1], axis=0)).then_inc(gathered[s], 16)

                pool.wait_ge(list_loaded, 16)
                pipelined(pool, SLOT_TILES, RING, [gather])

            @block.sync
            def _(sp):
                def load(t, s):
                    wait(sp, y_ready, t - RING + 1)
                    after_wait(sp, g)
                    e = sp.value_load(expert_row[:, ds(t, 1)], min_val=0, max_val=E - 1)
                    sp.dma_start(w[:, s, 0:WN - D], ins["moe_w"][ds(e, 1), :, 0:WN - D].rearrange("e p n -> p (e n)")).then_inc(w_loaded[s], 16)
                    sp.dma_start(w[0:I2, s, WN - D:], ins["moe_w"][ds(e, 1), 0:I2, WN - D:].rearrange("e p n -> p (e n)")).then_inc(w_loaded[s], 16)

                sp.dma_start(slot_token[:], list_dram.rearrange("(p i) n -> p (i n)", p=P)).then_inc(list_loaded, 16)
                sp.dma_start(expert_row[:], expert_dram.unsqueeze(0)).then_inc(expert_loaded, 16)
                sp.wait_ge(expert_loaded, 16)
                pipelined(sp, SLOT_TILES, RING, [load])

            @block.tensor
            def _(pe):
                def turn(t, s):
                    pe.wait_ge(gathered[s], uses(t, s) + 16)
                    wait(pe, x_copied, t - 1)
                    for h in range(DH):
                        mm = pe.transpose(x_ps[:, s % 2, h * P:(h + 1) * P], xg[:, s, h * P:(h + 1) * P], g.ident[:])
                    mm.then_inc(x_turned, 1)

                def up(t, s):
                    pe.wait_ge(w_loaded[s], 2 * uses(t, s) + 32)
                    pe.wait_ge(x_copied, t + 1)
                    wait(pe, gated, t - 1)
                    for h in range(DH):
                        mm = pe.matmul(up_ps[:, s % 2, 0:2 * I], xT[:, s, h * P:(h + 1) * P], w[:, s, h * 2 * I:(h + 1) * 2 * I], start=(h == 0), stop=(h == DH - 1))
                    mm.then_inc(up_ready, 1)

                def turn_hidden(t, s):
                    pe.wait_ge(gated, t + 1)
                    wait(pe, h_copied, t - 1)
                    pe.transpose(h_ps[:, s % 2, 0:P], hid[:, s, 0:P], g.ident[:])
                    pe.transpose(h_ps[0:I2, s % 2, P:2 * P], hid[:, s, P:I], g.ident[:]).then_inc(h_turned, 1)

                def down(t, s):
                    pe.wait_ge(h_copied, t + 1)
                    wait(pe, y_copied, t - 1)
                    pe.matmul(y_ps[:, s % 2, 0:D], hT[:, s, 0:P], w[:, s, 4 * I:4 * I + D], start=True, stop=False)
                    pe.matmul(y_ps[:, s % 2, 0:D], hT[0:I2, s, P:2 * P], w[0:I2, s, 4 * I + D:4 * I + 2 * D], start=False, stop=True).then_inc(y_ready, 1)

                pipelined(pe, SLOT_TILES, RING, [turn, up, turn_hidden, down])

            @block.vector
            def _(dve):
                def copy_x(t, s):
                    dve.wait_ge(x_turned, t + 1)
                    wait(dve, up_ready, t - RING + 1)
                    dve.tensor_copy(xT[:, s], x_ps[:, s % 2, 0:D]).then_inc(x_copied, 1)

                def gate(t, s):
                    dve.wait_ge(silu_done, t + 1)
                    wait(dve, h_turned, t - RING + 1)
                    dve.tensor_tensor(hid[:, s], act_g[:, s], up_ps[:, s % 2, I:2 * I], ALU.mult).then_inc(gated, 1)

                def copy_y(t, s):
                    dve.wait_ge(y_ready, t + 1)
                    wait(dve, y_stored[s], uses(t, s))
                    dve.tensor_copy(y_sb[:, s], y_ps[:, s % 2, 0:D]).then_inc(y_copied, 1)

                pipelined(dve, SLOT_TILES, RING, [copy_x, gate, lambda t, s: None, copy_y])

            @block.scalar
            def _(act):
                def silu(t, s):
                    act.wait_ge(up_ready, t + 1)
                    wait(act, gated, t - RING + 1)
                    act.activation(act_g[:, s], up_ps[:, s % 2, 0:I], ACT.Silu).then_inc(silu_done, 1)

                def copy_hidden(t, s):
                    act.wait_ge(h_turned, t + 1)
                    wait(act, y_ready, t - RING + 1)
                    act.activation(hT[:, s, 0:P], h_ps[:, s % 2, 0:P], ACT.Copy)
                    act.activation(hT[0:I2, s, P:2 * P], h_ps[0:I2, s % 2, P:2 * P], ACT.Copy).then_inc(h_copied, 1)

                def store(t, s):
                    act.wait_ge(y_copied, t + 1)
                    act.dma_start(y_dram[ds(t * P, P), :], y_sb[:, s]).then_inc(y_stored[s], 16)

                pipelined(act, SLOT_TILES, RING, [silu, copy_hidden, store])
                for s in range(RING):
                    act.wait_ge(y_stored[s], SLOT_TILES // RING * 16)

        FR = 4
        staged, fetched, diag_ready = k.sem("moe_f_staged"), k.sems("moe_f_fetched", FR), k.sem("moe_f_diag_ready")
        sum_ready, sum_added = k.sem("moe_f_sum_ready"), k.sem("moe_f_sum_added")
        with ExitStack() as c2:
            index = k.sb(c2, "moe_f_index", [P, FR, TOPK], I32)
            part = k.sb(c2, "moe_f_part", [P, FR, TOPK, D])
            diag = k.sb(c2, "moe_f_diag", [P, FR, TOPK, P])
            acc = k.ps(c2, "moe_f_acc", [P, 2, DH, 512])
            block = c2.enter_context(nc.Block())

            @block.gpsimd
            def _(pool):
                def fetch(t, s):
                    wait(pool, sum_ready, t - FR + 1)
                    pool.tensor_copy(index[:, s].unsqueeze(1), slot[:, ds(t, 1)]).then_inc(staged, 1)
                    pool.wait_ge(staged, t + 1)
                    after_wait(pool, g)
                    for n in range(TOPK):
                        pool.indirect_dma_start(part[:, s, n], None, y_dram, bass.IndirectOffsetOnAxis(ap=index[:, s, n:n + 1], axis=0)).then_inc(fetched[s], 16)

                pipelined(pool, TT, FR, [fetch])

            @block.vector
            def _(dve):
                def weigh(t, s):
                    wait(dve, sum_ready, t - FR + 1)
                    for n in range(TOPK):
                        last = dve.tensor_scalar(diag[:, s, n], g.ident[:], weight[:, ds(t, 1), n], None, ALU.mult)
                    last.then_inc(diag_ready, 1)

                def add(t, s):
                    dve.wait_ge(sum_ready, t + 1)
                    x = g.x[:, :, chunk(t, P)]
                    dve.tensor_tensor(x, acc[:, s % 2, :, 0:P], x, ALU.add).then_inc(sum_added, 1)

                pipelined(dve, TT, FR, [weigh, add])

            @block.tensor
            def _(pe):
                def total(t, s):
                    pe.wait_ge(diag_ready, t + 1)
                    pe.wait_ge(fetched[s], (t - s) * (16 // FR * TOPK) + 16 * TOPK)
                    wait(pe, sum_added, t - 1)
                    for m in range(DH):
                        for n in range(TOPK):
                            mm = pe.matmul(acc[:, s % 2, m, 0:P], part[:, s, n, m * P:(m + 1) * P], diag[:, s, n], start=(n == 0), stop=(n == TOPK - 1))
                    mm.then_inc(sum_ready, 1)

                pipelined(pe, TT, FR, [total])


class State:
    pass


STAGES = [mamba, cross_attention, routed_experts, min_gru, delay_attention, soft_experts]


def decoder(nc, ins, out):
    with ExitStack() as outer:
        k = Kit(nc, outer)
        g = State()
        g.x = k.sb(outer, "x", [P, DH, T])
        g.xn = k.sb(outer, "xn", [P, DH, T])
        g.ident = k.sb(outer, "ident", [P, P])
        g.mean_w = k.sb(outer, "mean_w", [P, P])
        g.ones = k.sb(outer, "ones", [P, P])
        g.eps = k.sb(outer, "eps", [P, 1])
        g.waits_passed = k.kept_sem("waits_passed")
        load_constants(k, g, ins)
        norm = LayerNorm(k)
        for stage in STAGES:
            stage(k, g, ins, norm)
            k.end_stage()
        stored = k.sem("x_stored")
        with nc.Block() as block:
            @block.sync
            def _(sp):
                sp.dma_start(out.rearrange("(h p) t -> p h t", p=P), g.x[:]).then_inc(stored, 16)
                sp.wait_ge(stored, 16)




def by_partition(v):
    return np.ascontiguousarray(v.reshape(-1, P).T)


def rotary(n):
    freq = np.float32(1.0) / np.float32(10000.0) ** (np.arange(0, HD, 2, dtype=np.float32) / np.float32(HD))
    pos = np.float32(10.0) * (np.arange(n, dtype=np.float32) / np.float32(n))
    angle = (pos[:, None] * freq).astype(np.float32)
    row = np.arange(P) % HD
    sign = np.where(row % 2 == 0, -1.0, 1.0)[:, None]
    return (np.cos(angle).T[row // 2].astype(np.float32), (sign * np.sin(angle).T[row // 2]).astype(np.float32))


def transforms():
    t = np.arange(L)
    f_cos, f_sin = np.arange(NF + 1), np.arange(1, NF)
    turn = lambda f: 2 * np.pi * ((t[:, None] * f[None, :]) % L) / L
    there = np.concatenate([np.cos(turn(f_cos)), np.sin(turn(f_sin))], axis=1)
    times = np.where((f_cos == 0) | (f_cos == NF), 1.0, 2.0)
    times = np.concatenate([times, np.full(NF - 1, 2.0)]) / (L * D)
    return there.astype(np.float32), np.ascontiguousarray((there * times).T).astype(np.float32)


def host_layout(a):
    f = {}
    c = np.ascontiguousarray
    f["xT"] = c(a["x"].reshape(T, D).T)
    f["ident"] = np.eye(P, dtype=np.float32)
    f["mamba_small"] = c(np.concatenate([
        a["L0_attn_conv_w"], a["L0_attn_conv_b"][:, None], a["L0_attn_dt_w"][:, None], a["L0_attn_dt_b"][:, None],
        a["L0_attn_D"][:, None], a["L0_attn_A_log"]], axis=1))
    f["mamba_norm"] = c(np.stack([by_partition(a["L0_attn_norm_w"]), by_partition(a["L0_attn_norm_b"])], axis=1))
    f["mamba_w_in"] = c(a["L0_attn_W_in"])
    f["mamba_xp_w"] = c(a["L0_attn_x_proj_w"][:, 1:])
    f["mamba_dt_rep"] = c(np.repeat(a["L0_attn_x_proj_w"][:, 0:1], P, axis=1))
    f["mamba_w_out"] = c(a["L0_attn_W_out"])

    def swapped(w):
        return w.reshape(*w.shape[:-1], -1, 2)[..., ::-1].reshape(w.shape)

    w_k, w_v = a["L0_xattn_Wkv"][:, :D], a["L0_xattn_Wkv"][:, D:]
    b_k, b_v = a["L0_xattn_bkv"][:D], a["L0_xattn_bkv"][D:]
    f["xattn_w_q"] = c(np.concatenate([a["L0_xattn_Wq"], swapped(a["L0_xattn_Wq"])], axis=1))
    f["xattn_w_kv"] = c(np.concatenate([w_k, swapped(w_k), w_v], axis=1))
    f["xattn_w_o"] = c(a["L0_xattn_Wo"])
    f["xattn_bias"] = c(np.concatenate([by_partition(v) for v in (
        a["L0_xattn_bq"], swapped(a["L0_xattn_bq"]), b_k, swapped(b_k), b_v, a["L0_xattn_bo"])], axis=1))
    f["xattn_rope"] = c(np.concatenate([*rotary(L), *rotary(S2)], axis=1))
    f["xattn_own_head"] = (np.arange(P)[:, None] // HD == np.arange(HPT)).astype(np.float32)
    f["xattn_keep"] = c(a["mask_BxS2_bf1"]).reshape(B * S2).view(np.uint8)
    f["ctxT"] = c(a["ctx_1024"].transpose(0, 2, 1))
    f["gru_w"] = c(a["L1_attn_W_hg"])
    f["gru_w_out"] = c(a["L1_attn_W_out"])
    f["delay_w"] = c(np.concatenate([a["L1_xattn_Wq"], a["L1_xattn_Wk"], a["L1_xattn_Wv"]], axis=1))
    f["delay_b_qk"] = c(np.concatenate([a["L1_xattn_bq"], a["L1_xattn_bk"]])[None])
    f["delay_w_o"] = c(a["L1_xattn_Wo"])
    f["delay_bias"] = c(np.concatenate([by_partition(a["L1_xattn_bv"]), by_partition(a["L1_xattn_bo"])], axis=1))
    f["delay_dft"], f["delay_idft"] = transforms()
    phi = a["L1_ffn_phi_w"]
    f["soft_phi"], f["soft_phi_b"] = c(phi.T), c(a["L1_ffn_phi_b"])
    f["soft_w"] = c(a["L1_ffn_expert_w"])
    f["soft_w_b"] = c(a["L1_ffn_expert_b"].reshape(NP_ // P, P // PS, D).transpose(1, 0, 2)).reshape(P // PS, -1)
    f["moe_gate_w"], f["moe_gate_b"] = c(a["L0_ffn_gate_w"].T), c(a["L0_ffn_gate_bias"])
    f["moe_before"] = (np.arange(P)[:, None] < np.arange(P)).astype(np.float32)
    f["moe_tri"] = (np.arange(NG)[:, None] > np.arange(NG)).astype(np.float32)
    f["moe_tile_id"] = np.arange(2 * P).reshape(2, P).T.astype(np.float32)
    f["moe_token"] = c(np.arange(T).reshape(TT, P).T.astype(np.int32))
    f["moe_s_up"] = c(np.concatenate([a["L0_ffn_Sg"], a["L0_ffn_Su"]]).T)
    s_down = np.zeros((-(-SI // P) * P, D), np.float32)
    s_down[:SI] = a["L0_ffn_Sd"].T
    f["moe_s_down"] = s_down
    up = np.concatenate([a["L0_ffn_Wg"], a["L0_ffn_Wu"]], axis=1).transpose(0, 2, 1)
    f["moe_w"] = np.zeros((E, P, 4 * I + 2 * D), np.float32)
    for h in range(DH):
        f["moe_w"][:, :, h * 2 * I:(h + 1) * 2 * I] = up[:, h * P:(h + 1) * P]
    down = a["L0_ffn_Wd"].transpose(0, 2, 1)
    f["moe_w"][:, :, 4 * I:4 * I + D] = down[:, :P]
    f["moe_w"][:, :I - P, 4 * I + D:] = down[:, P:]
    return f


def kernel(**inputs):
    import concourse.bacc as bacc
    from concourse.bass_utils import run_bass_kernel_spmd

    arrays = host_layout({name: np.asarray(v) for name, v in inputs.items()})
    nc = bacc.Bacc("TRN2", target_bir_lowering=False, num_devices=1)
    ins = {name: nc.dram_tensor(name, v.shape, mybir.dt.from_np(v.dtype), kind="ExternalInput").ap() for name, v in arrays.items()}
    out = nc.dram_tensor("out", [D, T], F32, kind="ExternalOutput").ap()
    decoder(nc, ins, out)
    got = run_bass_kernel_spmd(nc, [arrays], core_ids=[0]).results[0]["out"]
    return np.ascontiguousarray(got.T.reshape(B, L, D))
```
